# Optimizing a Trainium2 kernel written in Bass

```python
import numpy as np
import jax
import jax.numpy as jnp

def _softmax(x, axis=-1):
    return jax.nn.softmax(x, axis=axis)

def _gelu(x):
    return jax.nn.gelu(x, approximate=True)

def _silu(x):
    return jax.nn.silu(x)

def _sigmoid(x):
    return jax.nn.sigmoid(x)

def _layernorm(x, axis=-1, eps=1e-05):
    m = jnp.mean(x, axis=axis, keepdims=True)
    v = jnp.var(x, axis=axis, keepdims=True)
    return (x - m) / jnp.sqrt(v + eps)

def _scatter_add(tgt, idx, src, axis=0):
    return tgt.at[idx].add(src)

def _segment_sum(src, seg, n):
    return jax.ops.segment_sum(src, seg, n)
kernel_name = 'mk_vit_tower_cls_d1_tok_img768_r4_82b0e2'

def setup_inputs(seed: int=0):
    np.random.seed(seed)
    _w = jnp.asarray

    def _rec_inputs():
        import jax
        import jax.numpy as jnp
        _rk = jax.random.key(seed)
        x = 7.57192e-06 + 1.00007 * jax.random.normal(jax.random.fold_in(_rk, 1), (16, 3, 96, 96), jnp.float32)
        cls_tok = 0.02 * jax.random.normal(jax.random.fold_in(_rk, 5), (1, 1, 192), jnp.float32)
        return (x, cls_tok)
    x, cls_tok = _rec_inputs()

    def _L0_tok_setup():
        import jax, jax.numpy as jnp
        import numpy as np
        P = 16
        EPS = 1e-05
        key = jax.random.key(seed)
        k1, k2 = jax.random.split(key)
        B, C, H, Wd = (64, 3, 224, 224)
        patch_dim = P * P * C * 5
        hidden = 192
        x = jax.random.normal(k1, (B, C, H, Wd), dtype=jnp.float32)
        ln_gamma = jnp.ones((patch_dim,), jnp.float32)
        ln_beta = jnp.zeros((patch_dim,), jnp.float32)
        W = jax.random.normal(k2, (patch_dim, hidden), dtype=jnp.float32) * patch_dim ** (-0.5)
        b = jnp.zeros((hidden,), jnp.float32)
        return {'x': x, 'ln_gamma': ln_gamma, 'ln_beta': ln_beta, 'W': W, 'b': b}
    _L0_tok_all = _L0_tok_setup()
    _L0_tok_in = {k: v for k, v in _L0_tok_all.items() if k in ('ln_gamma', 'ln_beta', 'W', 'b')}
    del _L0_tok_all

    def _L0_attn_setup():
        import jax, jax.numpy as jnp
        import numpy as np
        NUM_HEADS = 12
        SCRA_SCALING = 10.0
        EPS = 1e-12
        key = jax.random.key(seed)
        ks = jax.random.split(key, 5)
        B, N, C = (2, 512, 192)
        return {'x': jax.random.normal(ks[0], (B, N, C), dtype=jnp.float32), 'qkv_w': jax.random.normal(ks[1], (3 * C, C), dtype=jnp.float32) * 0.02, 'qkv_b': jax.random.normal(ks[2], (3 * C,), dtype=jnp.float32) * 0.02, 'proj_w': jax.random.normal(ks[3], (C, C), dtype=jnp.float32) * 0.02, 'proj_b': jax.random.normal(ks[4], (C,), dtype=jnp.float32) * 0.02}
    _L0_attn_all = _L0_attn_setup()
    _L0_attn_in = {k: v for k, v in _L0_attn_all.items() if k in ('qkv_w', 'qkv_b', 'proj_w', 'proj_b')}
    del _L0_attn_all

    def _L0_ffn_setup():
        import jax, jax.numpy as jnp
        import numpy as np
        B, S, D_IN, D_HID, D_OUT = (32, 128, 192, 768, 192)
        key = jax.random.key(seed)
        k1, k2, k3, k4 = jax.random.split(key, 4)
        init_k = float(np.sqrt(1.0 / D_IN))
        init_k2 = float(np.sqrt(1.0 / D_HID))
        x = jax.random.normal(k1, (B, S, D_IN), dtype=jnp.float32)
        in_weight = jax.random.uniform(k2, (D_HID, D_IN), dtype=jnp.float32, minval=-init_k, maxval=init_k)
        in_bias = jax.random.uniform(k3, (D_HID,), dtype=jnp.float32, minval=-init_k, maxval=init_k)
        out_weight = jax.random.uniform(k4, (D_HID, D_OUT), dtype=jnp.float32, minval=-init_k2, maxval=init_k2)
        return {'x': x, 'in_weight': in_weight, 'in_bias': in_bias, 'out_weight': out_weight}
    _L0_ffn_all = _L0_ffn_setup()
    _L0_ffn_in = {k: v for k, v in _L0_ffn_all.items() if k in ('in_weight', 'in_bias', 'out_weight')}
    del _L0_ffn_all
    return {'x': x, 'cls_tok': cls_tok, 'L0_tok_ln_gamma': _L0_tok_in['ln_gamma'], 'L0_tok_ln_beta': _L0_tok_in['ln_beta'], 'L0_tok_W': _L0_tok_in['W'], 'L0_tok_b': _L0_tok_in['b'], 'L0_attn_qkv_w': _L0_attn_in['qkv_w'], 'L0_attn_qkv_b': _L0_attn_in['qkv_b'], 'L0_attn_proj_w': _L0_attn_in['proj_w'], 'L0_attn_proj_b': _L0_attn_in['proj_b'], 'L0_ffn_in_weight': _L0_ffn_in['in_weight'], 'L0_ffn_in_bias': _L0_ffn_in['in_bias'], 'L0_ffn_out_weight': _L0_ffn_in['out_weight']}

def reference(x, cls_tok, L0_tok_ln_gamma, L0_tok_ln_beta, L0_tok_W, L0_tok_b, L0_attn_qkv_w, L0_attn_qkv_b, L0_attn_proj_w, L0_attn_proj_b, L0_ffn_in_weight, L0_ffn_in_bias, L0_ffn_out_weight):
    import jax
    import jax.numpy as jnp

    def _L0_tok_ref(x, ln_gamma, ln_beta, W, b):
        import jax, jax.numpy as jnp
        import numpy as np
        P = 16
        EPS = 1e-05
        xc = jnp.concatenate([x, jnp.roll(x, 1, axis=3), jnp.roll(x, -1, axis=3), jnp.roll(x, 1, axis=2), jnp.roll(x, -1, axis=2)], axis=1)
        B, C5, H, Wd = xc.shape
        h, w = (H // P, Wd // P)
        t = xc.reshape(B, C5, h, P, w, P).transpose(0, 2, 4, 3, 5, 1).reshape(B, h * w, P * P * C5)
        mu = jnp.mean(t, axis=-1, keepdims=True)
        var = jnp.mean(jnp.square(t - mu), axis=-1, keepdims=True)
        y = (t - mu) * jax.lax.rsqrt(var + EPS) * ln_gamma + ln_beta
        return jnp.einsum('bnd,dk->bnk', y, W) + b

    def _L0_attn_ref(x, qkv_w, qkv_b, proj_w, proj_b):
        import jax, jax.numpy as jnp
        import numpy as np
        NUM_HEADS = 12
        SCRA_SCALING = 10.0
        EPS = 1e-12
        B, N, C = x.shape
        H = NUM_HEADS
        D = C // H
        scale = D ** (-0.5)
        xt = jnp.transpose(x, (1, 0, 2))
        qkv = xt @ qkv_w.T + qkv_b
        q, k, v = jnp.split(qkv, 3, axis=-1)

        def to_bh(t):
            return jnp.transpose(t.reshape(N, B * H, D), (1, 0, 2))
        q, k, v = (to_bh(q), to_bh(k), to_bh(v))
        attn = jax.nn.softmax(jnp.einsum('bnd,bmd->bnm', q, k) * scale, axis=-1)
        out = jnp.einsum('bnm,bmd->bnd', attn, v)
        out = jnp.transpose(out, (1, 0, 2)).reshape(N, B, C)
        out = out @ proj_w.T + proj_b
        out = jnp.transpose(out.reshape(N, B * H, D), (1, 0, 2))
        norm = jnp.linalg.norm(out, axis=-1, keepdims=True)
        sim_tokens = out / jnp.maximum(norm, EPS)
        sim = jnp.einsum('bnd,bmd->bnm', sim_tokens, sim_tokens) * SCRA_SCALING
        sim = jnp.where(sim < 0, -jnp.inf, sim)
        sim = jax.nn.softmax(sim, axis=-1)
        out2 = jnp.einsum('bnm,bmd->bnd', sim, v)
        out2 = jnp.transpose(out2, (1, 0, 2)).reshape(N, B, C)
        out2 = out2 @ proj_w.T + proj_b
        return jnp.transpose(out2, (1, 0, 2))

    def _L0_ffn_ref(x, in_weight, in_bias, out_weight):
        import jax, jax.numpy as jnp
        import numpy as np
        B, S, D_IN, D_HID, D_OUT = (32, 128, 192, 768, 192)
        lead = x.shape[:-1]
        xt = x.reshape(-1, in_weight.shape[1])
        h = jax.nn.gelu(jnp.einsum('td,hd->th', xt, in_weight) + in_bias, approximate=False)
        out = jnp.einsum('th,ho->to', h, out_weight)
        return out.reshape(*lead, out_weight.shape[1])
    h = _L0_tok_ref(x, L0_tok_ln_gamma, L0_tok_ln_beta, L0_tok_W, L0_tok_b)
    h = jnp.concatenate([jnp.broadcast_to(cls_tok, (h.shape[0], 1, h.shape[2])), h], axis=1)
    h = h + _L0_attn_ref(_layernorm(h, axis=-1), L0_attn_qkv_w, L0_attn_qkv_b, L0_attn_proj_w, L0_attn_proj_b)
    h = h + _L0_ffn_ref(_layernorm(h, axis=-1), L0_ffn_in_weight, L0_ffn_in_bias, L0_ffn_out_weight)
    return h

_drawn_inputs = setup_inputs


def setup_inputs(seed=0):
    import zlib

    import numpy as np

    out = dict(_drawn_inputs(seed))
    spreads = {'L0_tok_ln_gamma': (1.0, 0.2), 'L0_tok_ln_beta': (0.0, 0.1), 'L0_tok_b': (0.0, 0.1)}
    factors = {'cls_tok': 2.817,
     'L0_attn_qkv_w': 2.836,
     'L0_attn_qkv_b': 8.0,
     'L0_ffn_in_bias': 3.728,
     'L0_attn_proj_b': 2.719}
    for name, (base, spread) in spreads.items():
        noise = np.random.default_rng([zlib.crc32(name.encode()), seed]).standard_normal(out[name].shape)
        drawn = base * np.exp(spread * noise) if base else spread * noise
        out[name] = jnp.asarray(drawn.astype(out[name].dtype))
    for name, factor in factors.items():
        out[name] = (out[name] * factor).astype(out[name].dtype)
    return out
```

```python
from contextlib import ExitStack

import concourse.bass as bass
from concourse import mybir

F32 = mybir.dt.float32
ALU = mybir.AluOpType
ACT = mybir.ActivationFunctionType
AX = mybir.AxisListType

NIMG, CH, IMG, PS = 16, 3, 96, 16
GR = IMG // PS
ROWS = NIMG * GR
N = GR * GR + 1
T = NIMG * N
HID, HALF = 192, 96
NH, D = 12, 16
NSH = 5
FEAT = PS * PS * CH * NSH
NCHUNK = 2 * CH + 2
FFN = 768
NF = FFN // 128
NT = -(-T // 128)
TILES = [(128 * i, min(128, T - 128 * i)) for i in range(NT)]
NPAIR = NIMG // 2
PP = 64 + N
G3 = 3 * N
VW = D + 1
TH = T // 2
EPS = 1e-5
NORM_EPS = 1e-12
SCALE = float(D) ** -0.5
SIM_SCALE = 10.0
KCH = [128] * (2 * CH) + [HALF, HALF]


def vit(nc, x, cls_tok, gamma, beta, W, b_tok, qkv_w, qkv_b, proj_w, proj_b, in_w, in_b, out_w, out):
    with ExitStack() as ctx:
        def sb(name, shape):
            return ctx.enter_context(nc.sbuf_tensor(name, shape, F32))

        def sem(name):
            return ctx.enter_context(nc.semaphore(name))

        bank = [ctx.enter_context(nc.psum_tensor(f"bank{i}", [128, 512], F32)) for i in range(8)]

        X = sb("X", [ROWS, CH, PS * IMG])
        XTB = sb("XTB", [ROWS, 2, CH, IMG])
        XTBR = sb("XTBR", [ROWS, GR, 2 * CH, PS])
        XLR = sb("XLR", [ROWS, GR, 2, CH, PS])
        XTS = sb("XTS", [128, 2, NCHUNK, T])
        XT, XS = XTS[:, 0], XTS[:, 1]
        XR = XTS[0:ROWS, 1].rearrange("p k t -> p (k t)")[:, 0:2 * CH * GR * 128].rearrange(
            "p (k w f) -> p k w f", k=2 * CH, w=GR)
        WP = sb("WP", [128, NSH, 2, CH, HID])
        WH = sb("WH", [HALF, 2, HID])
        WE = sb("WE", [128, NCHUNK, HID + 1])
        GN = sb("GN", [128, 2, 2, NSH, CH])
        GP = sb("GP", [128, 2, 2, NSH, CH])
        GH = sb("GH", [HALF, 2, 2])
        ident = sb("ident", [128, 128])
        sh = [sb(f"sh{s}", [128, 128]) for s in range(4)]
        ZP = HALF - PS
        sel = sb("sel", [128, 6, ZP + PS + ZP])
        inv_n = sb("inv_n", [128, 1])
        sums = sb("sums", [HALF, 2, 2])
        R = sb("R", [4, HID])
        IND = sb("IND", [4, NIMG, N])
        neg0 = sb("neg0", [4, 128])
        g1n = sb("g1n", [128, HID])
        BASE = sb("BASE", [128, NT, HID])
        st = sb("st", [128, NT, 2])
        nvar = sb("nvar", [128, NT])
        std = sb("std", [128, NT])
        rstd = sb("rstd", [128, NT])
        u = sb("u", [128, 2, HID])
        h1 = sb("h1", [128, NT, HID])
        bn = sb("bn", [128, NT, 6])
        mv = sb("mv", [128, NT, 2])
        std1 = sb("std1", [128, NT])
        rstd1 = sb("rstd1", [128, NT])
        hn = sb("hn", [128, NT, HID])
        hnT = sb("hnT", [HALF + 1, 2, T])
        eps = sb("eps", [128, 1])
        m10 = sb("m10", [128, 1])
        qkvw = sb("qkvw", [HALF, 6, HID])
        projw = sb("projw", [HALF, 2, HID])
        inw = sb("inw", [128, NF, HID])
        w2 = sb("w2", [128, NF, HID])
        inbr = sb("inbr", [NF, 128])
        inb = sb("inb", [128, NF])
        WQ = sb("WQ", [HALF + 1, 2, 3, HID])
        WO = sb("WO", [HALF + 1, 2, HID])
        WI = sb("WI", [HALF, 2, FFN])
        mask6 = sb("mask6", [HALF, 6])
        mask12 = sb("mask12", [G3, 4, 3])
        qT, kT = (X[:, :, :].rearrange("p c w -> p (c w)")[:, 2 * T * k:2 * T * (k + 1)]
                  .rearrange("p (h t) -> p h t", h=2) for k in range(2))
        K6 = XTS[0:HALF].rearrange("p a k t -> p (a k t)")[:, 0:2 * 6 * T].rearrange(
            "p (h q b j n) -> p h q b j n", h=2, q=2, j=3, n=N)
        VB = sb("VB", [G3, NIMG, 4 * 3, VW])
        mx = sb("mx", [PP, 2, NH])
        Pr = sb("Pr", [PP, 2, NH, N])
        PT = sb("PT", [G3, 2, 4, PP])
        ro = sb("ro", [PP, 2, NH])
        On = sb("On", [PP, 2, HID])
        OT = sb("OT", [HALF + 1, 2, T])
        ysq = sb("ysq", [128, 2, HID])
        ss = sb("ss", [128, NT, NH])
        nrm = sb("nrm", [128, NT, NH])
        rn = sb("rn", [128, NT, NH])
        Y = sb("Y", [128, NT, HID])
        YT = sb("YT", [HALF, 2, T])
        E1 = sb("E1", [G3, 2, 4, 2 * N])
        E2 = sb("E2", [G3, 2, 4, 2 * N])
        h2 = sb("h2", [128, NT, HID])
        bn2 = sb("bn2", [128, NT, 6])
        mv2 = sb("mv2", [128, NT, 2])
        std2 = sb("std2", [128, NT])
        rstd2 = sb("rstd2", [128, NT])
        hn2 = sb("hn2", [128, NT, HID])
        hn2T = sb("hn2T", [HALF, 2, T])
        hn3 = WP[0:HALF + 1].rearrange("p s e c n -> p (s e c n)")[:, 0:2 * 3 * T].rearrange(
            "p (k b j n) -> p k b j n", k=2, j=3, n=N)
        hT = WP[:, :, :, :, :].rearrange("p s e c n -> p (s e c n)")[:, 0:NF * T].rearrange("p (f t) -> p f t", f=NF)
        res = sb("res", [128, NT, HID])

        S = {}
        for name in (
            "gb_in x0_in x1_in x2_in xtb_in w0_in w1_in w2_in w3_in w4_in wh_in gh_sb rows_in qkv_in proj_in "
            "ffnw_in bias_in out_done "
            "pool_step consts_ready wzero masks_ready ones_rows xlr_ready xtb_ready xr_v xr_a xcls_zero vones_ready "
            "dve_step act_step "
            "placed_mm placed cnt_mm cnt_done xt_mm xt_evac_v xt_evac_a xs_a xs_p weff sums_mm sums_sb "
            "rt_mm rt_sb g1_mm g1_sb base_mm base_sb wt_mm wt_v wt_a inb_sb "
            "emb_mm nvar_ready std_ready h1_ready mv_ready std1_ready hn_ready hnt_mm hnt_sb hn3_ready qk_mm q_sb k_sb "
            "k6_v k6_a k6_p v_mm v_sb "
            "s_mm p_sub p_exp pt_mm pt_sb pv_mm on_ready ot_mm ot_sb "
            "y_mm ysq_ready ss_ready nrm_ready y_ready yt_mm yt_sb t6_v t6_a t6_p "
            "s2_mm e1_ready e2_ready pv2_mm on2_ready ot2_mm ot2_sb "
            "y2_mm h2_mv std2_ready hn2_ready hn2t_mm hn2t_sb up_mm gelu_done down_mm res_ready"
        ).split():
            S[name] = sem(name)

        x_v = x.rearrange("b c (h r) w -> h b c (r w)", r=PS)
        W_v = W.rearrange("(p e s c) n -> p e s (c n)", p=128, e=2, s=NSH)
        W_px = W.rearrange("(r q s c) n -> r q s c n", r=PS, q=PS, s=NSH)
        g_v = [v.rearrange("(p k) -> p k", p=128) for v in (gamma, beta)]
        out_v = out.rearrange("b n k -> (b n) k")
        WPf = WP[:, :, :, :, :].rearrange("p s e c n -> p s e (c n)")

        def halo_rows(v, k, side):
            if k == 0:
                return v[:, 0 if side == 0 else PS - 1, 1 + side].rearrange("r c n -> c r n")
            return v[0 if side == 0 else PS - 1, :, 3 + side].rearrange("q c n -> c q n")

        def head_rows(half, hd):
            return K6[:, half, hd // 3, :, hd % 3, :]

        def reorder(c, e):
            return (XR[:, 2 * c + e].rearrange("p w (r h) -> p w r h", h=8),
                    X[:, c, :].rearrange("p (r w h e) -> p e w r h", w=GR, h=8, e=2)[:, e])

        block = ctx.enter_context(nc.Block())

        @block.sync
        def _(sp):
            for k in range(2):
                sp.dma_start(GN[:, k].rearrange("p e s c -> p (e s c)"), g_v[k]).then_inc(S["gb_in"], 16)
            for c in range(CH):
                for hy in range(GR):
                    sp.dma_start(X[NIMG * hy:NIMG * (hy + 1), c, :], x_v[hy, :, c]).then_inc(S[f"x{c}_in"], 16)
            for side in range(2):
                for hy in range(GR):
                    y = (PS * hy - 1) % IMG if side == 0 else (PS * hy + PS) % IMG
                    sp.dma_start(XTB[NIMG * hy:NIMG * (hy + 1), side], x[:, :, y, :]).then_inc(S["xtb_in"], 16)
            sp.dma_start(WPf[:, 0], W_v[:, :, 0]).then_inc(S["w0_in"], 16)
            sp.dma_start(WPf[:, 1, 1], W_v[:, 1, 1]).then_inc(S["w1_in"], 16)
            sp.dma_start(WPf[:, 2, 0], W_v[:, 0, 2]).then_inc(S["w2_in"], 16)
            sp.wait_ge(S["wzero"], 4)
            sp.dma_start(WPf[0:112, 1, 0], W_v[1:113, 0, 1]).then_inc(S["w1_in"], 16)
            sp.dma_start(WPf[112:127, 1, 0], W_v[113:128, 0, 1]).then_inc(S["w1_in"], 16)
            sp.dma_start(WPf[1:113, 2, 1], W_v[0:112, 1, 2]).then_inc(S["w2_in"], 16)
            sp.dma_start(WPf[113:128, 2, 1], W_v[112:127, 1, 2]).then_inc(S["w2_in"], 16)
            sp.dma_start(WPf[0:120, 3], W_v[8:128, :, 3]).then_inc(S["w3_in"], 16)
            sp.dma_start(WPf[8:128, 4], W_v[0:120, :, 4]).then_inc(S["w4_in"], 16)
            for k in range(2):
                for side in range(2):
                    src = halo_rows(W_px, k, side)
                    for c in range(CH):
                        a = 48 * side + PS * c
                        sp.dma_start(WH[a:a + PS, k, :], src[c]).then_inc(S["wh_in"], 16)
            sp.dma_start(R[2:3, :], b_tok.rearrange("(a n) -> a n", a=1)).then_inc(S["rows_in"], 16)
            sp.dma_start(R[3:4, :], cls_tok.rearrange("a b n -> (a b) n")).then_inc(S["rows_in"], 16)
            sp.dma_start(qkvw[:, :, :], qkv_w.rearrange("(o p) n -> p o n", p=HALF)).then_inc(S["qkv_in"], 16)
            sp.dma_start(projw[:, :, :], proj_w.rearrange("(o p) n -> p o n", p=HALF)).then_inc(S["proj_in"], 16)
            sp.dma_start(WQ[HALF:HALF + 1, 1, 0:2, :], qkv_b[0:2 * HID].rearrange("(a k n) -> a k n", a=1, k=2))\
              .then_inc(S["bias_in"], 16)
            for half in range(2):
                for par in range(2):
                    a = HALF * half + 48 * par
                    src = qkv_b[2 * HID + HALF * half:2 * HID + HALF * (half + 1)].rearrange(
                        "(a j q d) -> q a j d", a=1, q=2, d=D)[par]
                    sp.dma_start(WQ[HALF:HALF + 1, 1, 2, a:a + 48].rearrange("a (j d) -> a j d", d=D), src)\
                      .then_inc(S["bias_in"], 16)
            sp.dma_start(WO[HALF:HALF + 1, 1, :], proj_b.rearrange("(a n) -> a n", a=1)).then_inc(S["bias_in"], 16)
            sp.dma_start(inbr[:, :], in_b.rearrange("(f p) -> f p", p=128)).then_inc(S["bias_in"], 16)
            sp.dma_start(inw[:, :, :], in_w.rearrange("(f p) n -> p f n", p=128)).then_inc(S["ffnw_in"], 16)
            sp.dma_start(w2[:, :, :], out_w.rearrange("(f p) n -> p f n", p=128)).then_inc(S["ffnw_in"], 16)
            for i, (t0, n) in enumerate(TILES):
                sp.wait_ge(S["res_ready"], i + 1)
                sp.dma_start(out_v[t0:t0 + n, :], res[0:n, i, :]).then_inc(S["out_done"], 16)
            sp.wait_ge(S["out_done"], 16 * NT)

        @block.gpsimd
        def _(pool):
            g = nc.gpsimd
            steps = [0]

            def link(ins):
                steps[0] += 1
                ins.then_inc(S["pool_step"], 1)
                pool.wait_ge(S["pool_step"], steps[0])

            g.memset(ident[:, :], 0.0).then_inc(S["pool_step"], 1)
            for m in sh:
                g.memset(m[:, :], 0.0).then_inc(S["pool_step"], 1)
            g.memset(sel[:, :, :], 0.0).then_inc(S["pool_step"], 1)
            steps[0] = 6
            pool.wait_ge(S["pool_step"], 6)

            def diagonal(m, base, lo, hi):
                v = m[:, :].rearrange("p (a h) -> p a h", h=8)[:, :, lo:hi]
                return g.affine_select(out=v, in_=v, compare_op=ALU.not_equal, fill=1.0, base=-base - lo,
                                       pattern=[[-8, 16], [-1, hi - lo]], channel_multiplier=1)

            diagonal(ident, 0, 0, 8).then_inc(S["consts_ready"], 1)
            diagonal(sh[0], 1, 0, 7).then_inc(S["consts_ready"], 1)
            diagonal(sh[1], -1, 1, 8).then_inc(S["consts_ready"], 1)
            diagonal(sh[2], 8, 0, 8).then_inc(S["consts_ready"], 1)
            diagonal(sh[3], -8, 0, 8).then_inc(S["consts_ready"], 1)
            for q, base in enumerate((0, 7, 0, 0, 120, 120)):
                if q < 2:
                    m, pat = sel[:, q, ZP:ZP + PS], [[-8, PS]]
                else:
                    m, pat = sel[:, q, ZP + q % 2:ZP + PS:2], [[-1, 8]]
                g.affine_select(out=m, in_=m, compare_op=ALU.not_equal, fill=1.0, base=-base, pattern=pat,
                                channel_multiplier=1).then_inc(S["consts_ready"], 1)
            g.memset(inv_n[:, :], 1.0 / FEAT).then_inc(S["consts_ready"], 1)
            g.memset(eps[:, :], EPS).then_inc(S["consts_ready"], 1)
            g.memset(m10[:, :], -SIM_SCALE).then_inc(S["consts_ready"], 1)
            g.memset(XT[:, :, :].rearrange("p k (b n) -> p k b n", n=N)[:, :, :, 0], 0.0).then_inc(S["xcls_zero"], 1)

            for c in range(CH):
                pool.wait_ge(S[f"x{c}_in"], 16 * GR)
                Xc = X[:, c, :].rearrange("p (r w) -> p w r", w=IMG)
                g.tensor_copy(XLR[:, 1:GR, 0, c, :], Xc[:, PS - 1:IMG - 1:PS, :]).then_inc(S["xlr_ready"], 1)
                g.tensor_copy(XLR[:, 0, 0, c, :], Xc[:, IMG - 1, :]).then_inc(S["xlr_ready"], 1)
                g.tensor_copy(XLR[:, 0:GR - 1, 1, c, :], Xc[:, PS:IMG:PS, :]).then_inc(S["xlr_ready"], 1)
                g.tensor_copy(XLR[:, GR - 1, 1, c, :], Xc[:, 0, :]).then_inc(S["xlr_ready"], 1)

            pool.wait_ge(S["xtb_in"], 16 * 2 * GR)
            g.tensor_copy(XTBR[:, :, :, :], XTB[:, :, :, :].rearrange("p s c (w q) -> p w (s c) q", w=GR))\
             .then_inc(S["xtb_ready"], 1)

            pool.wait_ge(S["xcls_zero"], 1)
            for k in range(4):
                pool.wait_ge(S["xt_evac_v"], k + 1)
                pool.wait_ge(S["xt_evac_a"], k + 1)
                g.tensor_tensor(XS[0:KCH[k], k, :], XT[0:KCH[k], k, :], XT[0:KCH[k], k, :], ALU.mult)\
                 .then_inc(S["xs_p"], 1)

            link(g.memset(IND[:, :, 1:N], 1.0))
            link(g.memset(IND[:, :, 0:1], 0.0))
            link(g.affine_select(out=IND[:, :, 1:N], in_=IND[:, :, 1:N], compare_op=ALU.not_equal, fill=0.0,
                                 base=-3, pattern=[[0, NIMG], [0, N - 1]], channel_multiplier=1))
            link(g.affine_select(out=IND[:, :, 0:1], in_=IND[:, :, 0:1], compare_op=ALU.not_equal, fill=1.0,
                                 base=-3, pattern=[[0, NIMG], [0, 1]], channel_multiplier=1))
            link(g.memset(neg0[:, :], 0.0))
            g.memset(neg0[0:1, :], -1.0).then_inc(S["masks_ready"], 1)
            g.memset(IND[0:1, :, :], 0.0).then_inc(S["masks_ready"], 1)
            link(g.memset(mask6[:, :], 1.0))
            v6 = mask6[:, :].rearrange("p (q j) -> p q j", q=2)
            link(g.affine_select(out=v6, in_=v6, compare_op=ALU.is_ge, fill=0.0, base=0,
                                 pattern=[[-D, 2], [-2 * D, 3]], channel_multiplier=1))
            g.affine_select(out=v6, in_=v6, compare_op=ALU.is_ge, fill=0.0, base=D - 1,
                            pattern=[[D, 2], [2 * D, 3]], channel_multiplier=-1).then_inc(S["masks_ready"], 1)
            link(g.memset(mask12[:, :, :], 1.0))
            link(g.affine_select(out=mask12[:, :, :], in_=mask12[:, :, :], compare_op=ALU.is_ge, fill=0.0, base=0,
                                 pattern=[[0, 4], [-N, 3]], channel_multiplier=1))
            link(g.affine_select(out=mask12[:, :, :], in_=mask12[:, :, :], compare_op=ALU.is_ge, fill=0.0,
                                 base=N - 1, pattern=[[0, 4], [N, 3]], channel_multiplier=-1))
            for b in range(NIMG):
                ins = g.tensor_copy(VB[:, b, :, D], mask12[:, :, :].rearrange("p g j -> p (g j)"))
            ins.then_inc(S["vones_ready"], 1)

            pool.wait_ge(S["masks_ready"], 3)
            for half in range(2):
                pool.wait_ge(S["k_sb"], 2 * (half + 1))
                for hd in range(4, 6):
                    g.tensor_scalar(head_rows(half, hd), kT[:, half, :].rearrange("p (b n) -> p b n", n=N),
                                    mask6[:, hd:hd + 1], None, ALU.mult)\
                     .then_inc(S["k6_p"], 1)
            pool.wait_ge(S["s_mm"], NPAIR)
            for half in range(2):
                pool.wait_ge(S["yt_sb"], NT)
                for hd in range(4, 6):
                    g.tensor_scalar(head_rows(half, hd), YT[:, half, :].rearrange("p (b n) -> p b n", n=N),
                                    mask6[:, hd:hd + 1], None, ALU.mult)\
                     .then_inc(S["t6_p"], 1)

        @block.scalar
        def _(act):
            a = nc.scalar
            def evac_xt(k, hf):
                src = bank[2 * (k % 2) + hf][0:KCH[k], 0:3 * ROWS].rearrange("p (w h b) -> p w h b", w=3, h=GR)
                dst = XT[0:KCH[k], k, :].rearrange("p (b n) -> p n b", n=N)[:, 1:N, :]\
                    .rearrange("p (h w) b -> p w h b", w=GR)[:, 3 * hf:3 * hf + 3]
                return dst, src

            for c in range(CH):
                act.wait_ge(S[f"x{c}_in"], 16 * GR)
                dst, src = reorder(c, 1)
                for w in range(2):
                    ins = a.activation(dst[:, 3 * w:3 * w + 3], src[:, 3 * w:3 * w + 3], ACT.Copy)
                ins.then_inc(S["xr_a"], 1)
            for k in range(NCHUNK):
                act.wait_ge(S["xt_mm"], 2 * k + 2)
                dst, src = evac_xt(k, 1)
                for w in range(3):
                    ins = a.activation(dst[:, w], src[:, w], ACT.Copy)
                ins.then_inc(S["xt_evac_a"], 1)
                if k == 3:
                    act.wait_ge(S["xcls_zero"], 1)
                if k >= 4:
                    act.wait_ge(S["xt_evac_v"], k + 1)
                    act.wait_ge(S["xt_evac_a"], k + 1)
                    a.activation(XS[0:KCH[k], k, :], XT[0:KCH[k], k, :], ACT.Square).then_inc(S["xs_a"], 1)

            def std_of(dst, src, scale, done):
                a.activation(dst, src, ACT.Sqrt, bias=eps[0:dst.shape[0], :], scale=scale).then_inc(done, 1)

            act.wait_ge(S["consts_ready"], 14)
            for i in range(NT + 1):
                if i < NT:
                    n = TILES[i][1]
                    act.wait_ge(S["nvar_ready"], i + 1)
                    std_of(std[0:n, i:i + 1], nvar[0:n, i:i + 1], -1.0, S["std_ready"])
                if i >= 1:
                    n = TILES[i - 1][1]
                    act.wait_ge(S["mv_ready"], i)
                    std_of(std1[0:n, i - 1:i], mv[0:n, i - 1, 1:2], 1.0, S["std1_ready"])
            act.wait_ge(S["wt_mm"], 1)
            a.activation(WQ[0:HALF, 0, 0:2, :], bank[6][0:HALF, 0:2 * HID].rearrange("p (k n) -> p k n", k=2),
                         ACT.Copy).then_inc(S["wt_a"], 1)
            for i, (t0, n) in enumerate(TILES):
                act.wait_ge(S["hnt_mm"], i + 1)
                a.activation(hnT[0:HALF, :, t0:t0 + n],
                             bank[5 + i % 2][0:HALF, 0:256].rearrange("p (k t) -> p k t", k=2)[:, :, 0:n],
                             ACT.Copy).then_inc(S["hnt_sb"], 1)

            for half in range(2):
                for th in range(2):
                    act.wait_ge(S["qk_mm"], 4 * half + th + 1)
                    a.activation(qT[:, half, TH * th:TH * (th + 1)], bank[2 * half + th][0:HALF, 0:TH], ACT.Copy)\
                     .then_inc(S["q_sb"], 1)
            act.wait_ge(S["masks_ready"], 3)
            for half in range(2):
                act.wait_ge(S["k_sb"], 2 * (half + 1))
                a.activation(head_rows(half, 3), kT[:, half, :].rearrange("p (b n) -> p b n", n=N), ACT.Copy,
                             scale=mask6[:, 3:4]).then_inc(S["k6_a"], 1)

            for i in range(NPAIR + 3):
                if 1 <= i <= NPAIR:
                    p = i - 1
                    act.wait_ge(S["pt_mm"], p + 1)
                    if p >= 2:
                        act.wait_ge(S["pv_mm"], p - 1)
                    a.activation(PT[:, p % 2], bank[2 + p % 2][0:G3, 0:4 * PP].rearrange("p (g t) -> p g t", g=4),
                                 ACT.Copy).then_inc(S["pt_sb"], 1)
                if i < NPAIR:
                    act.wait_ge(S["p_sub"], i + 1)
                    a.activation(Pr[:, i % 2], Pr[:, i % 2], ACT.Exp, scale=SCALE).then_inc(S["p_exp"], 1)
                if i >= 3:
                    p = i - 3
                    act.wait_ge(S["ot_mm"], p + 1)
                    a.activation(OT[0:HALF, :, 2 * N * p:2 * N * (p + 1)].rearrange("p k (b n) -> p k b n", n=N),
                                 bank[6 + p % 2][0:HALF, 0:256].rearrange("p (k b n) -> p k b n", k=2, b=2)[:, :, :, 0:N],
                                 ACT.Copy).then_inc(S["ot_sb"], 1)

            for i, (t0, n) in enumerate(TILES):
                act.wait_ge(S["y_mm"], i + 1)
                if i >= 2:
                    act.wait_ge(S["ss_ready"], i - 1)
                a.activation(ysq[0:n, i % 2], bank[i][0:n, 0:HID], ACT.Square).then_inc(S["ysq_ready"], 1)
            act.wait_ge(S["ss_ready"], NT)
            a.activation(nrm[:, 0:NT - 1], ss[:, 0:NT - 1], ACT.Sqrt).then_inc(S["nrm_ready"], 1)
            nl = TILES[-1][1]
            a.activation(nrm[0:nl, NT - 1], ss[0:nl, NT - 1], ACT.Sqrt).then_inc(S["nrm_ready"], 1)
            for i, (t0, n) in enumerate(TILES):
                act.wait_ge(S["yt_mm"], i + 1)
                a.activation(YT[:, :, t0:t0 + n],
                             bank[5 + i % 2][0:HALF, 0:256].rearrange("p (k t) -> p k t", k=2)[:, :, 0:n],
                             ACT.Copy).then_inc(S["yt_sb"], 1)
            act.wait_ge(S["yt_sb"], NT)
            act.wait_ge(S["s_mm"], NPAIR)
            for half in range(2):
                a.activation(head_rows(half, 3), YT[:, half, :].rearrange("p (b n) -> p b n", n=N), ACT.Copy,
                             scale=mask6[:, 3:4]).then_inc(S["t6_a"], 1)

            for i in range(NPAIR + 3):
                if i < NPAIR:
                    act.wait_ge(S["s2_mm"], i + 1)
                    if i >= 2:
                        act.wait_ge(S["e2_ready"], i - 1)
                    a.activation(E1[:, i % 2], bank[i % 2][0:G3, 0:8 * N].rearrange("p (g t) -> p g t", g=4),
                                 ACT.Exp, bias=m10[0:G3, :], scale=SIM_SCALE).then_inc(S["e1_ready"], 1)
                if i >= 3:
                    p = i - 3
                    act.wait_ge(S["ot2_mm"], p + 1)
                    if p == 0:
                        act.wait_ge(S["y_mm"], NT)
                    a.activation(OT[0:HALF, :, 2 * N * p:2 * N * (p + 1)].rearrange("p k (b n) -> p k b n", n=N),
                                 bank[6 + p % 2][0:HALF, 0:256].rearrange("p (k b n) -> p k b n", k=2, b=2)[:, :, :, 0:N],
                                 ACT.Copy).then_inc(S["ot2_sb"], 1)

            for i, (t0, n) in enumerate(TILES):
                act.wait_ge(S["h2_mv"], i + 1)
                std_of(std2[0:n, i:i + 1], mv2[0:n, i, 1:2], 1.0, S["std2_ready"])
                act.wait_ge(S["hn2t_mm"], i + 1)
                a.activation(hn2T[:, :, t0:t0 + n],
                             bank[5 + i % 2][0:HALF, 0:256].rearrange("p (k t) -> p k t", k=2)[:, :, 0:n],
                             ACT.Copy).then_inc(S["hn2t_sb"], 1)
            act.wait_ge(S["inb_sb"], 1)
            for th in range(2):
                for f in range(NF):
                    q = NF * th + f
                    act.wait_ge(S["up_mm"], q + 1)
                    a.activation(hT[:, f, TH * th:TH * (th + 1)], bank[q % 3][:, 0:TH], ACT.Gelu,
                                 bias=inb[:, f:f + 1]).then_inc(S["gelu_done"], 1)

        @block.vector
        def _(dve):
            v = nc.vector
            steps = [0]

            def link(ins):
                steps[0] += 1
                ins.then_inc(S["dve_step"], 1)
                dve.wait_ge(S["dve_step"], steps[0])

            v.memset(WPf[96:128, 1, 0], 0.0).then_inc(S["wzero"], 1)
            v.memset(WPf[0:32, 2, 1], 0.0).then_inc(S["wzero"], 1)
            v.memset(WPf[96:128, 3], 0.0).then_inc(S["wzero"], 1)
            v.memset(WPf[0:32, 4], 0.0).then_inc(S["wzero"], 1)
            v.memset(hnT[HALF:HALF + 1, :, :], 1.0).then_inc(S["ones_rows"], 1)
            v.memset(OT[HALF:HALF + 1, 1, :], 1.0).then_inc(S["ones_rows"], 1)
            for c in range(CH):
                dve.wait_ge(S[f"x{c}_in"], 16 * GR)
                dst, src = reorder(c, 0)
                v.tensor_copy(dst, src).then_inc(S["xr_v"], 1)

            dve.wait_ge(S["gb_in"], 32)
            link(v.tensor_copy(GP[:, :, :, :, :], GN[:, :, :, :, :]))
            dve.wait_ge(S["placed_mm"], 3)
            pl = bank[4]
            link(v.tensor_copy(GP[:, :, 0, 1, :], pl[:, 0:6].rearrange("p (k c) -> p k c", k=2)))
            link(v.tensor_copy(GP[:, :, 1, 2, :], pl[:, 8:14].rearrange("p (k c) -> p k c", k=2)))
            for k in range(2):
                v.tensor_copy(GP[:, k, :, 3, :], pl[:, 16 + 6 * k:22 + 6 * k].rearrange("p (e c) -> p e c", e=2))
                ins = v.tensor_copy(GP[:, k, :, 4, :], pl[:, 32 + 6 * k:38 + 6 * k].rearrange("p (e c) -> p e c", e=2))
            ins.then_inc(S["placed"], 1)
            dve.wait_ge(S["placed_mm"], 3)
            v.tensor_copy(GH[:, :, :], pl[0:HALF, 56:60].rearrange("p (k g) -> p k g", k=2)).then_inc(S["gh_sb"], 1)
            dve.wait_ge(S["placed_mm"], 3)
            for e in range(2):
                v.tensor_copy(WE[:, e:2 * CH:2, HID], pl[:, 48 + e:49 + e].to_broadcast([128, CH]))
            v.memset(WE[0:HALF, 2 * CH:NCHUNK, HID:HID + 1], 1.0 / FEAT).then_inc(S["cnt_done"], 1)

            for k in range(NCHUNK):
                dve.wait_ge(S["xt_mm"], 2 * k + 1)
                src = bank[2 * (k % 2)][0:KCH[k], 0:3 * ROWS].rearrange("p (w h b) -> p w h b", w=3, h=GR)
                dst = XT[0:KCH[k], k, :].rearrange("p (b n) -> p n b", n=N)[:, 1:N, :]\
                    .rearrange("p (h w) b -> p w h b", w=GR)[:, 0:3]
                for w in range(3):
                    ins = v.tensor_copy(dst[:, w], src[:, w])
                ins.then_inc(S["xt_evac_v"], 1)

            dve.wait_ge(S["placed"], 1)
            order = [((0, 0), (0, 1)), ((1, 1), (1, 0)), ((2, 1), (2, 0)), ((3, 0), (3, 1)), ((4, 0), (4, 1))]
            arrive = [16, 48, 48, 16, 16]
            for q, pair in enumerate(order):
                dve.wait_ge(S[f"w{q}_in"], arrive[q])
                for e2, (s, e) in enumerate(pair):
                    for c in range(CH):
                        dst = WE[:, 2 * c + e2, 0:HID]
                        gcol = GP[:, 0, e, s, c:c + 1]
                        if q == 0:
                            ins = v.tensor_scalar(dst, WP[:, s, e, c, :], gcol, None, ALU.mult)
                        else:
                            dve.wait_ge(S["weff"], 6 * (q - 1) + CH * e2 + c + 1)
                            ins = v.scalar_tensor_tensor(out=dst, in0=WP[:, s, e, c, :], scalar=gcol, in1=dst,
                                                         op0=ALU.mult, op1=ALU.add)
                        ins.then_inc(S["weff"], 1)
            dve.wait_ge(S["wh_in"], 16 * 12)
            dve.wait_ge(S["gh_sb"], 1)
            for k in range(2):
                v.tensor_scalar(WE[0:HALF, 2 * CH + k, 0:HID], WH[:, k, :], GH[:, k, 0:1], None, ALU.mult)\
                 .then_inc(S["weff"], 1)

            dve.wait_ge(S["sums_mm"], 1)
            for hf in range(2):
                ins = v.tensor_copy(sums[:, hf, :], bank[5 + hf][0:HALF, 0:2])
            ins.then_inc(S["sums_sb"], 1)
            dve.wait_ge(S["rt_mm"], 1)
            v.tensor_copy(R[0:2, :], bank[7][0:2, 0:HID]).then_inc(S["rt_sb"], 1)
            dve.wait_ge(S["g1_mm"], 1)
            v.tensor_copy(g1n[:, :], bank[7][:, 0:HID]).then_inc(S["g1_sb"], 1)
            for q in range(3):
                dve.wait_ge(S["base_mm"], q + 1)
                w = 2 if q < 2 else 1
                n = 128 if q < 2 else TILES[-1][1]
                v.tensor_copy(BASE[0:n, 2 * q:2 * q + w, :],
                              bank[5 + q][0:n, 0:HID * w].rearrange("p (i n) -> p i n", i=w)).then_inc(S["base_sb"], 1)

            dve.wait_ge(S["base_sb"], 3)
            for i in range(NT + 2):
                if i < NT:
                    n = TILES[i][1]
                    dve.wait_ge(S["emb_mm"], i + 1)
                    link(v.tensor_copy(st[0:n, i, :], bank[i][0:n, HID:HID + 2]))
                    link(v.scalar_tensor_tensor(out=nvar[0:n, i:i + 1], in0=st[0:n, i, 0:1], scalar=st[0:n, i, 0:1],
                                                in1=st[0:n, i, 1:2], op0=ALU.mult, op1=ALU.subtract))
                    v.tensor_scalar(nvar[0:n, i:i + 1], nvar[0:n, i:i + 1], 0.0, None, ALU.min)\
                     .then_inc(S["nvar_ready"], 1)
                if 1 <= i <= NT:
                    k = i - 1
                    n = TILES[k][1]
                    link(v.scalar_tensor_tensor(out=u[0:n, k % 2], in0=g1n[0:n, :], scalar=st[0:n, k, 0:1],
                                                in1=bank[k][0:n, 0:HID], op0=ALU.mult, op1=ALU.add))
                    dve.wait_ge(S["std_ready"], k + 1)
                    link(v.reciprocal(rstd[0:n, k:k + 1], std[0:n, k:k + 1]))
                    v.scalar_tensor_tensor(out=h1[0:n, k], in0=u[0:n, k % 2], scalar=rstd[0:n, k:k + 1],
                                           in1=BASE[0:n, k], op0=ALU.mult, op1=ALU.add).then_inc(S["h1_ready"], 1)
                    dve.wait_ge(S["h1_ready"], k + 1)
                    link(v.bn_stats(bn[0:n, k], h1[0:n, k]))
                    v.bn_aggr(mv[0:n, k], bn[0:n, k]).then_inc(S["mv_ready"], 1)
                if i >= 2:
                    k = i - 2
                    n = TILES[k][1]
                    dve.wait_ge(S["std1_ready"], k + 1)
                    link(v.reciprocal(rstd1[0:n, k:k + 1], std1[0:n, k:k + 1]))
                    v.tensor_scalar(hn[0:n, k], h1[0:n, k], mv[0:n, k, 0:1], rstd1[0:n, k:k + 1],
                                    ALU.subtract, ALU.mult).then_inc(S["hn_ready"], 1)

            dve.wait_ge(S["wt_mm"], 1)
            v.tensor_copy(WQ[0:HALF, 1, 0:2, :], bank[7][0:HALF, 0:2 * HID].rearrange("p (k n) -> p k n", k=2))\
             .then_inc(S["wt_v"], 1)
            for kh in range(2):
                dve.wait_ge(S["wt_mm"], 2)
                for half in range(2):
                    v.tensor_copy(
                        WQ[0:HALF, kh, 2, HALF * half:HALF * (half + 1)].rearrange("p (q j d) -> p j q d", q=2, j=3),
                        bank[5][0:HALF, HID * kh + HALF * half:HID * kh + HALF * (half + 1)]
                        .rearrange("p (j q d) -> p j q d", q=2, j=3)).then_inc(S["wt_v"], 1)

            dve.wait_ge(S["hnt_sb"], NT)
            dve.wait_ge(S["masks_ready"], 3)
            for j in range(3):
                v.tensor_copy(hn3[:, :, :, j, :], hnT[:, :, :].rearrange("p k (b n) -> p k b n", n=N))\
                 .then_inc(S["hn3_ready"], 1)
            for half in range(2):
                for th in range(2):
                    dve.wait_ge(S["qk_mm"], 4 * half + 2 + th + 1)
                    v.tensor_copy(kT[:, half, TH * th:TH * (th + 1)], bank[4 + 2 * half + th][0:HALF, 0:TH])\
                     .then_inc(S["k_sb"], 1)
                dve.wait_ge(S["k_sb"], 2 * (half + 1))
                for hd in range(3):
                    v.tensor_scalar(head_rows(half, hd), kT[:, half, :].rearrange("p (b n) -> p b n", n=N),
                                    mask6[:, hd:hd + 1], None, ALU.mult)\
                     .then_inc(S["k6_v"], 1)
            dve.wait_ge(S["vones_ready"], 1)
            for p in range(NPAIR):
                dve.wait_ge(S["v_mm"], p + 1)
                for bb in range(2):
                    ins = v.tensor_tensor(
                        VB[:, 2 * p + bb, :, 0:D],
                        bank[p % 4][0:G3, HID * bb:HID * (bb + 1)].rearrange("p (h d) -> p h d", d=D),
                        mask12[:, :, :].rearrange("p g j -> p (g j)").unsqueeze(2).to_broadcast([G3, 12, D]),
                        ALU.mult)
                ins.then_inc(S["v_sb"], 1)

            def normalise(p, src, done):
                o = src[0:PP, 0:NH * VW].rearrange("p (h d) -> p h d", d=VW)
                link(v.reciprocal(ro[:, p % 2], o[:, :, D]))
                v.tensor_tensor(On[:, p % 2].rearrange("p (h d) -> p h d", d=D), o[:, :, 0:D],
                                ro[:, p % 2].unsqueeze(2).to_broadcast([PP, NH, D]), ALU.mult).then_inc(done, 1)

            for i in range(NPAIR + 2):
                if i < NPAIR:
                    dve.wait_ge(S["s_mm"], i + 1)
                    s3 = bank[i % 2][0:PP, 0:NH * N].rearrange("p (h m) -> p h m", m=N)
                    link(v.tensor_reduce(mx[:, i % 2], s3, AX.X, ALU.max))
                    if i >= 2:
                        dve.wait_ge(S["pt_mm"], i - 1)
                    v.tensor_tensor(Pr[:, i % 2], s3, mx[:, i % 2].unsqueeze(2).to_broadcast([PP, NH, N]),
                                    ALU.subtract).then_inc(S["p_sub"], 1)
                if i >= 2:
                    p = i - 2
                    dve.wait_ge(S["pv_mm"], p + 1)
                    if p >= 2:
                        dve.wait_ge(S["ot_mm"], p - 1)
                    normalise(p, bank[4 + p % 2], S["on_ready"])

            dve.wait_ge(S["wt_mm"], 3)
            v.tensor_copy(inb[:, :], bank[7][:, 2 * HID:2 * HID + NF]).then_inc(S["inb_sb"], 1)
            v.tensor_copy(WO[0:HALF, :, :], bank[7][0:HALF, 0:2 * HID].rearrange("p (k n) -> p k n", k=2))\
             .then_inc(S["wt_v"], 1)
            WIf = WI[:, :, :].rearrange("p k f -> p (k f)")
            for q in range(3):
                dve.wait_ge(S["wt_mm"], 4 + q)
                v.tensor_copy(WIf[:, 512 * q:512 * (q + 1)], bank[5 + q][0:HALF, :]).then_inc(S["wt_v"], 1)
            for i, (t0, n) in enumerate(TILES):
                dve.wait_ge(S["ysq_ready"], i + 1)
                v.tensor_reduce(ss[0:n, i], ysq[0:n, i % 2].rearrange("p (h d) -> p h d", d=D), AX.X, ALU.add)\
                 .then_inc(S["ss_ready"], 1)
            dve.wait_ge(S["nrm_ready"], 2)
            nl = TILES[-1][1]
            v.tensor_scalar(nrm[:, 0:NT - 1], nrm[:, 0:NT - 1], NORM_EPS, None, ALU.max)
            link(v.tensor_scalar(nrm[0:nl, NT - 1], nrm[0:nl, NT - 1], NORM_EPS, None, ALU.max))
            v.reciprocal(rn[:, 0:NT - 1], nrm[:, 0:NT - 1])
            link(v.reciprocal(rn[0:nl, NT - 1], nrm[0:nl, NT - 1]))
            for i, (t0, n) in enumerate(TILES):
                v.tensor_tensor(Y[0:n, i].rearrange("p (h d) -> p h d", d=D),
                                bank[i][0:n, 0:HID].rearrange("p (h d) -> p h d", d=D),
                                rn[0:n, i].unsqueeze(2).to_broadcast([n, NH, D]), ALU.mult).then_inc(S["y_ready"], 1)
            dve.wait_ge(S["s_mm"], NPAIR)
            dve.wait_ge(S["yt_sb"], NT)
            for half in range(2):
                for hd in range(3):
                    v.tensor_scalar(head_rows(half, hd), YT[:, half, :].rearrange("p (b n) -> p b n", n=N),
                                    mask6[:, hd:hd + 1], None, ALU.mult)\
                     .then_inc(S["t6_v"], 1)

            for i in range(NPAIR + 2):
                if i < NPAIR:
                    dve.wait_ge(S["e1_ready"], i + 1)
                    if i >= 2:
                        dve.wait_ge(S["pv2_mm"], i - 1)
                    v.scalar_tensor_tensor(out=E2[:, i % 2].rearrange("p g t -> p (g t)"),
                                           in0=bank[i % 2][0:G3, 0:8 * N], scalar=0.0,
                                           in1=E1[:, i % 2].rearrange("p g t -> p (g t)"),
                                           op0=ALU.is_ge, op1=ALU.mult).then_inc(S["e2_ready"], 1)
                if i >= 2:
                    p = i - 2
                    dve.wait_ge(S["pv2_mm"], p + 1)
                    if p >= 2:
                        dve.wait_ge(S["ot2_mm"], p - 1)
                    normalise(p, bank[4 + p % 2], S["on2_ready"])

            for i in range(NT + 1):
                if i < NT:
                    n = TILES[i][1]
                    dve.wait_ge(S["y2_mm"], i + 1)
                    link(v.tensor_tensor(h2[0:n, i], bank[i][0:n, 0:HID], h1[0:n, i], ALU.add))
                    link(v.bn_stats(bn2[0:n, i], h2[0:n, i]))
                    v.bn_aggr(mv2[0:n, i], bn2[0:n, i]).then_inc(S["h2_mv"], 1)
                if i >= 1:
                    k = i - 1
                    n = TILES[k][1]
                    dve.wait_ge(S["std2_ready"], k + 1)
                    link(v.reciprocal(rstd2[0:n, k:k + 1], std2[0:n, k:k + 1]))
                    v.tensor_scalar(hn2[0:n, k], h2[0:n, k], mv2[0:n, k, 0:1], rstd2[0:n, k:k + 1],
                                    ALU.subtract, ALU.mult).then_inc(S["hn2_ready"], 1)
            for i, (t0, n) in enumerate(TILES):
                dve.wait_ge(S["down_mm"], i + 1)
                v.tensor_tensor(res[0:n, i], bank[3 + i][0:n, 0:HID], h2[0:n, i], ALU.add).then_inc(S["res_ready"], 1)

        @block.tensor
        def _(pe):
            t = nc.tensor
            pe.wait_ge(S["gb_in"], 32)
            pe.wait_ge(S["consts_ready"], 12)
            pl = bank[4]
            t.matmul(pl[:, 0:6], sh[0][:, :], GN[:, :, 0, 1, :], start=True, stop=True)
            t.matmul(pl[:, 8:14], sh[1][:, :], GN[:, :, 1, 2, :], start=True, stop=True)
            for k in range(2):
                t.matmul(pl[:, 16 + 6 * k:22 + 6 * k], sh[2][:, :], GN[:, k, :, 3, :], start=True, stop=True)
                ins = t.matmul(pl[:, 32 + 6 * k:38 + 6 * k], sh[3][:, :], GN[:, k, :, 4, :], start=True, stop=True)
            ins.then_inc(S["placed_mm"], 1)
            for e in range(2):
                ms = [ident, ident, sh[1 - e], sh[2], sh[3]]
                for q, m in enumerate(ms):
                    ins = t.matmul(pl[:, 48 + e:49 + e], m[:, :], inv_n[:, :], start=q == 0, stop=q == 4)
            ins.then_inc(S["placed_mm"], 1)
            for k in range(2):
                takes = [[(0, 0, 1)], [(1, 1, 2)]] if k == 0 else [[(2, 0, 3), (3, 1, 3)], [(4, 0, 4), (5, 1, 4)]]
                every = [(q, e, s, side, c) for side in range(2) for q, e, s in takes[side] for c in range(CH)]
                for n, (q, e, s, side, c) in enumerate(every):
                    z0 = ZP - PS * (CH * side + c)
                    ins = t.matmul(pl[0:HALF, 56 + 2 * k:58 + 2 * k], sel[:, q, z0:z0 + HALF], GN[:, :, e, s, c],
                                   start=n == 0, stop=n == len(every) - 1)
            ins.then_inc(S["placed_mm"], 1)

            for k in range(NCHUNK):
                if k < 2 * CH:
                    pe.wait_ge(S["xr_a" if k % 2 else "xr_v"], k // 2 + 1)
                elif k == 2 * CH:
                    pe.wait_ge(S["xlr_ready"], 4 * CH)
                else:
                    pe.wait_ge(S["xtb_ready"], 1)
                if k >= 2:
                    pe.wait_ge(S["xt_evac_v"], k - 1)
                    pe.wait_ge(S["xt_evac_a"], k - 1)
                for wx in range(GR):
                    if k < 2 * CH:
                        src = XR[:, k, wx]
                    elif k == 2 * CH:
                        src = XLR[:, wx].rearrange("p s c r -> p (s c r)")
                    else:
                        src = XTBR[:, wx].rearrange("p s q -> p (s q)")
                    dst = bank[2 * (k % 2) + wx // 3][0:KCH[k], ROWS * (wx % 3):ROWS * (wx % 3 + 1)]
                    ins = t.transpose(dst, src, ident[0:ROWS, 0:ROWS])
                    if wx % 3 == 2:
                        ins.then_inc(S["xt_mm"], 1)

            pe.wait_ge(S["placed"], 1)
            slabs = [(s, e, c) for s in range(NSH) for e in range(2) for c in range(CH)]
            arrive = [16, 48, 48, 16, 16]
            for q, (s, e, c) in enumerate(slabs):
                if q % 6 == 0:
                    pe.wait_ge(S[f"w{s}_in"], arrive[s])
                for hf in range(2):
                    t.matmul(bank[5 + hf][0:HALF, 0:2], WP[:, s, e, c, HALF * hf:HALF * (hf + 1)], GP[:, :, e, s, c],
                             start=q == 0, stop=False)
            pe.wait_ge(S["wh_in"], 16 * 12)
            pe.wait_ge(S["gh_sb"], 1)
            for k in range(2):
                for hf in range(2):
                    ins = t.matmul(bank[5 + hf][0:HALF, 0:2], WH[:, k, HALF * hf:HALF * (hf + 1)], GH[:, k, :],
                                   start=False, stop=k == 1)
            ins.then_inc(S["sums_mm"], 1)

            pe.wait_ge(S["xs_p"], 4)
            pe.wait_ge(S["xs_a"], NCHUNK - 4)
            pe.wait_ge(S["cnt_done"], 1)
            pe.wait_ge(S["xt_evac_v"], NCHUNK)
            pe.wait_ge(S["xt_evac_a"], NCHUNK)
            for i, (t0, n) in enumerate(TILES):
                for k in range(NCHUNK):
                    t.matmul(bank[i][0:n, HID + 1:HID + 2], XS[0:KCH[k], k, t0:t0 + n], WE[0:KCH[k], k, HID:HID + 1],
                             start=k == 0, stop=k == NCHUNK - 1)

            def emb(i, ks):
                t0, n = TILES[i]
                for k in ks:
                    ins = t.matmul(bank[i][0:n, 0:HID + 1], XT[0:KCH[k], k, t0:t0 + n], WE[0:KCH[k], k, :],
                                   start=k == 0, stop=k == NCHUNK - 1)
                return ins

            pe.wait_ge(S["weff"], 6 * NSH)
            for k in range(4):
                for i in range(NT):
                    emb(i, [k])
            pe.wait_ge(S["sums_sb"], 1)
            for hf in range(2):
                ins = t.transpose(bank[7][0:2, HALF * hf:HALF * (hf + 1)], sums[:, hf, :], ident[0:HALF, 0:HALF])
            ins.then_inc(S["rt_mm"], 1)
            pe.wait_ge(S["weff"], 6 * NSH + 2)
            emb(0, range(4, NCHUNK)).then_inc(S["emb_mm"], 1)
            pe.wait_ge(S["rt_sb"], 1)
            pe.wait_ge(S["rows_in"], 32)
            pe.wait_ge(S["masks_ready"], 2)
            t.matmul(bank[7][:, 0:HID], neg0[:, :], R[:, :], start=True, stop=True).then_inc(S["g1_mm"], 1)
            for q in range(3):
                if q == 2:
                    pe.wait_ge(S["g1_sb"], 1)
                for i in (2 * q, 2 * q + 1):
                    if i < NT:
                        t0, n = TILES[i]
                        ins = t.matmul(bank[5 + q][0:n, HID * (i % 2):HID * (i % 2 + 1)],
                                       IND[:, :, :].rearrange("p b n -> p (b n)")[:, t0:t0 + n], R[:, :],
                                       start=True, stop=True)
                ins.then_inc(S["base_mm"], 1)
            for i in range(1, NT):
                emb(i, range(4, NCHUNK)).then_inc(S["emb_mm"], 1)

            pe.wait_ge(S["qkv_in"], 16)
            pe.wait_ge(S["base_sb"], 3)
            for kh in range(2):
                for o in range(4):
                    ins = t.transpose(bank[6 + kh][0:HALF, HALF * o:HALF * (o + 1)],
                                      qkvw[:, o, HALF * kh:HALF * (kh + 1)], ident[0:HALF, 0:HALF])
            ins.then_inc(S["wt_mm"], 1)
            for kh in range(2):
                for o in range(2):
                    ins = t.transpose(bank[5][0:HALF, HID * kh + HALF * o:HID * kh + HALF * (o + 1)],
                                      qkvw[:, 4 + o, HALF * kh:HALF * (kh + 1)], ident[0:HALF, 0:HALF])
            ins.then_inc(S["wt_mm"], 1)

            def to_features(src, i, dst):
                n = TILES[i][1]
                for kh in range(2):
                    ins = t.transpose(dst[0:HALF, 128 * kh:128 * kh + n], src[0:n, i, HALF * kh:HALF * (kh + 1)],
                                      ident[0:n, 0:n])
                return ins

            pe.wait_ge(S["wt_v"], 5)
            pe.wait_ge(S["wt_a"], 1)
            for i in range(NT):
                pe.wait_ge(S["hn_ready"], i + 1)
                if i >= 2:
                    pe.wait_ge(S["hnt_sb"], i - 1)
                to_features(hn, i, bank[5 + i % 2]).then_inc(S["hnt_mm"], 1)

            pe.wait_ge(S["ones_rows"], 2)
            pe.wait_ge(S["bias_in"], 16 * 7)
            pe.wait_ge(S["hnt_sb"], NT)
            for half in range(2):
                for qk in range(2):
                    for th in range(2):
                        dst = bank[4 * qk + 2 * half + th][0:HALF, 0:TH]
                        for kh in range(2):
                            K = HALF + kh
                            ins = t.matmul(dst, WQ[0:K, kh, qk, HALF * half:HALF * (half + 1)],
                                           hnT[0:K, kh, TH * th:TH * (th + 1)], start=kh == 0, stop=kh == 1)
                        ins.then_inc(S["qk_mm"], 1)
            pe.wait_ge(S["q_sb"], 4)
            pe.wait_ge(S["hn3_ready"], 3)
            for p in range(NPAIR):
                if p >= 4:
                    pe.wait_ge(S["v_sb"], p - 3)
                for bb in range(2):
                    b = 2 * p + bb
                    for kh in range(2):
                        K = HALF + kh
                        ins = t.matmul(bank[p % 4][0:G3, HID * bb:HID * (bb + 1)],
                                       hn3[0:K, kh, b].rearrange("p j n -> p (j n)"),
                                       WQ[0:K, kh, 2, :], start=kh == 0, stop=kh == 1)
                ins.then_inc(S["v_mm"], 1)

            def rows_of(bb):
                return 64 if bb == 0 else N

            def scores(p):
                for bb in range(2):
                    b, M = 2 * p + bb, rows_of(bb)
                    for half in range(2):
                        ins = t.matmul(bank[p % 2][64 * bb:64 * bb + M, 6 * N * half:6 * N * (half + 1)],
                                       qT[:, half, N * b:N * b + M],
                                       K6[:, half, :, b].rearrange("p q j n -> p q (j n)"),
                                       start=True, stop=True)
                return ins

            def values(p, weights, dst):
                for bb in range(2):
                    for g in range(4):
                        o = dst[64 * bb:64 * bb + rows_of(bb), 0:NH * VW].rearrange(
                            "p (h j q d) -> p h q j d", h=2, j=3, q=2)[:, g // 2, g % 2]
                        ins = t.matmul(o, weights(g, bb),
                                       VB[:, 2 * p + bb, 3 * g:3 * g + 3, :].rearrange("p j d -> p (j d)"),
                                       start=True, stop=True)
                return ins

            def out_features(p, dst):
                for kh in range(2):
                    ins = t.transpose(dst[0:HALF, 128 * kh:128 * kh + PP], On[:, p % 2, HALF * kh:HALF * (kh + 1)],
                                      ident[0:PP, 0:PP])
                return ins

            pe.wait_ge(S["k6_v"], 6)
            pe.wait_ge(S["k6_a"], 2)
            pe.wait_ge(S["k6_p"], 4)
            pe.wait_ge(S["v_sb"], NPAIR)
            for i in range(NPAIR + 3):
                if i < NPAIR:
                    if i >= 2:
                        pe.wait_ge(S["p_sub"], i - 1)
                    scores(i).then_inc(S["s_mm"], 1)
                if 1 <= i <= NPAIR:
                    p = i - 1
                    pe.wait_ge(S["p_exp"], p + 1)
                    if p >= 2:
                        pe.wait_ge(S["pt_sb"], p - 1)
                    for g in range(4):
                        ins = t.transpose(bank[2 + p % 2][0:G3, PP * g:PP * (g + 1)],
                                          Pr[:, p % 2, 3 * g:3 * g + 3, :].rearrange("p h m -> p (h m)"),
                                          ident[0:PP, 0:PP])
                    ins.then_inc(S["pt_mm"], 1)
                if 2 <= i <= NPAIR + 1:
                    p = i - 2
                    pe.wait_ge(S["pt_sb"], p + 1)
                    if p >= 2:
                        pe.wait_ge(S["on_ready"], p - 1)
                    values(p, lambda g, bb: PT[:, p % 2, g, 64 * bb:64 * bb + rows_of(bb)], bank[4 + p % 2])\
                        .then_inc(S["pv_mm"], 1)
                if i >= 3:
                    p = i - 3
                    pe.wait_ge(S["on_ready"], p + 1)
                    if p >= 2:
                        pe.wait_ge(S["ot_sb"], p - 1)
                    out_features(p, bank[6 + p % 2]).then_inc(S["ot_mm"], 1)

            pe.wait_ge(S["proj_in"], 16)
            pe.wait_ge(S["ot_sb"], NPAIR)
            for kh in range(2):
                for o in range(2):
                    src = projw[:, o, HALF * kh:HALF * (kh + 1)]
                    ins = t.transpose(bank[7][0:HALF, HID * kh + HALF * o:HID * kh + HALF * (o + 1)], src,
                                      ident[0:HALF, 0:HALF])
            t.transpose(bank[7][:, 2 * HID:2 * HID + NF], inbr[:, :], ident[0:NF, 0:NF]).then_inc(S["wt_mm"], 1)

            def project(i):
                t0, n = TILES[i]
                for kh in range(2):
                    K = HALF + kh
                    ins = t.matmul(bank[i][0:n, 0:HID], OT[0:K, kh, t0:t0 + n], WO[0:K, kh, :],
                                   start=kh == 0, stop=kh == 1)
                return ins

            pe.wait_ge(S["ones_rows"], 2)
            pe.wait_ge(S["wt_v"], 6)
            for i in range(NT):
                project(i).then_inc(S["y_mm"], 1)

            pe.wait_ge(S["ffnw_in"], 32)
            for q in range(2 * NF):
                kh, f = divmod(q, NF)
                ins = t.transpose(bank[5 + q // 4][0:HALF, 128 * (q % 4):128 * (q % 4 + 1)],
                                  inw[:, f, HALF * kh:HALF * (kh + 1)], ident[:, :])
                if q % 4 == 3:
                    ins.then_inc(S["wt_mm"], 1)

            pe.wait_ge(S["wt_v"], 9)
            for i in range(NT):
                pe.wait_ge(S["y_ready"], i + 1)
                if i >= 2:
                    pe.wait_ge(S["yt_sb"], i - 1)
                to_features(Y, i, bank[5 + i % 2]).then_inc(S["yt_mm"], 1)

            pe.wait_ge(S["yt_sb"], NT)
            pe.wait_ge(S["t6_v"], 6)
            pe.wait_ge(S["t6_a"], 2)
            pe.wait_ge(S["t6_p"], 4)
            for i in range(NPAIR + 3):
                if i < NPAIR:
                    if i >= 2:
                        pe.wait_ge(S["e2_ready"], i - 1)
                    for g in range(4):
                        half, par = divmod(g, 2)
                        for bb in range(2):
                            cols = slice(N * (2 * i + bb), N * (2 * i + bb + 1))
                            ins = t.matmul(bank[i % 2][0:G3, N * (2 * g + bb):N * (2 * g + bb + 1)],
                                           K6[:, half, par, 2 * i + bb].rearrange("p j n -> p (j n)"), YT[:, half, cols],
                                           start=True, stop=True)
                    ins.then_inc(S["s2_mm"], 1)
                if 2 <= i <= NPAIR + 1:
                    p = i - 2
                    pe.wait_ge(S["e2_ready"], p + 1)
                    if p >= 2:
                        pe.wait_ge(S["on2_ready"], p - 1)
                    values(p, lambda g, bb: E2[:, p % 2, g, N * bb:N * bb + rows_of(bb)], bank[4 + p % 2])\
                        .then_inc(S["pv2_mm"], 1)
                if i >= 3:
                    p = i - 3
                    pe.wait_ge(S["on2_ready"], p + 1)
                    if p >= 2:
                        pe.wait_ge(S["ot2_sb"], p - 1)
                    out_features(p, bank[6 + p % 2]).then_inc(S["ot2_mm"], 1)

            pe.wait_ge(S["ot2_sb"], NPAIR)
            for i in range(NT):
                project(i).then_inc(S["y2_mm"], 1)

            for i in range(NT):
                pe.wait_ge(S["hn2_ready"], i + 1)
                if i >= 2:
                    pe.wait_ge(S["hn2t_sb"], i - 1)
                to_features(hn2, i, bank[5 + i % 2]).then_inc(S["hn2t_mm"], 1)
            for th in range(2):
                pe.wait_ge(S["hn2t_sb"], 3 if th == 0 else NT)
                for f in range(NF):
                    q = NF * th + f
                    if q >= 3:
                        pe.wait_ge(S["gelu_done"], q - 2)
                    for kh in range(2):
                        ins = t.matmul(bank[q % 3][:, 0:TH], WI[:, kh, 128 * f:128 * (f + 1)],
                                       hn2T[:, kh, TH * th:TH * (th + 1)], start=kh == 0, stop=kh == 1)
                    ins.then_inc(S["up_mm"], 1)
            for i, (t0, n) in enumerate(TILES):
                pe.wait_ge(S["gelu_done"], NF if t0 + n <= TH else 2 * NF)
                for f in range(NF):
                    ins = t.matmul(bank[3 + i][0:n, 0:HID], hT[:, f, t0:t0 + n], w2[:, f, :],
                                   start=f == 0, stop=f == NF - 1)
                ins.then_inc(S["down_mm"], 1)


_INS = ["x", "cls_tok", "L0_tok_ln_gamma", "L0_tok_ln_beta", "L0_tok_W", "L0_tok_b", "L0_attn_qkv_w",
        "L0_attn_qkv_b", "L0_attn_proj_w", "L0_attn_proj_b", "L0_ffn_in_weight", "L0_ffn_in_bias",
        "L0_ffn_out_weight"]


def kernel(**inputs):
    import numpy as _np
    import concourse.bacc as _bacc
    from concourse import mybir as _mybir
    from concourse.bass_utils import run_bass_kernel_spmd as _run

    nc = _bacc.Bacc("TRN2", target_bir_lowering=False, num_devices=1)
    arrays, args = {}, []
    for name in _INS:
        a = _np.ascontiguousarray(inputs[name])
        arrays[f"in_{name}"] = a
        args.append(nc.dram_tensor(f"in_{name}", a.shape, _mybir.dt.from_np(a.dtype), kind="ExternalInput").ap())
    args.append(nc.dram_tensor("out_0", (NIMG, N, HID), F32, kind="ExternalOutput").ap())
    vit(nc, *args)
    r = _run(nc, [arrays], core_ids=[0])
    return r.results[0]["out_0"]
```

```python
from contextlib import ExitStack

import concourse.bass as bass
from concourse import mybir

F32 = mybir.dt.float32
ALU = mybir.AluOpType
ACT = mybir.ActivationFunctionType
AX = mybir.AxisListType

NIMG, CH, IMG, PS = 16, 3, 96, 16
GR = IMG // PS
ROWS = NIMG * GR
N = GR * GR + 1
T = NIMG * N
HID, HALF = 192, 96
NH, D = 12, 16
NSH = 5
FEAT = PS * PS * CH * NSH
NCHUNK = 2 * CH + 2
FFN = 768
NF = FFN // 128
NT = -(-T // 128)
TILES = [(128 * i, min(128, T - 128 * i)) for i in range(NT)]
NPAIR = NIMG // 2
PP = 64 + N
G3 = 3 * N
VW = D + 1
TH = T // 2
EPS = 1e-5
NORM_EPS = 1e-12
SCALE = float(D) ** -0.5
SIM_SCALE = 10.0
LAST_PAIR = [(t0 + n - 1) // (2 * N) for t0, n in TILES]
Y_STEP = [p + 4 for p in LAST_PAIR]
ROOT_STEP = [max(y + 1, NPAIR) for y in Y_STEP]
T_STEP = [r + 1 for r in ROOT_STEP]
STEPS = T_STEP[-1] + 1
UP_BANKS, DOWN_BANKS = (0, 1, 6), (3, 4, 7, 2, 5)
EARLY = NPAIR // 2
MASKED = [(half, hd) for hd in range(6) for half in range(2)]
KCH = [128] * (2 * CH) + [HALF, HALF]


def vit(nc, x, cls_tok, gamma, beta, W, b_tok, qkv_w, qkv_b, proj_w, proj_b, in_w, in_b, out_w, out):
    with ExitStack() as ctx:
        def sb(name, shape):
            return ctx.enter_context(nc.sbuf_tensor(name, shape, F32))

        def sem(name):
            return ctx.enter_context(nc.semaphore(name))

        bank = [ctx.enter_context(nc.psum_tensor(f"bank{i}", [128, 512], F32)) for i in range(8)]

        X = sb("X", [ROWS, CH, PS * IMG])
        XTB = sb("XTB", [ROWS, 2, CH, IMG])
        XTBR = sb("XTBR", [ROWS, GR, 2 * CH, PS])
        XLR = sb("XLR", [ROWS, GR, 2, CH, PS])
        XTS = sb("XTS", [128, 2, NCHUNK, T])
        XT, XS = XTS[:, 0], XTS[:, 1]
        XR = XTS[0:ROWS, 1].rearrange("p k t -> p (k t)")[:, 0:2 * CH * GR * 128].rearrange(
            "p (k w f) -> p k w f", k=2 * CH, w=GR)
        WP = sb("WP", [128, NSH, 2, CH, HID])
        WH = sb("WH", [HALF, 2, HID])
        WE = sb("WE", [128, NCHUNK, HID + 1])
        GN = sb("GN", [128, 2, 2, NSH, CH])
        GP = sb("GP", [128, 2, 2, NSH, CH])
        GH = sb("GH", [HALF, 2, 2])
        ident = sb("ident", [128, 128])
        sh = [sb(f"sh{s}", [128, 128]) for s in range(4)]
        inv_n = sb("inv_n", [128, 4])
        R = sb("R", [4, HID])
        IND = sb("IND", [4, NIMG, N])
        neg0 = sb("neg0", [4, 128])
        g1n = sb("g1n", [128, HID])
        BASE = sb("BASE", [128, NT, HID])
        st = sb("st", [128, NT, 2])
        nvar = sb("nvar", [128, NT])
        std = sb("std", [128, NT])
        rstd = sb("rstd", [128, NT])
        u = sb("u", [128, 2, HID])
        h1 = sb("h1", [128, NT, HID])
        bn = sb("bn", [128, NT, 6])
        mv = sb("mv", [128, NT, 2])
        std1 = sb("std1", [128, NT])
        rstd1 = sb("rstd1", [128, NT])
        hn = sb("hn", [128, NT, HID])
        hnT = sb("hnT", [HALF + 1, 2, T])
        eps = sb("eps", [128, 1])
        m10 = sb("m10", [128, 1])
        qkvw = sb("qkvw", [HALF, 6, HID])
        projw = sb("projw", [HALF, 2, HID])
        inw = sb("inw", [128, NF, HID])
        w2 = sb("w2", [128, NF, HID])
        inbr = sb("inbr", [NF, 128])
        inb = sb("inb", [128, NF])
        WQ = sb("WQ", [HALF + 1, 2, 3, HID])
        WO = sb("WO", [HALF + 1, 2, HID])
        WI = sb("WI", [HALF, 2, FFN])
        mask6 = sb("mask6", [HALF, 6])
        mask12 = sb("mask12", [G3, 4, 3])
        qT, kT = (X[:, :, :].rearrange("p c w -> p (c w)")[:, 2 * T * k:2 * T * (k + 1)]
                  .rearrange("p (h t) -> p h t", h=2) for k in range(2))
        K6 = XTS[0:HALF].rearrange("p a k t -> p (a k t)")[:, 0:2 * 6 * T].rearrange(
            "p (h q b j n) -> p h q b j n", h=2, q=2, j=3, n=N)
        VB = sb("VB", [G3, NIMG, 4 * 3, VW])
        mx = sb("mx", [PP, 2, NH])
        Pr = sb("Pr", [PP, 2, NH, N])
        PT = sb("PT", [G3, 2, 4, PP])
        ro = sb("ro", [PP, 2, NH])
        On = sb("On", [PP, 2, HID])
        OT = sb("OT", [HALF + 1, 2, T])
        ysq = sb("ysq", [128, 2, HID])
        ss = sb("ss", [128, NT, NH])
        nrm = sb("nrm", [128, NT, NH])
        rn = sb("rn", [128, NT, NH])
        Y = sb("Y", [128, NT, HID])
        YT = sb("YT", [HALF, 2, T])
        E1 = sb("E1", [G3, 2, 4, 2 * N])
        E2 = sb("E2", [G3, 2, 4, 2 * N])
        h2 = sb("h2", [128, NT, HID])
        bn2 = sb("bn2", [128, NT, 6])
        mv2 = sb("mv2", [128, NT, 2])
        std2 = sb("std2", [128, NT])
        rstd2 = sb("rstd2", [128, NT])
        hn2 = sb("hn2", [128, NT, HID])
        hn2T = sb("hn2T", [HALF, 2, T])
        hn3 = WP[0:HALF + 1].rearrange("p s e c n -> p (s e c n)")[:, 0:2 * 3 * T].rearrange(
            "p (k b j n) -> p k b j n", k=2, j=3, n=N)
        hT = WP[:, :, :, :, :].rearrange("p s e c n -> p (s e c n)")[:, 0:NF * T].rearrange("p (f t) -> p f t", f=NF)
        res = sb("res", [128, NT, HID])

        S = {}
        for name in (
            "gb_in x0_in x1_in x2_in xtb_in w0_in w1_in w2_in w3_in w4_in wh_in gh_in rows_in qkv_in proj_in "
            "ffnw_in bias_in out_done "
            "pool_step consts_ready wzero masks_ready ones_rows xlr_ready xtb_ready xr_v xr_a xcls_zero vones_ready "
            "dve_step act_step "
            "placed_mm placed cnt_done xt_mm xt_evac_v xt_evac_a xs_a weff weff_a xs_sum sq_mm gp_own sums_mm "
            "sums_sb g1_mm g1_sb base_mm base_sb wt_mm wt_a "
            "emb_mm nvar_ready std_ready h1_ready mv_ready std1_ready hn_ready hnt_mm hnt_sb hn3_early hn3_late q_mm k_mm q_sb k_sb "
            "k6_v k6_a v_mm v_sb "
            "s_mm p_sub p_exp pt_mm pt_sb pv_mm on_ready ot_mm ot_sb "
            "y_mm ysq_ready ss_ready nrm_ready y_ready yt_mm yt_sb t6_v t6_a wo_sb wi_sb ysb_ready "
            "s2_mm e1_ready e2_ready pv2_mm on2_ready ot2_mm ot2_sb "
            "y2_mm h2_mv std2_ready hn2_ready hn2t_mm hn2t_sb up_mm gelu_done down_mm res_ready"
        ).split():
            S[name] = sem(name)

        x_v = x.rearrange("b c (h r) w -> h b c (r w)", r=PS)
        W_v = W.rearrange("(p e s c) n -> p e s (c n)", p=128, e=2, s=NSH)
        W_px = W.rearrange("(r q s c) n -> r q s c n", r=PS, q=PS, s=NSH)
        g_v = [v.rearrange("(p k) -> p k", p=128) for v in (gamma, beta)]
        out_v = out.rearrange("b n k -> (b n) k")
        WPf = WP[:, :, :, :, :].rearrange("p s e c n -> p s e (c n)")

        def halo_rows(v, k, side):
            if k == 0:
                return v[:, 0 if side == 0 else PS - 1, 1 + side].rearrange("r c n -> c r n")
            return v[0 if side == 0 else PS - 1, :, 3 + side].rearrange("q c n -> c q n")

        def head_rows(half, hd, th):
            return K6[:, half, hd // 3, NIMG // 2 * th:NIMG // 2 * (th + 1), hd % 3, :]

        def tokens(buf, half, th):
            return buf[:, half, TH * th:TH * (th + 1)].rearrange("p (b n) -> p b n", n=N)

        def reorder(c, e):
            return (XR[:, 2 * c + e].rearrange("p w (r h) -> p w r h", h=8),
                    X[:, c, :].rearrange("p (r w h e) -> p e w r h", w=GR, h=8, e=2)[:, e])

        block = ctx.enter_context(nc.Block())

        @block.sync
        def _(sp):
            for k in range(2):
                sp.dma_start(GN[:, k].rearrange("p e s c -> p (e s c)"), g_v[k]).then_inc(S["gb_in"], 16)
            for c in range(CH):
                sp.dma_start(X[:, c, :], x_v[:, :, c]).then_inc(S[f"x{c}_in"], 16)
            for side in range(2):
                edge, h0 = (0, 1) if side == 0 else (GR - 1, 0)
                y = (PS * edge - 1) % IMG if side == 0 else (PS * edge + PS) % IMG
                sp.dma_start(XTB[NIMG * edge:NIMG * (edge + 1), side], x[:, :, y, :]).then_inc(S["xtb_in"], 16)
                y0 = PS - 1 if side == 0 else PS
                for c in range(CH):
                    src = x[:, c, y0:y0 + PS * (GR - 2) + 1:PS, :].rearrange("b h w -> h b w")
                    sp.dma_start(XTB[NIMG * h0:NIMG * (h0 + GR - 1), side, c], src).then_inc(S["xtb_in"], 16)
            sp.dma_start(WPf[:, 0], W_v[:, :, 0]).then_inc(S["w0_in"], 16)
            sp.dma_start(WPf[:, 1, 1], W_v[:, 1, 1]).then_inc(S["w1_in"], 16)
            sp.dma_start(WPf[:, 2, 0], W_v[:, 0, 2]).then_inc(S["w2_in"], 16)
            sp.wait_ge(S["wzero"], 4)
            sp.dma_start(WPf[0:112, 1, 0], W_v[1:113, 0, 1]).then_inc(S["w1_in"], 16)
            sp.dma_start(WPf[112:127, 1, 0], W_v[113:128, 0, 1]).then_inc(S["w1_in"], 16)
            sp.dma_start(WPf[1:113, 2, 1], W_v[0:112, 1, 2]).then_inc(S["w2_in"], 16)
            sp.dma_start(WPf[113:128, 2, 1], W_v[112:127, 1, 2]).then_inc(S["w2_in"], 16)
            sp.dma_start(WPf[0:120, 3], W_v[8:128, :, 3]).then_inc(S["w3_in"], 16)
            sp.dma_start(WPf[8:128, 4], W_v[0:120, :, 4]).then_inc(S["w4_in"], 16)
            for k in range(2):
                for side in range(2):
                    src = halo_rows(W_px, k, side)
                    sp.dma_start(WH[48 * side:48 * (side + 1), k, :], src).then_inc(S["wh_in"], 16)
                    for n, v in enumerate((gamma, beta)):
                        px = v.rearrange("(r q s c n) -> r q s c n", r=PS, q=PS, s=NSH, n=1)
                        sp.dma_start(GH[48 * side:48 * (side + 1), k, n:n + 1], halo_rows(px, k, side),
                                     allow_slow_non_contiguous=True)\
                          .then_inc(S["gh_in"], 16)
            sp.dma_start(R[2:3, :], b_tok.rearrange("(a n) -> a n", a=1)).then_inc(S["rows_in"], 16)
            sp.dma_start(R[3:4, :], cls_tok.rearrange("a b n -> (a b) n")).then_inc(S["rows_in"], 16)
            sp.dma_start(qkvw[:, :, :], qkv_w.rearrange("(o p) n -> p o n", p=HALF)).then_inc(S["qkv_in"], 16)
            sp.dma_start(projw[:, :, :], proj_w.rearrange("(o p) n -> p o n", p=HALF)).then_inc(S["proj_in"], 16)
            sp.dma_start(WQ[HALF:HALF + 1, 1, 0:2, :], qkv_b[0:2 * HID].rearrange("(a k n) -> a k n", a=1, k=2))\
              .then_inc(S["bias_in"], 16)
            for half in range(2):
                for par in range(2):
                    a = HALF * half + 48 * par
                    src = qkv_b[2 * HID + HALF * half:2 * HID + HALF * (half + 1)].rearrange(
                        "(a j q d) -> q a j d", a=1, q=2, d=D)[par]
                    sp.dma_start(WQ[HALF:HALF + 1, 1, 2, a:a + 48].rearrange("a (j d) -> a j d", d=D), src)\
                      .then_inc(S["bias_in"], 16)
            sp.dma_start(WO[HALF:HALF + 1, 1, :], proj_b.rearrange("(a n) -> a n", a=1)).then_inc(S["bias_in"], 16)
            sp.dma_start(inbr[:, :], in_b.rearrange("(f p) -> f p", p=128)).then_inc(S["bias_in"], 16)
            sp.dma_start(inw[:, :, :], in_w.rearrange("(f p) n -> p f n", p=128)).then_inc(S["ffnw_in"], 16)
            sp.dma_start(w2[:, :, :], out_w.rearrange("(f p) n -> p f n", p=128)).then_inc(S["ffnw_in"], 16)
            for i, (t0, n) in enumerate(TILES):
                sp.wait_ge(S["res_ready"], i + 1)
                sp.dma_start(out_v[t0:t0 + n, :], res[0:n, i, :]).then_inc(S["out_done"], 16)
            sp.wait_ge(S["out_done"], 16 * NT)

        @block.gpsimd
        def _(pool):
            g = nc.gpsimd
            steps = [0]

            def link(ins):
                steps[0] += 1
                ins.then_inc(S["pool_step"], 1)
                pool.wait_ge(S["pool_step"], steps[0])

            g.memset(ident[:, :], 0.0).then_inc(S["pool_step"], 1)
            for m in sh:
                g.memset(m[:, :], 0.0).then_inc(S["pool_step"], 1)
            steps[0] = 5
            pool.wait_ge(S["pool_step"], 5)

            def diagonal(m, base, lo, hi):
                v = m[:, :].rearrange("p (a h) -> p a h", h=8)[:, :, lo:hi]
                return g.affine_select(out=v, in_=v, compare_op=ALU.not_equal, fill=1.0, base=-base - lo,
                                       pattern=[[-8, 16], [-1, hi - lo]], channel_multiplier=1)

            diagonal(ident, 0, 0, 8).then_inc(S["consts_ready"], 1)
            diagonal(sh[0], 1, 0, 7).then_inc(S["consts_ready"], 1)
            diagonal(sh[1], -1, 1, 8).then_inc(S["consts_ready"], 1)
            diagonal(sh[2], 8, 0, 8).then_inc(S["consts_ready"], 1)
            diagonal(sh[3], -8, 0, 8).then_inc(S["consts_ready"], 1)
            g.memset(inv_n[:, 0:2], 1.0 / FEAT).then_inc(S["consts_ready"], 1)
            g.memset(inv_n[:, 2:4], 2.0 / FEAT).then_inc(S["consts_ready"], 1)
            g.memset(eps[:, :], EPS).then_inc(S["consts_ready"], 1)
            g.memset(m10[:, :], -SIM_SCALE).then_inc(S["consts_ready"], 1)
            g.memset(XT[:, :, :].rearrange("p k (b n) -> p k b n", n=N)[:, :, :, 0], 0.0).then_inc(S["xcls_zero"], 1)

            for c in range(CH):
                pool.wait_ge(S[f"x{c}_in"], 16)
                Xc = X[:, c, :].rearrange("p (r w) -> p w r", w=IMG)
                g.tensor_copy(XLR[:, 1:GR, 0, c, :], Xc[:, PS - 1:IMG - 1:PS, :]).then_inc(S["xlr_ready"], 1)
                g.tensor_copy(XLR[:, 0, 0, c, :], Xc[:, IMG - 1, :]).then_inc(S["xlr_ready"], 1)
                g.tensor_copy(XLR[:, 0:GR - 1, 1, c, :], Xc[:, PS:IMG:PS, :]).then_inc(S["xlr_ready"], 1)
                g.tensor_copy(XLR[:, GR - 1, 1, c, :], Xc[:, 0, :]).then_inc(S["xlr_ready"], 1)

            
            link(g.memset(IND[:, :, 1:N], 1.0))
            link(g.memset(IND[:, :, 0:1], 0.0))
            link(g.affine_select(out=IND[:, :, 1:N], in_=IND[:, :, 1:N], compare_op=ALU.not_equal, fill=0.0,
                                 base=-3, pattern=[[0, NIMG], [0, N - 1]], channel_multiplier=1))
            link(g.affine_select(out=IND[:, :, 0:1], in_=IND[:, :, 0:1], compare_op=ALU.not_equal, fill=1.0,
                                 base=-3, pattern=[[0, NIMG], [0, 1]], channel_multiplier=1))
            link(g.memset(neg0[:, :], 0.0))
            g.memset(neg0[0:1, :], -1.0).then_inc(S["masks_ready"], 1)
            g.memset(IND[0:1, :, :], 0.0).then_inc(S["masks_ready"], 1)
            link(g.memset(mask6[:, :], 1.0))
            v6 = mask6[:, :].rearrange("p (q j) -> p q j", q=2)
            link(g.affine_select(out=v6, in_=v6, compare_op=ALU.is_ge, fill=0.0, base=0,
                                 pattern=[[-D, 2], [-2 * D, 3]], channel_multiplier=1))
            g.affine_select(out=v6, in_=v6, compare_op=ALU.is_ge, fill=0.0, base=D - 1,
                            pattern=[[D, 2], [2 * D, 3]], channel_multiplier=-1).then_inc(S["masks_ready"], 1)
            link(g.memset(mask12[:, :, :], 1.0))
            link(g.affine_select(out=mask12[:, :, :], in_=mask12[:, :, :], compare_op=ALU.is_ge, fill=0.0, base=0,
                                 pattern=[[0, 4], [-N, 3]], channel_multiplier=1))
            link(g.affine_select(out=mask12[:, :, :], in_=mask12[:, :, :], compare_op=ALU.is_ge, fill=0.0,
                                 base=N - 1, pattern=[[0, 4], [N, 3]], channel_multiplier=-1))

            for n, (k, into, rows) in enumerate(((2, 0, 128), (3, 1, 128), (4, 0, 128), (5, 1, 128), (7, 6, HALF))):
                pool.wait_ge(S["xs_a"], k + 1)
                if n in (2, 3):
                    pool.wait_ge(S["xs_sum"], n - 1)
                g.tensor_tensor(XS[0:rows, into, :], XS[0:rows, into, :], XS[0:rows, k, :], ALU.add)\
                 .then_inc(S["xs_sum"], 1)
            for b in range(NIMG):
                ins = g.tensor_copy(VB[:, b, :, D], mask12[:, :, :].rearrange("p g j -> p (g j)"))
            ins.then_inc(S["vones_ready"], 1)

            pool.wait_ge(S["vones_ready"], 1)
            g.memset(hnT[HALF:HALF + 1, :, :], 1.0).then_inc(S["ones_rows"], 1)
            g.memset(OT[HALF:HALF + 1, 1, :], 1.0).then_inc(S["ones_rows"], 1)

        @block.scalar
        def _(act):
            a = nc.scalar
            def evac_xt(k, hf):
                src = bank[2 * (k % 2) + hf][0:KCH[k], 0:3 * ROWS].rearrange("p (w h b) -> p w h b", w=3, h=GR)
                dst = XT[0:KCH[k], k, :].rearrange("p (b n) -> p n b", n=N)[:, 1:N, :]\
                    .rearrange("p (h w) b -> p w h b", w=GR)[:, 3 * hf:3 * hf + 3]
                return dst, src

            for c in range(CH):
                act.wait_ge(S[f"x{c}_in"], 16)
                dst, src = reorder(c, 1)
                for w in range(2):
                    ins = a.activation(dst[:, 3 * w:3 * w + 3], src[:, 3 * w:3 * w + 3], ACT.Copy)
                ins.then_inc(S["xr_a"], 1)
            act.wait_ge(S["xtb_in"], 16 * 2 * (CH + 1))
            a.activation(XTBR[:, :, :, :], XTB[:, :, :, :].rearrange("p s c (w q) -> p w (s c) q", w=GR), ACT.Copy)\
             .then_inc(S["xtb_ready"], 1)
            for k in range(NCHUNK):
                act.wait_ge(S["xt_mm"], 2 * k + 2)
                dst, src = evac_xt(k, 1)
                for w in range(3):
                    ins = a.activation(dst[:, w], src[:, w], ACT.Copy)
                ins.then_inc(S["xt_evac_a"], 1)
            act.wait_ge(S["w0_in"], 16)
            act.wait_ge(S["gp_own"], 1)
            for e in range(2):
                for c in range(CH):
                    a.activation(WE[:, 2 * c + e, 0:HID], WP[:, 0, e, c, :], ACT.Copy, scale=GP[:, 0, e, 0, c:c + 1])\
                     .then_inc(S["weff_a"], 1)
            act.wait_ge(S["xcls_zero"], 1)
            for k in range(NCHUNK):
                act.wait_ge(S["xt_evac_v"], k + 1)
                act.wait_ge(S["xt_evac_a"], k + 1)
                a.activation(XS[0:KCH[k], k, :], XT[0:KCH[k], k, :], ACT.Square).then_inc(S["xs_a"], 1)
            act.wait_ge(S["base_mm"], 1)
            a.activation(g1n[:, :], bank[7][:, 0:HID], ACT.Copy).then_inc(S["g1_sb"], 1)
            nl = TILES[-1][1]
            a.activation(BASE[0:nl, NT - 1, :], bank[7][0:nl, HID:2 * HID], ACT.Copy).then_inc(S["base_sb"], 1)
            for q in range(2):
                act.wait_ge(S["base_mm"], q + 2)
                a.activation(BASE[:, 2 * q:2 * q + 2, :],
                             bank[6 - q][:, 0:HID * 2].rearrange("p (i n) -> p i n", i=2), ACT.Copy)\
                 .then_inc(S["base_sb"], 1)

            def std_of(dst, src, scale, done):
                a.activation(dst, src, ACT.Sqrt, bias=eps[0:dst.shape[0], :], scale=scale).then_inc(done, 1)

            act.wait_ge(S["consts_ready"], 9)
            def mask_rows(buf, half, hd, th, done):
                a.activation(head_rows(half, hd, th), tokens(buf, half, th), ACT.Copy, scale=mask6[:, hd:hd + 1])\
                 .then_inc(done, 1)

            def from_transposed(dst, i, src):
                t0, n = TILES[i]
                return a.activation(dst[:, :, t0:t0 + n],
                                    src[0:HALF, 0:256].rearrange("p (k t) -> p k t", k=2)[:, :, 0:n], ACT.Copy)

            def rows_out(i):
                act.wait_ge(S["hnt_mm"], i + 1)
                from_transposed(hnT[0:HALF], i, bank[i % 2]).then_inc(S["hnt_sb"], 1)

            def queries_out(th):
                for half in range(2):
                    act.wait_ge(S["q_mm"], 2 * th + half + 1)
                    a.activation(qT[:, half, TH * th:TH * (th + 1)], bank[(5, 6, 3, 4)[2 * th + half]][0:HALF, 0:TH],
                                 ACT.Copy).then_inc(S["q_sb"], 1)

            for i in range(NT + 1):
                if i >= 1:
                    n = TILES[i - 1][1]
                    act.wait_ge(S["mv_ready"], i)
                    std_of(std1[0:n, i - 1:i], mv[0:n, i - 1, 1:2], 1.0, S["std1_ready"])
                if i == NT - 1:
                    act.wait_ge(S["wt_mm"], 1)
                    for kh in range(2):
                        a.activation(WQ[0:HALF, kh, 0:2, :],
                                     bank[6 + kh][0:HALF, 0:2 * HID].rearrange("p (k n) -> p k n", k=2), ACT.Copy)\
                         .then_inc(S["wt_a"], 1)
                    act.wait_ge(S["wt_mm"], 2)
                    for kh in range(2):
                        for half in range(2):
                            c0 = HALF * half
                            a.activation(WQ[0:HALF, kh, 2, c0:c0 + HALF].rearrange("p (q j d) -> p j q d", q=2, j=3),
                                         bank[5][0:HALF, HID * kh + c0:HID * kh + c0 + HALF]
                                         .rearrange("p (j q d) -> p j q d", q=2, j=3), ACT.Copy)\
                             .then_inc(S["wt_a"], 1)
                if i < NT:
                    n = TILES[i][1]
                    act.wait_ge(S["nvar_ready"], i + 1)
                    std_of(std[0:n, i:i + 1], nvar[0:n, i:i + 1], -1.0, S["std_ready"])
                if i == NT - 1:
                    for q in range(3):
                        rows_out(q)
            for i in range(3, NT):
                rows_out(i)
            queries_out(0)
            act.wait_ge(S["masks_ready"], 3)
            act.wait_ge(S["k_sb"], 2)
            for half, hd in MASKED[8:]:
                mask_rows(kT, half, hd, 0, S["k6_a"])
            queries_out(1)

            for i in range(STEPS):
                if 1 <= i <= NPAIR:
                    p = i - 1
                    act.wait_ge(S["pt_mm"], p + 1)
                    if p >= 2:
                        act.wait_ge(S["pv_mm"], p - 1)
                    a.activation(PT[:, p % 2], bank[2][0:G3, 0:4 * PP].rearrange("p (g t) -> p g t", g=4),
                                 ACT.Copy).then_inc(S["pt_sb"], 1)
                if i < NPAIR:
                    act.wait_ge(S["p_sub"], i + 1)
                    a.activation(Pr[:, i % 2], Pr[:, i % 2], ACT.Exp, scale=SCALE).then_inc(S["p_exp"], 1)
                if i < EARLY:
                    act.wait_ge(S["k_sb"], 4)
                    mask_rows(kT, *MASKED[8 + i], 1, S["k6_a"])
                    if i < 3:
                        a.activation(hn3[:, :, NIMG // 2:NIMG, i, :],
                                     hnT[:, :, TH:T].rearrange("p k (b n) -> p k b n", n=N), ACT.Copy)\
                         .then_inc(S["hn3_late"], 1)
                if 3 <= i < NPAIR + 3:
                    p = i - 3
                    act.wait_ge(S["ot_mm"], p + 1)
                    a.activation(OT[0:HALF, :, 2 * N * p:2 * N * (p + 1)].rearrange("p k (b n) -> p k b n", n=N),
                                 bank[4][0:HALF, 0:256].rearrange("p (k b n) -> p k b n", k=2, b=2)[:, :, :, 0:N],
                                 ACT.Copy).then_inc(S["ot_sb"], 1)
                if i == 4:
                    act.wait_ge(S["wt_mm"], 3)
                    a.activation(inb[:, :], bank[7][:, 2 * HID:2 * HID + NF], ACT.Copy).then_inc(S["wo_sb"], 1)
                    a.activation(WO[0:HALF, :, :], bank[7][0:HALF, 0:2 * HID].rearrange("p (k n) -> p k n", k=2),
                                 ACT.Copy).then_inc(S["wo_sb"], 1)
                for k, (t0, n) in enumerate(TILES):
                    if i == Y_STEP[k]:
                        act.wait_ge(S["y_mm"], k + 1)
                        a.activation(Y[0:n, k], bank[6 + k % 2][0:n, 0:HID], ACT.Copy).then_inc(S["ysb_ready"], 1)
                        if k >= 2:
                            act.wait_ge(S["ss_ready"], k - 1)
                        a.activation(ysq[0:n, k % 2], bank[6 + k % 2][0:n, 0:HID], ACT.Square)\
                         .then_inc(S["ysq_ready"], 1)
                for k, (t0, n) in enumerate(TILES):
                    if i == ROOT_STEP[k]:
                        act.wait_ge(S["ss_ready"], k + 1)
                        a.activation(nrm[0:n, k], ss[0:n, k], ACT.Sqrt).then_inc(S["nrm_ready"], 1)
                for k in range(NT):
                    if i == T_STEP[k]:
                        act.wait_ge(S["yt_mm"], k + 1)
                        from_transposed(YT, k, bank[(5, 2)[k % 2]]).then_inc(S["yt_sb"], 1)

            act.wait_ge(S["yt_sb"], 3)
            for half, hd in MASKED[8:]:
                mask_rows(YT, half, hd, 0, S["t6_a"])
            WIf = WI[:, :, :].rearrange("p k f -> p (k f)")
            for i in range(STEPS):
                if i < NPAIR:
                    act.wait_ge(S["s2_mm"], i + 1)
                    if i >= 2:
                        act.wait_ge(S["e2_ready"], i - 1)
                    a.activation(E1[:, i % 2], bank[i % 2][0:G3, 0:8 * N].rearrange("p (g t) -> p g t", g=4),
                                 ACT.Exp, bias=m10[0:G3, :], scale=SIM_SCALE).then_inc(S["e1_ready"], 1)
                if i < 3:
                    act.wait_ge(S["wt_mm"], 4 + i)
                    a.activation(WIf[:, 512 * i:512 * (i + 1)], bank[(4, 6, 7)[i]][0:HALF, :], ACT.Copy)\
                     .then_inc(S["wi_sb"], 1)
                if 3 <= i < NPAIR + 3:
                    p = i - 3
                    act.wait_ge(S["ot2_mm"], p + 1)
                    a.activation(OT[0:HALF, :, 2 * N * p:2 * N * (p + 1)].rearrange("p k (b n) -> p k b n", n=N),
                                 bank[4][0:HALF, 0:256].rearrange("p (k b n) -> p k b n", k=2, b=2)[:, :, :, 0:N],
                                 ACT.Copy).then_inc(S["ot2_sb"], 1)
                for k, (t0, n) in enumerate(TILES):
                    if i == ROOT_STEP[k]:
                        act.wait_ge(S["h2_mv"], k + 1)
                        std_of(std2[0:n, k:k + 1], mv2[0:n, k, 1:2], 1.0, S["std2_ready"])
                for k in range(NT):
                    if i == T_STEP[k]:
                        act.wait_ge(S["hn2t_mm"], k + 1)
                        from_transposed(hn2T, k, bank[(5, 2)[k % 2]]).then_inc(S["hn2t_sb"], 1)

            for th in range(2):
                for f in range(NF):
                    q = NF * th + f
                    act.wait_ge(S["up_mm"], q + 1)
                    a.activation(hT[:, f, TH * th:TH * (th + 1)], bank[UP_BANKS[q % 3]][:, 0:TH], ACT.Gelu,
                                 bias=inb[:, f:f + 1]).then_inc(S["gelu_done"], 1)

        @block.vector
        def _(dve):
            v = nc.vector
            steps = [0]

            def link(ins):
                steps[0] += 1
                ins.then_inc(S["dve_step"], 1)
                dve.wait_ge(S["dve_step"], steps[0])

            v.memset(WPf[96:128, 1, 0], 0.0).then_inc(S["wzero"], 1)
            v.memset(WPf[0:32, 2, 1], 0.0).then_inc(S["wzero"], 1)
            v.memset(WPf[96:128, 3], 0.0).then_inc(S["wzero"], 1)
            v.memset(WPf[0:32, 4], 0.0).then_inc(S["wzero"], 1)
            dve.wait_ge(S["gb_in"], 32)
            v.tensor_copy(GP[:, :, :, :, :], GN[:, :, :, :, :]).then_inc(S["gp_own"], 1)
            for c in range(CH):
                dve.wait_ge(S[f"x{c}_in"], 16)
                dst, src = reorder(c, 0)
                v.tensor_copy(dst, src).then_inc(S["xr_v"], 1)
            dve.wait_ge(S["gp_own"], 1)
            dve.wait_ge(S["placed_mm"], 2)
            pl = bank[4]
            link(v.tensor_copy(GP[:, :, 0, 1, :], pl[:, 0:6].rearrange("p (k c) -> p k c", k=2)))
            link(v.tensor_copy(GP[:, :, 1, 2, :], pl[:, 8:14].rearrange("p (k c) -> p k c", k=2)))
            for q in range(2):
                ins = v.tensor_copy(GP[:, :, :, 3 + q, :],
                                    pl[:, 16 + 12 * q:28 + 12 * q].rearrange("p (k e c) -> p k e c", k=2, e=2))
            ins.then_inc(S["placed"], 1)
            for e in range(2):
                v.tensor_copy(WE[:, e:2 * CH:2, HID], pl[:, 48 + e:49 + e].to_broadcast([128, CH]))
            v.memset(WE[0:HALF, 2 * CH:NCHUNK, HID:HID + 1], 1.0 / FEAT).then_inc(S["cnt_done"], 1)

            for k in range(NCHUNK):
                dve.wait_ge(S["xt_mm"], 2 * k + 1)
                src = bank[2 * (k % 2)][0:KCH[k], 0:3 * ROWS].rearrange("p (w h b) -> p w h b", w=3, h=GR)
                dst = XT[0:KCH[k], k, :].rearrange("p (b n) -> p n b", n=N)[:, 1:N, :]\
                    .rearrange("p (h w) b -> p w h b", w=GR)[:, 0:3]
                for w in range(3):
                    ins = v.tensor_copy(dst[:, w], src[:, w])
                ins.then_inc(S["xt_evac_v"], 1)

            dve.wait_ge(S["placed"], 1)
            order = [((0, 0), (0, 1)), ((1, 1), (1, 0)), ((2, 1), (2, 0)), ((3, 0), (3, 1)), ((4, 0), (4, 1))]
            arrive = [16, 48, 48, 16, 16]
            for q, pair in enumerate(order):
                if q == 0:
                    continue
                dve.wait_ge(S[f"w{q}_in"], arrive[q])
                for e2, (s, e) in enumerate(pair):
                    for c in range(CH):
                        dst = WE[:, 2 * c + e2, 0:HID]
                        gcol = GP[:, 0, e, s, c:c + 1]
                        n = CH * e2 + c + 1
                        if q == 1:
                            dve.wait_ge(S["weff_a"], n)
                        else:
                            dve.wait_ge(S["weff"], 6 * (q - 2) + n)
                        v.scalar_tensor_tensor(out=dst, in0=WP[:, s, e, c, :], scalar=gcol, in1=dst,
                                               op0=ALU.mult, op1=ALU.add).then_inc(S["weff"], 1)
            dve.wait_ge(S["wh_in"], 16 * 4)
            dve.wait_ge(S["gh_in"], 16 * 8)
            for k in range(2):
                v.tensor_scalar(WE[0:HALF, 2 * CH + k, 0:HID], WH[:, k, :], GH[:, k, 0:1], None, ALU.mult)\
                 .then_inc(S["weff"], 1)

            dve.wait_ge(S["sums_mm"], 1)
            v.tensor_copy(R[0:2, :], bank[5][0:2, 0:HID]).then_inc(S["sums_sb"], 1)

            for i in range(NT + 2):
                if i >= 2:
                    k = i - 2
                    n = TILES[k][1]
                    dve.wait_ge(S["std1_ready"], k + 1)
                    link(v.reciprocal(rstd1[0:n, k:k + 1], std1[0:n, k:k + 1]))
                    v.tensor_scalar(hn[0:n, k], h1[0:n, k], mv[0:n, k, 0:1], rstd1[0:n, k:k + 1],
                                    ALU.subtract, ALU.mult).then_inc(S["hn_ready"], 1)
                if 1 <= i <= NT:
                    k = i - 1
                    n = TILES[k][1]
                    if k == 0:
                        dve.wait_ge(S["g1_sb"], 1)
                        dve.wait_ge(S["base_sb"], 3)
                    link(v.scalar_tensor_tensor(out=u[0:n, k % 2], in0=g1n[0:n, :], scalar=st[0:n, k, 0:1],
                                                in1=bank[k][0:n, 0:HID], op0=ALU.mult, op1=ALU.add))
                    dve.wait_ge(S["std_ready"], k + 1)
                    link(v.reciprocal(rstd[0:n, k:k + 1], std[0:n, k:k + 1]))
                    v.scalar_tensor_tensor(out=h1[0:n, k], in0=u[0:n, k % 2], scalar=rstd[0:n, k:k + 1],
                                           in1=BASE[0:n, k], op0=ALU.mult, op1=ALU.add).then_inc(S["h1_ready"], 1)
                    dve.wait_ge(S["h1_ready"], k + 1)
                    link(v.bn_stats(bn[0:n, k], h1[0:n, k]))
                    v.bn_aggr(mv[0:n, k], bn[0:n, k]).then_inc(S["mv_ready"], 1)
                if i < NT:
                    n = TILES[i][1]
                    dve.wait_ge(S["sq_mm"], 3 * NT)
                    if i >= 2:
                        dve.wait_ge(S["emb_mm"], i - 1)
                    link(v.tensor_copy(st[0:n, i, :], bank[i][0:n, HID:HID + 2]))
                    link(v.scalar_tensor_tensor(out=nvar[0:n, i:i + 1], in0=st[0:n, i, 0:1], scalar=st[0:n, i, 0:1],
                                                in1=st[0:n, i, 1:2], op0=ALU.mult, op1=ALU.subtract))
                    v.tensor_scalar(nvar[0:n, i:i + 1], nvar[0:n, i:i + 1], 0.0, None, ALU.min)\
                     .then_inc(S["nvar_ready"], 1)

            def mask_rows(buf, half, hd, th, done):
                v.tensor_scalar(head_rows(half, hd, th), tokens(buf, half, th), mask6[:, hd:hd + 1], None, ALU.mult)\
                 .then_inc(done, 1)

            for th in range(2):
                for half in range(2):
                    dve.wait_ge(S["k_mm"], 2 * th + half + 1)
                    v.tensor_copy(kT[:, half, TH * th:TH * (th + 1)], bank[(7, 2, 6, 7)[2 * th + half]][0:HALF, 0:TH])\
                     .then_inc(S["k_sb"], 1)
                if th == 0:
                    dve.wait_ge(S["masks_ready"], 3)
                    dve.wait_ge(S["k_sb"], 2)
                    for half, hd in MASKED[:8]:
                        mask_rows(kT, half, hd, 0, S["k6_v"])
            dve.wait_ge(S["hnt_sb"], NT)
            dve.wait_ge(S["ones_rows"], 2)
            for j in range(3):
                v.tensor_copy(hn3[:, :, 0:NIMG // 2, j, :], hnT[:, :, 0:TH].rearrange("p k (b n) -> p k b n", n=N))\
                 .then_inc(S["hn3_early"], 1)

            def normalise(p, src, done):
                o = src[0:PP, 0:NH * VW].rearrange("p (h d) -> p h d", d=VW)
                link(v.reciprocal(ro[:, p % 2], o[:, :, D]))
                v.tensor_tensor(On[:, p % 2].rearrange("p (h d) -> p h d", d=D), o[:, :, 0:D],
                                ro[:, p % 2].unsqueeze(2).to_broadcast([PP, NH, D]), ALU.mult).then_inc(done, 1)

            for i in range(STEPS):
                if i < NPAIR:
                    dve.wait_ge(S["s_mm"], i + 1)
                    s3 = bank[i % 2][0:PP, 0:NH * N].rearrange("p (h m) -> p h m", m=N)
                    link(v.tensor_reduce(mx[:, i % 2], s3, AX.X, ALU.max))
                    if i >= 2:
                        dve.wait_ge(S["pt_mm"], i - 1)
                    v.tensor_tensor(Pr[:, i % 2], s3, mx[:, i % 2].unsqueeze(2).to_broadcast([PP, NH, N]),
                                    ALU.subtract).then_inc(S["p_sub"], 1)
                    dve.wait_ge(S["vones_ready"], 1)
                    dve.wait_ge(S["v_mm"], i + 1)
                    for bb in range(2):
                        ins = v.tensor_tensor(
                            VB[:, 2 * i + bb, :, 0:D],
                            bank[5][0:G3, HID * bb:HID * (bb + 1)].rearrange("p (h d) -> p h d", d=D),
                            mask12[:, :, :].rearrange("p g j -> p (g j)").unsqueeze(2).to_broadcast([G3, 12, D]),
                            ALU.mult)
                    ins.then_inc(S["v_sb"], 1)
                if i < EARLY:
                    dve.wait_ge(S["k_sb"], 4)
                    for half, hd in MASKED[2 * i:2 * i + 2]:
                        mask_rows(kT, half, hd, 1, S["k6_v"])
                if 2 <= i < NPAIR + 2:
                    p = i - 2
                    dve.wait_ge(S["pv_mm"], p + 1)
                    if p >= 2:
                        dve.wait_ge(S["ot_mm"], p - 1)
                    normalise(p, bank[3], S["on_ready"])
                for k, (t0, n) in enumerate(TILES):
                    if i == T_STEP[k]:
                        dve.wait_ge(S["nrm_ready"], k + 1)
                        link(v.tensor_scalar(nrm[0:n, k], nrm[0:n, k], NORM_EPS, None, ALU.max))
                        link(v.reciprocal(rn[0:n, k], nrm[0:n, k]))
                        dve.wait_ge(S["ysb_ready"], k + 1)
                        v.tensor_tensor(Y[0:n, k].rearrange("p (h d) -> p h d", d=D),
                                        Y[0:n, k].rearrange("p (h d) -> p h d", d=D),
                                        rn[0:n, k].unsqueeze(2).to_broadcast([n, NH, D]), ALU.mult)\
                         .then_inc(S["y_ready"], 1)
                for k, (t0, n) in enumerate(TILES):
                    if i == Y_STEP[k]:
                        dve.wait_ge(S["ysq_ready"], k + 1)
                        v.tensor_reduce(ss[0:n, k], ysq[0:n, k % 2].rearrange("p (h d) -> p h d", d=D), AX.X, ALU.add)\
                         .then_inc(S["ss_ready"], 1)

            dve.wait_ge(S["s_mm"], EARLY)
            dve.wait_ge(S["yt_sb"], 3)
            for half, hd in MASKED[:8]:
                mask_rows(YT, half, hd, 0, S["t6_v"])

            for i in range(STEPS):
                if i < NPAIR:
                    dve.wait_ge(S["e1_ready"], i + 1)
                    if i >= 2:
                        dve.wait_ge(S["pv2_mm"], i - 1)
                    v.scalar_tensor_tensor(out=E2[:, i % 2].rearrange("p g t -> p (g t)"),
                                           in0=bank[i % 2][0:G3, 0:8 * N], scalar=0.0,
                                           in1=E1[:, i % 2].rearrange("p g t -> p (g t)"),
                                           op0=ALU.is_ge, op1=ALU.mult).then_inc(S["e2_ready"], 1)
                if i < EARLY:
                    dve.wait_ge(S["s_mm"], NPAIR)
                    dve.wait_ge(S["yt_sb"], NT)
                    for half, hd in MASKED[3 * i:3 * i + 3]:
                        mask_rows(YT, half, hd, 1, S["t6_v"])
                if 2 <= i < NPAIR + 2:
                    p = i - 2
                    dve.wait_ge(S["pv2_mm"], p + 1)
                    if p >= 2:
                        dve.wait_ge(S["ot2_mm"], p - 1)
                    normalise(p, bank[3], S["on2_ready"])
                for k, (t0, n) in enumerate(TILES):
                    if i == T_STEP[k]:
                        dve.wait_ge(S["std2_ready"], k + 1)
                        link(v.reciprocal(rstd2[0:n, k:k + 1], std2[0:n, k:k + 1]))
                        v.tensor_scalar(hn2[0:n, k], h2[0:n, k], mv2[0:n, k, 0:1], rstd2[0:n, k:k + 1],
                                        ALU.subtract, ALU.mult).then_inc(S["hn2_ready"], 1)
                for k, (t0, n) in enumerate(TILES):
                    if i == Y_STEP[k]:
                        dve.wait_ge(S["y2_mm"], k + 1)
                        link(v.tensor_tensor(h2[0:n, k], bank[6 + k % 2][0:n, 0:HID], h1[0:n, k], ALU.add))
                        link(v.bn_stats(bn2[0:n, k], h2[0:n, k]))
                        v.bn_aggr(mv2[0:n, k], bn2[0:n, k]).then_inc(S["h2_mv"], 1)
            for i, (t0, n) in enumerate(TILES):
                dve.wait_ge(S["down_mm"], i + 1)
                v.tensor_tensor(res[0:n, i], bank[DOWN_BANKS[i]][0:n, 0:HID], h2[0:n, i], ALU.add).then_inc(S["res_ready"], 1)

        @block.tensor
        def _(pe):
            t = nc.tensor
            pe.wait_ge(S["gb_in"], 32)
            pe.wait_ge(S["consts_ready"], 7)
            pl = bank[4]
            t.matmul(pl[:, 0:6], sh[0][:, :], GN[:, :, 0, 1, :], start=True, stop=True)
            t.matmul(pl[:, 8:14], sh[1][:, :], GN[:, :, 1, 2, :], start=True, stop=True)
            for q in range(2):
                ins = t.matmul(pl[:, 16 + 12 * q:28 + 12 * q], sh[2 + q][:, :], GN[:, :, :, 3 + q, :], start=True, stop=True)
            ins.then_inc(S["placed_mm"], 1)
            t.matmul(pl[:, 48:50], ident[:, :], inv_n[:, 2:4], start=True, stop=False)
            for q in range(2):
                t.matmul(pl[:, 48:50], sh[2 + q][:, :], inv_n[:, 0:2], start=False, stop=False)
            t.matmul(pl[:, 48:49], sh[1][:, :], inv_n[:, 0:1], start=False, stop=False)
            t.matmul(pl[:, 49:50], sh[0][:, :], inv_n[:, 0:1], start=False, stop=True).then_inc(S["placed_mm"], 1)

            for k in range(NCHUNK):
                if k < 2 * CH:
                    pe.wait_ge(S["xr_a" if k % 2 else "xr_v"], k // 2 + 1)
                elif k == 2 * CH:
                    pe.wait_ge(S["xlr_ready"], 4 * CH)
                else:
                    pe.wait_ge(S["xtb_ready"], 1)
                if k >= 2:
                    pe.wait_ge(S["xt_evac_v"], k - 1)
                    pe.wait_ge(S["xt_evac_a"], k - 1)
                for wx in range(GR):
                    if k < 2 * CH:
                        src = XR[:, k, wx]
                    elif k == 2 * CH:
                        src = XLR[:, wx].rearrange("p s c r -> p (s c r)")
                    else:
                        src = XTBR[:, wx].rearrange("p s q -> p (s q)")
                    dst = bank[2 * (k % 2) + wx // 3][0:KCH[k], ROWS * (wx % 3):ROWS * (wx % 3 + 1)]
                    ins = t.transpose(dst, src, ident[0:ROWS, 0:ROWS])
                    if wx % 3 == 2:
                        ins.then_inc(S["xt_mm"], 1)

            pe.wait_ge(S["placed"], 1)
            arrive = [16, 48, 48, 16, 16]
            for s in range(NSH):
                pe.wait_ge(S[f"w{s}_in"], arrive[s])
                for e in range(2):
                    for c in range(CH):
                        t.matmul(bank[5][0:2, 0:HID], GP[:, :, e, s, c], WP[:, s, e, c, :],
                                 start=(s, e, c) == (0, 0, 0), stop=False)
            pe.wait_ge(S["wh_in"], 16 * 4)
            pe.wait_ge(S["gh_in"], 16 * 8)
            for k in range(2):
                ins = t.matmul(bank[5][0:2, 0:HID], GH[:, k, :], WH[:, k, :], start=False, stop=k == 1)
            ins.then_inc(S["sums_mm"], 1)

            def emb(i, ks):
                t0, n = TILES[i]
                for k in ks:
                    ins = t.matmul(bank[i][0:n, 0:HID + 1], XT[0:KCH[k], k, t0:t0 + n], WE[0:KCH[k], k, :],
                                   start=k == 0, stop=k == NCHUNK - 1)
                return ins

            for n, k in enumerate((0, 2, 4, 1, 3, 5)):
                pe.wait_ge(S["weff"], 6 * (NSH - 2) + n + 1)
                for i in range(2):
                    emb(i, [k])
            pe.wait_ge(S["weff"], 6 * (NSH - 1) + 2)
            for i in range(2):
                emb(i, (6, 7))
            pe.wait_ge(S["sums_sb"], 1)
            pe.wait_ge(S["rows_in"], 32)
            pe.wait_ge(S["masks_ready"], 2)
            t.matmul(bank[7][:, 0:HID], neg0[:, :], R[:, :], start=True, stop=True)

            def base(i, dst, c0):
                t0, n = TILES[i]
                return t.matmul(dst[0:n, c0:c0 + HID], IND[:, :, :].rearrange("p b n -> p (b n)")[:, t0:t0 + n], R[:, :],
                                start=True, stop=True)

            base(NT - 1, bank[7], HID).then_inc(S["base_mm"], 1)
            for q in range(2):
                for i in range(2):
                    ins = base(2 * q + i, bank[6 - q], HID * i)
                ins.then_inc(S["base_mm"], 1)
            pe.wait_ge(S["xs_sum"], 5)
            pe.wait_ge(S["xs_a"], NCHUNK)
            pe.wait_ge(S["cnt_done"], 1)
            for i, (t0, n) in enumerate(TILES):
                for k in (0, 1, 6):
                    t.matmul(bank[i][0:n, HID + 1:HID + 2], XS[0:KCH[k], k, t0:t0 + n], WE[0:KCH[k], k, HID:HID + 1],
                             start=k == 0, stop=k == 6).then_inc(S["sq_mm"], 1)

            for i in range(2, NT):
                if i == NT - 1:
                    pe.wait_ge(S["qkv_in"], 16)
                    pe.wait_ge(S["base_sb"], 3)
                    for kh in range(2):
                        for o in range(4):
                            ins = t.transpose(bank[6 + kh][0:HALF, HALF * o:HALF * (o + 1)],
                                              qkvw[:, o, HALF * kh:HALF * (kh + 1)], ident[0:HALF, 0:HALF])
                    ins.then_inc(S["wt_mm"], 1)
                    for kh in range(2):
                        for o in range(2):
                            ins = t.transpose(bank[5][0:HALF, HID * kh + HALF * o:HID * kh + HALF * (o + 1)],
                                              qkvw[:, 4 + o, HALF * kh:HALF * (kh + 1)], ident[0:HALF, 0:HALF])
                    ins.then_inc(S["wt_mm"], 1)
                emb(i, (0, 2, 4, 1, 3, 5, 6, 7)).then_inc(S["emb_mm"], 1)

            def to_features(src, i, dst):
                n = TILES[i][1]
                for kh in range(2):
                    ins = t.transpose(dst[0:HALF, 128 * kh:128 * kh + n], src[0:n, i, HALF * kh:HALF * (kh + 1)],
                                      ident[0:n, 0:n])
                return ins

            def queries_keys(th):
                for qk, done in ((1, S["k_mm"]), (0, S["q_mm"])):
                    for half in range(2):
                        dst = bank[((5, 6, 3, 4), (7, 2, 6, 7))[qk][2 * th + half]][0:HALF, 0:TH]
                        for kh in range(2):
                            K = HALF + kh
                            ins = t.matmul(dst, WQ[0:K, kh, qk, HALF * half:HALF * (half + 1)],
                                           hnT[0:K, kh, TH * th:TH * (th + 1)], start=kh == 0, stop=kh == 1)
                        ins.then_inc(done, 1)

            def to_feature_rows(i):
                pe.wait_ge(S["hn_ready"], i + 1)
                if i >= 2:
                    pe.wait_ge(S["hnt_sb"], i - 1)
                to_features(hn, i, bank[i % 2]).then_inc(S["hnt_mm"], 1)

            for i in range(3):
                to_feature_rows(i)
            pe.wait_ge(S["ones_rows"], 2)
            pe.wait_ge(S["bias_in"], 16 * 7)
            pe.wait_ge(S["wt_a"], 6)
            pe.wait_ge(S["hnt_sb"], 3)
            queries_keys(0)
            for i in range(3, NT):
                to_feature_rows(i)
            pe.wait_ge(S["hnt_sb"], NT)
            pe.wait_ge(S["k_sb"], 1)
            pe.wait_ge(S["q_sb"], 2)
            queries_keys(1)

            def value_rows(p):
                pe.wait_ge(*((S["hn3_early"], 3) if p < EARLY else (S["hn3_late"], 3)))
                if p >= 1:
                    pe.wait_ge(S["v_sb"], p)
                for bb in range(2):
                    b = 2 * p + bb
                    for kh in range(2):
                        K = HALF + kh
                        ins = t.matmul(bank[5][0:G3, HID * bb:HID * (bb + 1)],
                                       hn3[0:K, kh, b].rearrange("p j n -> p (j n)"),
                                       WQ[0:K, kh, 2, :], start=kh == 0, stop=kh == 1)
                return ins

            def rows_of(bb):
                return 64 if bb == 0 else N

            def scores(p):
                for half in range(2):
                    for bb in range(2):
                        b, M = 2 * p + bb, rows_of(bb)
                        ins = t.matmul(bank[p % 2][64 * bb:64 * bb + M, 6 * N * half:6 * N * (half + 1)],
                                       qT[:, half, N * b:N * b + M],
                                       K6[:, half, :, b].rearrange("p q j n -> p q (j n)"),
                                       start=True, stop=True)
                return ins

            def values(p, weights, dst):
                for g in range(4):
                    for bb in range(2):
                        o = dst[64 * bb:64 * bb + rows_of(bb), 0:NH * VW].rearrange(
                            "p (h j q d) -> p h q j d", h=2, j=3, q=2)[:, g // 2, g % 2]
                        ins = t.matmul(o, weights(g, bb),
                                       VB[:, 2 * p + bb, 3 * g:3 * g + 3, :].rearrange("p j d -> p (j d)"),
                                       start=True, stop=True)
                return ins

            def out_features(p, dst):
                for kh in range(2):
                    ins = t.transpose(dst[0:HALF, 128 * kh:128 * kh + PP], On[:, p % 2, HALF * kh:HALF * (kh + 1)],
                                      ident[0:PP, 0:PP])
                return ins

            def project(i):
                t0, n = TILES[i]
                for kh in range(2):
                    K = HALF + kh
                    ins = t.matmul(bank[6 + i % 2][0:n, 0:HID], OT[0:K, kh, t0:t0 + n], WO[0:K, kh, :],
                                   start=kh == 0, stop=kh == 1)
                return ins

            pe.wait_ge(S["k6_v"], 8)
            pe.wait_ge(S["k6_a"], 4)
            pe.wait_ge(S["q_sb"], 4)
            for i in range(STEPS):
                if i < NPAIR:
                    if i >= 2:
                        pe.wait_ge(S["p_sub"], i - 1)
                    if i == EARLY:
                        pe.wait_ge(S["k6_v"], 16)
                        pe.wait_ge(S["k6_a"], 8)
                    scores(i).then_inc(S["s_mm"], 1)
                    value_rows(i).then_inc(S["v_mm"], 1)
                if i == 3:
                    pe.wait_ge(S["proj_in"], 16)
                    pe.wait_ge(S["k_sb"], 4)
                    for kh in range(2):
                        for o in range(2):
                            src = projw[:, o, HALF * kh:HALF * (kh + 1)]
                            t.transpose(bank[7][0:HALF, HID * kh + HALF * o:HID * kh + HALF * (o + 1)], src,
                                        ident[0:HALF, 0:HALF])
                    t.transpose(bank[7][:, 2 * HID:2 * HID + NF], inbr[:, :], ident[0:NF, 0:NF])\
                        .then_inc(S["wt_mm"], 1)
                if 1 <= i <= NPAIR:
                    p = i - 1
                    pe.wait_ge(S["p_exp"], p + 1)
                    if p >= 1:
                        pe.wait_ge(S["pt_sb"], p)
                    else:
                        pe.wait_ge(S["k_sb"], 2)
                    for g in range(4):
                        ins = t.transpose(bank[2][0:G3, PP * g:PP * (g + 1)],
                                          Pr[:, p % 2, 3 * g:3 * g + 3, :].rearrange("p h m -> p (h m)"),
                                          ident[0:PP, 0:PP])
                    ins.then_inc(S["pt_mm"], 1)
                if 2 <= i <= NPAIR + 1:
                    p = i - 2
                    pe.wait_ge(S["pt_sb"], p + 1)
                    pe.wait_ge(S["v_sb"], p + 1)
                    if p >= 1:
                        pe.wait_ge(S["on_ready"], p)
                    values(p, lambda g, bb: PT[:, p % 2, g, 64 * bb:64 * bb + rows_of(bb)], bank[3])\
                        .then_inc(S["pv_mm"], 1)
                if 3 <= i < NPAIR + 3:
                    p = i - 3
                    pe.wait_ge(S["on_ready"], p + 1)
                    if p >= 1:
                        pe.wait_ge(S["ot_sb"], p)
                    out_features(p, bank[4]).then_inc(S["ot_mm"], 1)
                for k in range(NT):
                    if i == Y_STEP[k]:
                        pe.wait_ge(S["wo_sb"], 2)
                        pe.wait_ge(S["ot_sb"], LAST_PAIR[k] + 1)
                        if k >= 2:
                            pe.wait_ge(S["ysq_ready"], k - 1)
                        project(k).then_inc(S["y_mm"], 1)
                for k in range(NT):
                    if i == T_STEP[k]:
                        pe.wait_ge(S["y_ready"], k + 1)
                        if k >= 2:
                            pe.wait_ge(S["yt_sb"], k - 1)
                        else:
                            pe.wait_ge(S["v_sb"], NPAIR)
                            pe.wait_ge(S["pt_sb"], NPAIR)
                        to_features(Y, k, bank[(5, 2)[k % 2]]).then_inc(S["yt_mm"], 1)

            pe.wait_ge(S["ffnw_in"], 32)
            pe.wait_ge(S["ysq_ready"], NT)
            pe.wait_ge(S["ot_sb"], NPAIR)
            for q in range(2 * NF):
                kh, f = divmod(q, NF)
                ins = t.transpose(bank[(4, 6, 7)[q // 4]][0:HALF, 128 * (q % 4):128 * (q % 4 + 1)],
                                  inw[:, f, HALF * kh:HALF * (kh + 1)], ident[:, :])
                if q % 4 == 3:
                    ins.then_inc(S["wt_mm"], 1)

            pe.wait_ge(S["t6_v"], 8)
            pe.wait_ge(S["t6_a"], 4)
            for i in range(STEPS):
                if i < NPAIR:
                    if i >= 2:
                        pe.wait_ge(S["e2_ready"], i - 1)
                    if i == EARLY:
                        pe.wait_ge(S["t6_v"], 20)
                    for g in range(4):
                        half, par = divmod(g, 2)
                        for bb in range(2):
                            cols = slice(N * (2 * i + bb), N * (2 * i + bb + 1))
                            ins = t.matmul(bank[i % 2][0:G3, N * (2 * g + bb):N * (2 * g + bb + 1)],
                                           K6[:, half, par, 2 * i + bb].rearrange("p j n -> p (j n)"), YT[:, half, cols],
                                           start=True, stop=True)
                    ins.then_inc(S["s2_mm"], 1)
                if 2 <= i <= NPAIR + 1:
                    p = i - 2
                    pe.wait_ge(S["e2_ready"], p + 1)
                    if p >= 1:
                        pe.wait_ge(S["on2_ready"], p)
                    values(p, lambda g, bb: E2[:, p % 2, g, N * bb:N * bb + rows_of(bb)], bank[3])\
                        .then_inc(S["pv2_mm"], 1)
                if 3 <= i < NPAIR + 3:
                    p = i - 3
                    pe.wait_ge(S["on2_ready"], p + 1)
                    if p >= 1:
                        pe.wait_ge(S["ot2_sb"], p)
                    else:
                        pe.wait_ge(S["wi_sb"], 1)
                    out_features(p, bank[4]).then_inc(S["ot2_mm"], 1)
                for k in range(NT):
                    if i == Y_STEP[k]:
                        pe.wait_ge(S["ot2_sb"], LAST_PAIR[k] + 1)
                        if k >= 2:
                            pe.wait_ge(S["h2_mv"], k - 1)
                        else:
                            pe.wait_ge(S["wi_sb"], 3)
                        project(k).then_inc(S["y2_mm"], 1)
                for k in range(NT):
                    if i == T_STEP[k]:
                        pe.wait_ge(S["hn2_ready"], k + 1)
                        if k >= 2:
                            pe.wait_ge(S["hn2t_sb"], k - 1)
                        to_features(hn2, k, bank[(5, 2)[k % 2]]).then_inc(S["hn2t_mm"], 1)

            for th in range(2):
                pe.wait_ge(S["hn2t_sb"], 3 if th == 0 else NT)
                for f in range(NF):
                    q = NF * th + f
                    if q >= 3:
                        pe.wait_ge(S["gelu_done"], q - 2)
                    for kh in range(2):
                        ins = t.matmul(bank[UP_BANKS[q % 3]][:, 0:TH], WI[:, kh, 128 * f:128 * (f + 1)],
                                       hn2T[:, kh, TH * th:TH * (th + 1)], start=kh == 0, stop=kh == 1)
                    ins.then_inc(S["up_mm"], 1)
            for i, (t0, n) in enumerate(TILES):
                pe.wait_ge(S["gelu_done"], NF if t0 + n <= TH else 2 * NF)
                for f in range(NF):
                    ins = t.matmul(bank[DOWN_BANKS[i]][0:n, 0:HID], hT[:, f, t0:t0 + n], w2[:, f, :],
                                   start=f == 0, stop=f == NF - 1)
                ins.then_inc(S["down_mm"], 1)


_INS = ["x", "cls_tok", "L0_tok_ln_gamma", "L0_tok_ln_beta", "L0_tok_W", "L0_tok_b", "L0_attn_qkv_w",
        "L0_attn_qkv_b", "L0_attn_proj_w", "L0_attn_proj_b", "L0_ffn_in_weight", "L0_ffn_in_bias",
        "L0_ffn_out_weight"]


def kernel(**inputs):
    import numpy as _np
    import concourse.bacc as _bacc
    from concourse import mybir as _mybir
    from concourse.bass_utils import run_bass_kernel_spmd as _run

    nc = _bacc.Bacc("TRN2", target_bir_lowering=False, num_devices=1)
    arrays, args = {}, []
    for name in _INS:
        a = _np.ascontiguousarray(inputs[name])
        arrays[f"in_{name}"] = a
        args.append(nc.dram_tensor(f"in_{name}", a.shape, _mybir.dt.from_np(a.dtype), kind="ExternalInput").ap())
    args.append(nc.dram_tensor("out_0", (NIMG, N, HID), F32, kind="ExternalOutput").ap())
    vit(nc, *args)
    r = _run(nc, [arrays], core_ids=[0])
    return r.results[0]["out_0"]
```

```python
from contextlib import ExitStack

import concourse.bass as bass
from concourse import mybir

F32 = mybir.dt.float32
ALU = mybir.AluOpType
ACT = mybir.ActivationFunctionType
AX = mybir.AxisListType

NIMG, CH, IMG, PS = 16, 3, 96, 16
GR = IMG // PS
ROWS = NIMG * GR
N = GR * GR + 1
T = NIMG * N
HID, HALF = 192, 96
NH, D = 12, 16
NSH = 5
FEAT = PS * PS * CH * NSH
NCHUNK = 2 * CH + 2
FFN = 768
NF = FFN // 128
NT = -(-T // 128)
TILES = [(128 * i, min(128, T - 128 * i)) for i in range(NT)]
NPAIR = NIMG // 2
PP = 64 + N
G3 = 3 * N
VW = D + 1
TH = T // 2
EPS = 1e-5
NORM_EPS = 1e-12
SCALE = float(D) ** -0.5
SIM_SCALE = 10.0
LAST_PAIR = [(t0 + n - 1) // (2 * N) for t0, n in TILES]
Y_STEP = [min(p + 4, NPAIR + 2) for p in LAST_PAIR]
ROOT_STEP = [max(y, NPAIR) for y in Y_STEP]
ROOT2_STEP = ROOT_STEP[:2] + [NPAIR + 2] + ROOT_STEP[3:]
T_STEP = [max(r + 1, NPAIR + 2) for r in ROOT_STEP]
STEPS = T_STEP[-1] + 1
OUT_BANKS = [(3, 2)] * (NPAIR - 1) + [(1, 0)]
HN2T_BANKS = (5, 1, 2, 5, 1)
UP_BANKS, DOWN_BANKS = (0, 2, 3), (6, 4, 7, 1, 5)
UP_FIRST = 2
GROUPS = [(0, 6, 2), (6, 10, 3), (10, NIMG, NT)]
AHEAD = 2
EARLY = NPAIR // 2
MASKED = [(half, hd) for hd in range(6) for half in range(2)]
KCH = [128] * (2 * CH) + [HALF, HALF]


def vit(nc, x, cls_tok, gamma, beta, W, b_tok, qkv_w, qkv_b, proj_w, proj_b, in_w, in_b, out_w, out):
    with ExitStack() as ctx:
        def sb(name, shape):
            return ctx.enter_context(nc.sbuf_tensor(name, shape, F32))

        def sem(name):
            return ctx.enter_context(nc.semaphore(name))

        bank = [ctx.enter_context(nc.psum_tensor(f"bank{i}", [128, 512], F32)) for i in range(8)]

        X = sb("X", [ROWS, CH, PS * IMG])
        XTB = sb("XTB", [ROWS, 2, CH, IMG])
        XTBR = sb("XTBR", [ROWS, GR, 2 * CH, PS])
        XLR = sb("XLR", [ROWS, GR, 2, CH, PS])
        XTS = sb("XTS", [128, 2, NCHUNK, T])
        XT, XS = XTS[:, 0], XTS[:, 1]
        XR = XTS[0:ROWS, 1].rearrange("p k t -> p (k t)")[:, 0:2 * CH * GR * 128].rearrange(
            "p (k w f) -> p k w f", k=2 * CH, w=GR)
        WP = sb("WP", [128, NSH, 2, CH, HID])
        WH = sb("WH", [HALF, 2, HID])
        WE = sb("WE", [128, NCHUNK, HID + 1])
        GN = sb("GN", [128, 2, 2, NSH, CH])
        GP = sb("GP", [128, 2, 2, NSH, CH])
        GH = sb("GH", [HALF, 2, 2])
        ident = sb("ident", [128, 128])
        sh = [sb(f"sh{s}", [128, 128]) for s in range(4)]
        inv_n = sb("inv_n", [128, 4])
        one = sb("one", [128, 1])
        R = sb("R", [4, HID])
        IND = sb("IND", [4, NIMG, N])
        neg0 = sb("neg0", [4, 128])
        g1n = sb("g1n", [128, HID])
        BASE = sb("BASE", [128, NT, HID])
        st = sb("st", [128, NT, 2])
        nvar = sb("nvar", [128, NT])
        std = sb("std", [128, NT])
        rstd = sb("rstd", [128, NT])
        u = sb("u", [128, 2, HID])
        h1 = sb("h1", [128, NT, HID])
        bn = sb("bn", [128, NT, 6])
        mv = sb("mv", [128, NT, 2])
        std1 = sb("std1", [128, NT])
        rstd1 = sb("rstd1", [128, NT])
        hn = sb("hn", [128, NT, HID])
        hnT = sb("hnT", [HALF + 1, 2, T])
        eps = sb("eps", [128, 1])
        m10 = sb("m10", [128, 1])
        qkvw = sb("qkvw", [HALF, 6, HID])
        projw = sb("projw", [HALF, 2, HID])
        inw = sb("inw", [128, NF, HID])
        w2 = sb("w2", [128, NF, HID])
        inbr = sb("inbr", [NF, 128])
        inb = sb("inb", [128, NF])
        WQ = sb("WQ", [HALF + 1, 2, 3, HID])
        WO = sb("WO", [HALF + 1, 2, HID])
        WI = sb("WI", [HALF, 2, FFN])
        mask6 = sb("mask6", [HALF, 6])
        qT, kT = (X[:, :, :].rearrange("p c w -> p (c w)")[:, 2 * T * k:2 * T * (k + 1)]
                  .rearrange("p (h t) -> p h t", h=2) for k in range(2))
        K6 = XTS[0:HALF].rearrange("p a k t -> p (a k t)")[:, 0:2 * 6 * T].rearrange(
            "p (h q b j n) -> p h q b j n", h=2, q=2, j=3, n=N)
        V2 = XTS[0:PP].rearrange("p a k t -> p (a k t)")[:, 2 * 6 * T:2 * 6 * T + NPAIR * NH * VW].rearrange(
            "p (i h d) -> p i h d", i=NPAIR, h=NH)
        VB = sb("VB", [G3, NIMG, 3, 4 * VW])
        mx = sb("mx", [PP, 2, NH])
        Pr = sb("Pr", [PP, 2, NH, N])
        PT = sb("PT", [G3, 2, 4, PP])
        ro = sb("ro", [PP, 2, NH])
        On = sb("On", [PP, 2, HID])
        OT = sb("OT", [HALF + 1, 2, T])
        ysq = sb("ysq", [128, 2, HID])
        ss = sb("ss", [128, NT, NH])
        nrm = sb("nrm", [128, NT, NH])
        rn = sb("rn", [128, NT, NH])
        Y = sb("Y", [128, NT, HID])
        YT = sb("YT", [HALF, 2, T])
        E1 = sb("E1", [PP, 2, NH * N])
        E2 = sb("E2", [PP, 3, NH * N])
        h2 = sb("h2", [128, NT, HID])
        bn2 = sb("bn2", [128, NT, 6])
        mv2 = sb("mv2", [128, NT, 2])
        std2 = sb("std2", [128, NT])
        rstd2 = sb("rstd2", [128, NT])
        hn2 = sb("hn2", [128, NT, HID])
        hn2T = sb("hn2T", [HALF, 2, T])
        hT = WP[:, :, :, :, :].rearrange("p s e c n -> p (s e c n)")[:, 0:NF * T].rearrange("p (f t) -> p f t", f=NF)
        res = sb("res", [128, NT, HID])

        S = {}
        for name in (
            "gb_in x0_in x1_in x2_in xtb_in w0_in w1_in w2_in w3_in w4_in wh_in gh_in rows_in qkv_in proj_in "
            "ffnw_in bias_in out_done "
            "pool_step consts_ready wzero masks_ready ones_rows xlr_ready xtb_ready xr_v xr_a xcls_zero "
            "dve_step "
            "placed_mm placed cnt_done xt_mm xt_evac_v xt_evac_a xs_a weff weff_a xs_sum sq_sum "
            "one_ready sq_mm gp_own sums_mm "
            "sums_sb g1_sb base_mm base_sb wt_mm wt_a "
            "emb_mm nvar_ready std_ready h1_ready mv_ready std1_ready hn_ready hnt_mm hnt_sb "
            "vb_zero vb0_in vb1_in v2_ones v2_mm v2_sb q_mm k_mm q_sb k_sb k6_v k6_a "
            "s_mm p_sub p_exp pt_mm pt_sb pv_mm on_ready ot_mm ot_sb "
            "y_mm ysq_ready ss_ready nrm_ready y_ready yt_mm yt_sb t6_v t6_a wo_sb wi_mm wi_sb ysb_ready "
            "s2_mm e1_ready e2_ready pv2_mm on2_ready ot2_mm ot2_sb "
            "y2_mm h2_mv std2_ready hn2_ready hn2t_mm hn2t_sb up_mm gelu_done down_mm res_ready"
        ).split():
            S[name] = sem(name)

        x_v = x.rearrange("b c (h r) w -> h b c (r w)", r=PS)
        W_v = W.rearrange("(p e s c) n -> p e s (c n)", p=128, e=2, s=NSH)
        W_px = W.rearrange("(r q s c) n -> r q s c n", r=PS, q=PS, s=NSH)
        g_v = [v.rearrange("(p k) -> p k", p=128) for v in (gamma, beta)]
        out_v = out.rearrange("b n k -> (b n) k")
        WPf = WP[:, :, :, :, :].rearrange("p s e c n -> p s e (c n)")

        def halo_rows(v, k, side):
            if k == 0:
                return v[:, 0 if side == 0 else PS - 1, 1 + side].rearrange("r c n -> c r n")
            return v[0 if side == 0 else PS - 1, :, 3 + side].rearrange("q c n -> c q n")

        def head_rows(half, hd, b0, b1):
            return K6[:, half, hd // 3, b0:b1, hd % 3, :]

        def tokens(buf, half, b0, b1):
            return buf[:, half, N * b0:N * b1].rearrange("p (b n) -> p b n", n=N)

        def pair_values(b, c0):
            return b[0:PP, c0:c0 + HID].rearrange("p (g j d) -> p g j d", g=4, j=3)

        def v2_rows(p):
            return V2[:, p, :, 0:D].rearrange("p (j g) d -> p g j d", g=4)

        def reorder(c, e):
            return (XR[:, 2 * c + e].rearrange("p w (r h) -> p w r h", h=8),
                    X[:, c, :].rearrange("p (r w h e) -> p e w r h", w=GR, h=8, e=2)[:, e])

        block = ctx.enter_context(nc.Block())

        @block.sync
        def _(sp):
            for k in range(2):
                sp.dma_start(GN[:, k].rearrange("p e s c -> p (e s c)"), g_v[k]).then_inc(S["gb_in"], 16)
            for c in range(CH):
                sp.dma_start(X[:, c, :], x_v[:, :, c]).then_inc(S[f"x{c}_in"], 16)
            for side in range(2):
                edge, h0 = (0, 1) if side == 0 else (GR - 1, 0)
                y = (PS * edge - 1) % IMG if side == 0 else (PS * edge + PS) % IMG
                sp.dma_start(XTB[NIMG * edge:NIMG * (edge + 1), side], x[:, :, y, :]).then_inc(S["xtb_in"], 16)
                y0 = PS - 1 if side == 0 else PS
                for c in range(CH):
                    src = x[:, c, y0:y0 + PS * (GR - 2) + 1:PS, :].rearrange("b h w -> h b w")
                    sp.dma_start(XTB[NIMG * h0:NIMG * (h0 + GR - 1), side, c], src).then_inc(S["xtb_in"], 16)
            sp.dma_start(WPf[:, 0], W_v[:, :, 0]).then_inc(S["w0_in"], 16)
            sp.dma_start(WPf[:, 1, 1], W_v[:, 1, 1]).then_inc(S["w1_in"], 16)
            sp.dma_start(WPf[:, 2, 0], W_v[:, 0, 2]).then_inc(S["w2_in"], 16)
            sp.wait_ge(S["wzero"], 4)
            sp.dma_start(WPf[0:112, 1, 0], W_v[1:113, 0, 1]).then_inc(S["w1_in"], 16)
            sp.dma_start(WPf[112:127, 1, 0], W_v[113:128, 0, 1]).then_inc(S["w1_in"], 16)
            sp.dma_start(WPf[1:113, 2, 1], W_v[0:112, 1, 2]).then_inc(S["w2_in"], 16)
            sp.dma_start(WPf[113:128, 2, 1], W_v[112:127, 1, 2]).then_inc(S["w2_in"], 16)
            sp.dma_start(WPf[0:120, 3], W_v[8:128, :, 3]).then_inc(S["w3_in"], 16)
            sp.dma_start(WPf[8:128, 4], W_v[0:120, :, 4]).then_inc(S["w4_in"], 16)
            for k in range(2):
                for side in range(2):
                    src = halo_rows(W_px, k, side)
                    sp.dma_start(WH[48 * side:48 * (side + 1), k, :], src).then_inc(S["wh_in"], 16)
                    for n, v in enumerate((gamma, beta)):
                        px = v.rearrange("(r q s c n) -> r q s c n", r=PS, q=PS, s=NSH, n=1)
                        sp.dma_start(GH[48 * side:48 * (side + 1), k, n:n + 1], halo_rows(px, k, side),
                                     allow_slow_non_contiguous=True)\
                          .then_inc(S["gh_in"], 16)
            sp.dma_start(R[2:3, :], b_tok.rearrange("(a n) -> a n", a=1)).then_inc(S["rows_in"], 16)
            sp.dma_start(R[3:4, :], cls_tok.rearrange("a b n -> (a b) n")).then_inc(S["rows_in"], 16)
            sp.dma_start(qkvw[:, :, :], qkv_w.rearrange("(o p) n -> p o n", p=HALF)).then_inc(S["qkv_in"], 16)
            sp.dma_start(projw[:, :, :], proj_w.rearrange("(o p) n -> p o n", p=HALF)).then_inc(S["proj_in"], 16)
            sp.dma_start(WQ[HALF:HALF + 1, 1, 0:2, :], qkv_b[0:2 * HID].rearrange("(a k n) -> a k n", a=1, k=2))\
              .then_inc(S["bias_in"], 16)
            for half in range(2):
                for par in range(2):
                    a = HALF * half + 48 * par
                    src = qkv_b[2 * HID + HALF * half:2 * HID + HALF * (half + 1)].rearrange(
                        "(a j q d) -> q a j d", a=1, q=2, d=D)[par]
                    sp.dma_start(WQ[HALF:HALF + 1, 1, 2, a:a + 48].rearrange("a (j d) -> a j d", d=D), src)\
                      .then_inc(S["bias_in"], 16)
            sp.dma_start(WO[HALF:HALF + 1, 1, :], proj_b.rearrange("(a n) -> a n", a=1)).then_inc(S["bias_in"], 16)
            sp.dma_start(inbr[:, :], in_b.rearrange("(f p) -> f p", p=128)).then_inc(S["bias_in"], 16)
            sp.dma_start(inw[:, :, :], in_w.rearrange("(f p) n -> p f n", p=128)).then_inc(S["ffnw_in"], 16)
            sp.dma_start(w2[:, :, :], out_w.rearrange("(f p) n -> p f n", p=128)).then_inc(S["ffnw_in"], 16)
            sp.wait_ge(S["vb_zero"], 1)
            for th in range(2):
                sp.wait_ge(S["v2_sb"], EARLY * (th + 1))
                for j in range(3):
                    for bb in range(2):
                        b0 = NIMG // 2 * th + bb
                        sp.dma_start(VB[N * j:N * (j + 1), b0:NIMG // 2 * (th + 1):2, j, :],
                                     V2[64 * bb:64 * bb + N, EARLY * th:EARLY * (th + 1), 4 * j:4 * (j + 1), :]
                                     .rearrange("p i h d -> p i (h d)")).then_inc(S[f"vb{th}_in"], 16)
            for i, (t0, n) in enumerate(TILES):
                sp.wait_ge(S["res_ready"], i + 1)
                sp.dma_start(out_v[t0:t0 + n, :], res[0:n, i, :]).then_inc(S["out_done"], 16)
            sp.wait_ge(S["out_done"], 16 * NT)

        @block.gpsimd
        def _(pool):
            g = nc.gpsimd
            steps = [0]

            def link(ins):
                steps[0] += 1
                ins.then_inc(S["pool_step"], 1)
                pool.wait_ge(S["pool_step"], steps[0])

            g.memset(ident[:, :], 0.0).then_inc(S["pool_step"], 1)
            for m in sh:
                g.memset(m[:, :], 0.0).then_inc(S["pool_step"], 1)
            steps[0] = 5
            pool.wait_ge(S["pool_step"], 5)

            def diagonal(m, base, lo, hi):
                v = m[:, :].rearrange("p (a h) -> p a h", h=8)[:, :, lo:hi]
                return g.affine_select(out=v, in_=v, compare_op=ALU.not_equal, fill=1.0, base=-base - lo,
                                       pattern=[[-8, 16], [-1, hi - lo]], channel_multiplier=1)

            diagonal(ident, 0, 0, 8).then_inc(S["consts_ready"], 1)
            diagonal(sh[0], 1, 0, 7).then_inc(S["consts_ready"], 1)
            diagonal(sh[1], -1, 1, 8).then_inc(S["consts_ready"], 1)
            diagonal(sh[2], 8, 0, 8).then_inc(S["consts_ready"], 1)
            diagonal(sh[3], -8, 0, 8).then_inc(S["consts_ready"], 1)
            g.memset(inv_n[:, 0:2], 1.0 / FEAT).then_inc(S["consts_ready"], 1)
            g.memset(inv_n[:, 2:4], 2.0 / FEAT).then_inc(S["consts_ready"], 1)
            g.memset(one[:, :], 1.0).then_inc(S["one_ready"], 1)
            g.memset(eps[:, :], EPS).then_inc(S["consts_ready"], 1)
            g.memset(m10[:, :], -SIM_SCALE).then_inc(S["consts_ready"], 1)
            g.memset(XT[:, :, :].rearrange("p k (b n) -> p k b n", n=N)[:, :, :, 0], 0.0).then_inc(S["xcls_zero"], 1)

            for c in range(CH):
                pool.wait_ge(S[f"x{c}_in"], 16)
                Xc = X[:, c, :].rearrange("p (r w) -> p w r", w=IMG)
                g.tensor_copy(XLR[:, 1:GR, 0, c, :], Xc[:, PS - 1:IMG - 1:PS, :]).then_inc(S["xlr_ready"], 1)
                g.tensor_copy(XLR[:, 0, 0, c, :], Xc[:, IMG - 1, :]).then_inc(S["xlr_ready"], 1)
                g.tensor_copy(XLR[:, 0:GR - 1, 1, c, :], Xc[:, PS:IMG:PS, :]).then_inc(S["xlr_ready"], 1)
                g.tensor_copy(XLR[:, GR - 1, 1, c, :], Xc[:, 0, :]).then_inc(S["xlr_ready"], 1)

            
            link(g.memset(IND[:, :, 1:N], 1.0))
            link(g.memset(IND[:, :, 0:1], 0.0))
            link(g.affine_select(out=IND[:, :, 1:N], in_=IND[:, :, 1:N], compare_op=ALU.not_equal, fill=0.0,
                                 base=-3, pattern=[[0, NIMG], [0, N - 1]], channel_multiplier=1))
            link(g.affine_select(out=IND[:, :, 0:1], in_=IND[:, :, 0:1], compare_op=ALU.not_equal, fill=1.0,
                                 base=-3, pattern=[[0, NIMG], [0, 1]], channel_multiplier=1))
            link(g.memset(neg0[:, :], 0.0))
            g.memset(neg0[0:1, :], -1.0).then_inc(S["masks_ready"], 1)
            g.memset(IND[0:1, :, :], 0.0).then_inc(S["masks_ready"], 1)
            link(g.memset(mask6[:, :], 1.0))
            v6 = mask6[:, :].rearrange("p (q j) -> p q j", q=2)
            link(g.affine_select(out=v6, in_=v6, compare_op=ALU.is_ge, fill=0.0, base=0,
                                 pattern=[[-D, 2], [-2 * D, 3]], channel_multiplier=1))
            g.affine_select(out=v6, in_=v6, compare_op=ALU.is_ge, fill=0.0, base=D - 1,
                            pattern=[[D, 2], [2 * D, 3]], channel_multiplier=-1).then_inc(S["masks_ready"], 1)
            for n, (k, into, rows) in enumerate(((2, 0, 128), (3, 1, 128), (4, 0, 128), (5, 1, 128), (7, 6, HALF))):
                pool.wait_ge(S["xs_a"], k + 1)
                if n in (2, 3):
                    pool.wait_ge(S["xs_sum"], n - 1)
                g.tensor_tensor(XS[0:rows, into, :], XS[0:rows, into, :], XS[0:rows, k, :], ALU.add)\
                 .then_inc(S["xs_sum"], 1)
            pool.wait_ge(S["xs_sum"], 5)
            g.memset(VB[:, :, :, :], 0.0).then_inc(S["vb_zero"], 1)

            pool.wait_ge(S["vb_zero"], 1)
            g.memset(hnT[HALF:HALF + 1, :, :], 1.0).then_inc(S["ones_rows"], 1)
            g.memset(OT[HALF:HALF + 1, 1, :], 1.0).then_inc(S["ones_rows"], 1)
            pool.wait_ge(S["ones_rows"], 2)
            pool.wait_ge(S["sq_mm"], NT)
            g.memset(V2[:, :, :, D], 1.0).then_inc(S["v2_ones"], 1)

        @block.scalar
        def _(act):
            a = nc.scalar

            def evac_xt(k, hf):
                src = bank[2 * (k % 2) + hf][0:KCH[k], 0:3 * ROWS].rearrange("p (w h b) -> p w h b", w=3, h=GR)
                dst = XT[0:KCH[k], k, :].rearrange("p (b n) -> p n b", n=N)[:, 1:N, :]\
                    .rearrange("p (h w) b -> p w h b", w=GR)[:, 3 * hf:3 * hf + 3]
                return dst, src

            def parity_rows(c):
                act.wait_ge(S[f"x{c}_in"], 16)
                dst, src = reorder(c, 1)
                for w in range(2):
                    ins = a.activation(dst[:, 3 * w:3 * w + 3], src[:, 3 * w:3 * w + 3], ACT.Copy)
                ins.then_inc(S["xr_a"], 1)

            for c in range(2):
                parity_rows(c)
            for k in range(NCHUNK):
                act.wait_ge(S["xt_mm"], 2 * k + 2)
                dst, src = evac_xt(k, 1)
                for w in range(3):
                    ins = a.activation(dst[:, w], src[:, w], ACT.Copy)
                ins.then_inc(S["xt_evac_a"], 1)
                if k == 0:
                    parity_rows(2)
                if k == 3:
                    act.wait_ge(S["xtb_in"], 16 * 2 * (CH + 1))
                    a.activation(XTBR[:, :, :, :], XTB[:, :, :, :].rearrange("p s c (w q) -> p w (s c) q", w=GR),
                                 ACT.Copy).then_inc(S["xtb_ready"], 1)
            act.wait_ge(S["w0_in"], 16)
            act.wait_ge(S["gp_own"], 1)
            for e in range(2):
                for c in range(CH):
                    a.activation(WE[:, 2 * c + e, 0:HID], WP[:, 0, e, c, :], ACT.Copy, scale=GP[:, 0, e, 0, c:c + 1])\
                     .then_inc(S["weff_a"], 1)
            act.wait_ge(S["xcls_zero"], 1)
            for k in range(NCHUNK):
                act.wait_ge(S["xt_evac_v"], k + 1)
                act.wait_ge(S["xt_evac_a"], k + 1)
                a.activation(XS[0:KCH[k], k, :], XT[0:KCH[k], k, :], ACT.Square).then_inc(S["xs_a"], 1)
            act.wait_ge(S["base_mm"], 1)
            a.activation(g1n[:, :], bank[7][:, 0:HID], ACT.Copy).then_inc(S["g1_sb"], 1)
            nl = TILES[-1][1]
            a.activation(BASE[0:nl, NT - 1, :], bank[7][0:nl, HID:2 * HID], ACT.Copy).then_inc(S["base_sb"], 1)
            for q in range(2):
                act.wait_ge(S["base_mm"], q + 2)
                a.activation(BASE[:, 2 * q:2 * q + 2, :],
                             bank[6 - q][:, 0:HID * 2].rearrange("p (i n) -> p i n", i=2), ACT.Copy)\
                 .then_inc(S["base_sb"], 1)

            def std_of(dst, src, scale, done):
                a.activation(dst, src, ACT.Sqrt, bias=eps[0:dst.shape[0], :], scale=scale).then_inc(done, 1)

            act.wait_ge(S["consts_ready"], 9)

            def mask_rows(buf, half, hd, images, done):
                a.activation(head_rows(half, hd, *images), tokens(buf, half, *images), ACT.Copy, scale=mask6[:, hd:hd + 1])\
                 .then_inc(done, 1)

            def from_transposed(dst, i, src):
                t0, n = TILES[i]
                return a.activation(dst[:, :, t0:t0 + n],
                                    src[0:HALF, 0:256].rearrange("p (k t) -> p k t", k=2)[:, :, 0:n], ACT.Copy)

            WIf = WI[:, :, :].rearrange("p k f -> p (k f)")

            def rows_out(i):
                act.wait_ge(S["hnt_mm"], i + 1)
                from_transposed(hnT[0:HALF], i, bank[i % 2]).then_inc(S["hnt_sb"], 1)

            def queries_out(th):
                for half in range(2):
                    act.wait_ge(S["q_mm"], 2 * th + half + 1)
                    a.activation(qT[:, half, TH * th:TH * (th + 1)], bank[(5, 6, 3, 4)[2 * th + half]][0:HALF, 0:TH],
                                 ACT.Copy).then_inc(S["q_sb"], 1)

            for i in range(NT + 1):
                if i == NT - 1:
                    for q in range(2):
                        rows_out(q)
                if i == NT:
                    for c in range(3):
                        act.wait_ge(S["wi_mm"], c + 1)
                        a.activation(WIf[:, 512 * c:512 * (c + 1)], bank[7 - c][0:HALF, :], ACT.Copy)\
                         .then_inc(S["wi_sb"], 1)
                    rows_out(2)
                if i >= 1:
                    n = TILES[i - 1][1]
                    act.wait_ge(S["mv_ready"], i)
                    std_of(std1[0:n, i - 1:i], mv[0:n, i - 1, 1:2], 1.0, S["std1_ready"])
                if i < NT:
                    n = TILES[i][1]
                    act.wait_ge(S["nvar_ready"], i + 1)
                    std_of(std[0:n, i:i + 1], nvar[0:n, i:i + 1], -1.0, S["std_ready"])
                if i == NT - 2:
                    act.wait_ge(S["wt_mm"], 1)
                    for kh in range(2):
                        a.activation(WQ[0:HALF, kh, 0:2, :],
                                     bank[6 + kh][0:HALF, 0:2 * HID].rearrange("p (k n) -> p k n", k=2), ACT.Copy)\
                         .then_inc(S["wt_a"], 1)
                    act.wait_ge(S["wt_mm"], 2)
                    for kh in range(2):
                        for half in range(2):
                            c0 = HALF * half
                            a.activation(WQ[0:HALF, kh, 2, c0:c0 + HALF].rearrange("p (q j d) -> p j q d", q=2, j=3),
                                         bank[5][0:HALF, HID * kh + c0:HID * kh + c0 + HALF]
                                         .rearrange("p (j q d) -> p j q d", q=2, j=3), ACT.Copy)\
                             .then_inc(S["wt_a"], 1)
            queries_out(0)
            for i in range(3, NT):
                rows_out(i)
            act.wait_ge(S["masks_ready"], 3)
            act.wait_ge(S["k_sb"], 2)
            for half, hd in MASKED[8:]:
                mask_rows(kT, half, hd, (0, NIMG // 2), S["k6_a"])
            queries_out(1)

            def mask_group(g):
                b0, b1, tiles = GROUPS[g]
                act.wait_ge(S["yt_sb"], tiles)
                act.wait_ge(S["s_mm"], b1 // 2)
                for half, hd in MASKED[8:]:
                    mask_rows(YT, half, hd, (b0, b1), S["t6_a"])

            def weigh(p):
                act.wait_ge(S["s2_mm"], p + 1)
                if p >= 2:
                    act.wait_ge(S["e2_ready"], p - 1)
                a.activation(E1[:, p % 2], bank[p % 2][0:PP, 0:NH * N], ACT.Exp, bias=m10[0:PP, :],
                             scale=SIM_SCALE).then_inc(S["e1_ready"], 1)

            for i in range(STEPS):
                if i < EARLY:
                    act.wait_ge(S["v2_mm"], EARLY + i + 1)
                    a.activation(v2_rows(EARLY + i), pair_values(bank[5], 0), ACT.Copy).then_inc(S["v2_sb"], 1)
                if 1 <= i <= NPAIR:
                    p = i - 1
                    act.wait_ge(S["pt_mm"], p + 1)
                    if p >= 2:
                        act.wait_ge(S["pv_mm"], p - 1)
                    a.activation(PT[:, p % 2], bank[2][0:G3, 0:4 * PP].rearrange("p (g t) -> p g t", g=4),
                                 ACT.Copy).then_inc(S["pt_sb"], 1)
                if i < NPAIR:
                    act.wait_ge(S["p_sub"], i + 1)
                    a.activation(Pr[:, i % 2], Pr[:, i % 2], ACT.Exp, scale=SCALE).then_inc(S["p_exp"], 1)
                if i < EARLY:
                    act.wait_ge(S["k_sb"], 4)
                    mask_rows(kT, *MASKED[8 + i], (NIMG // 2, NIMG), S["k6_a"])
                if 3 <= i < NPAIR + 3:
                    p = i - 3
                    act.wait_ge(S["ot_mm"], p + 1)
                    a.activation(OT[0:HALF, :, 2 * N * p:2 * N * (p + 1)].rearrange("p k (b n) -> p k b n", n=N),
                                 bank[4][0:HALF, 0:256].rearrange("p (k b n) -> p k b n", k=2, b=2)[:, :, :, 0:N],
                                 ACT.Copy).then_inc(S["ot_sb"], 1)
                if i == 4:
                    act.wait_ge(S["wt_mm"], 3)
                    a.activation(inb[:, :], bank[7][:, 2 * HID:2 * HID + NF], ACT.Copy).then_inc(S["wo_sb"], 1)
                    a.activation(WO[0:HALF, :, :], bank[7][0:HALF, 0:2 * HID].rearrange("p (k n) -> p k n", k=2),
                                 ACT.Copy).then_inc(S["wo_sb"], 1)
                for k, (t0, n) in enumerate(TILES):
                    if i == Y_STEP[k]:
                        act.wait_ge(S["y_mm"], k + 1)
                        a.activation(Y[0:n, k], bank[6 + k % 2][0:n, 0:HID], ACT.Copy).then_inc(S["ysb_ready"], 1)
                        if k >= 2:
                            act.wait_ge(S["ss_ready"], k - 1)
                        a.activation(ysq[0:n, k % 2], bank[6 + k % 2][0:n, 0:HID], ACT.Square)\
                         .then_inc(S["ysq_ready"], 1)
                if i == STEPS - 1:
                    for p in range(AHEAD):
                        weigh(p)
                for k in range(NT):
                    if i == T_STEP[k]:
                        act.wait_ge(S["yt_mm"], k + 1)
                        from_transposed(YT, k, bank[(5, 2)[k % 2]]).then_inc(S["yt_sb"], 1)
                for k, (t0, n) in enumerate(TILES):
                    if i == ROOT_STEP[k]:
                        act.wait_ge(S["ss_ready"], k + 1)
                        a.activation(nrm[0:n, k], ss[0:n, k], ACT.Sqrt).then_inc(S["nrm_ready"], 1)
                if i == T_STEP[1]:
                    for g in range(2):
                        mask_group(g)

            for i in range(AHEAD, STEPS):
                if i == AHEAD:
                    mask_group(2)
                if i < NPAIR:
                    weigh(i)
                if 3 <= i < NPAIR + 3:
                    p = i - 3
                    act.wait_ge(S["ot2_mm"], p + 1)
                    a.activation(OT[0:HALF, :, 2 * N * p:2 * N * (p + 1)].rearrange("p k (b n) -> p k b n", n=N),
                                 bank[4][0:HALF, 0:256].rearrange("p (k b n) -> p k b n", k=2, b=2)[:, :, :, 0:N],
                                 ACT.Copy).then_inc(S["ot2_sb"], 1)
                for k, (t0, n) in enumerate(TILES):
                    if i == ROOT2_STEP[k] and k <= 2:
                        act.wait_ge(S["h2_mv"], k + 1)
                        std_of(std2[0:n, k:k + 1], mv2[0:n, k, 1:2], 1.0, S["std2_ready"])
                for k in range(NT):
                    if i == T_STEP[k] and k < 3:
                        act.wait_ge(S["hn2t_mm"], k + 1)
                        from_transposed(hn2T, k, bank[HN2T_BANKS[k]]).then_inc(S["hn2t_sb"], 1)
                for k, (t0, n) in enumerate(TILES):
                    if i == ROOT2_STEP[k] and k > 2:
                        act.wait_ge(S["h2_mv"], k + 1)
                        std_of(std2[0:n, k:k + 1], mv2[0:n, k, 1:2], 1.0, S["std2_ready"])

            for th in range(2):
                for f in range(NF):
                    q = NF * th + f
                    act.wait_ge(S["up_mm"], q + 1)
                    if q == UP_FIRST:
                        for k in range(3, NT):
                            act.wait_ge(S["hn2t_mm"], k + 1)
                            from_transposed(hn2T, k, bank[HN2T_BANKS[k]]).then_inc(S["hn2t_sb"], 1)
                    a.activation(hT[:, f, TH * th:TH * (th + 1)], bank[UP_BANKS[q % 3]][:, 0:TH], ACT.Gelu,
                                 bias=inb[:, f:f + 1]).then_inc(S["gelu_done"], 1)

        @block.vector
        def _(dve):
            v = nc.vector
            steps = [0]

            def link(ins):
                steps[0] += 1
                ins.then_inc(S["dve_step"], 1)
                dve.wait_ge(S["dve_step"], steps[0])

            v.memset(WPf[96:128, 1, 0], 0.0).then_inc(S["wzero"], 1)
            v.memset(WPf[0:32, 2, 1], 0.0).then_inc(S["wzero"], 1)
            v.memset(WPf[96:128, 3], 0.0).then_inc(S["wzero"], 1)
            v.memset(WPf[0:32, 4], 0.0).then_inc(S["wzero"], 1)
            dve.wait_ge(S["gb_in"], 32)
            v.tensor_copy(GP[:, :, :, :, :], GN[:, :, :, :, :]).then_inc(S["gp_own"], 1)

            def parity_rows(c):
                dve.wait_ge(S[f"x{c}_in"], 16)
                dst, src = reorder(c, 0)
                v.tensor_copy(dst, src).then_inc(S["xr_v"], 1)

            def features_out(k):
                dve.wait_ge(S["xt_mm"], 2 * k + 1)
                src = bank[2 * (k % 2)][0:KCH[k], 0:3 * ROWS].rearrange("p (w h b) -> p w h b", w=3, h=GR)
                dst = XT[0:KCH[k], k, :].rearrange("p (b n) -> p n b", n=N)[:, 1:N, :]\
                    .rearrange("p (h w) b -> p w h b", w=GR)[:, 0:3]
                for w in range(3):
                    ins = v.tensor_copy(dst[:, w], src[:, w])
                ins.then_inc(S["xt_evac_v"], 1)

            for c in range(2):
                parity_rows(c)
            features_out(0)
            parity_rows(2)
            features_out(1)
            dve.wait_ge(S["gp_own"], 1)
            dve.wait_ge(S["placed_mm"], 2)
            pl = bank[4]
            link(v.tensor_copy(GP[:, :, 0, 1, :], pl[:, 0:6].rearrange("p (k c) -> p k c", k=2)))
            link(v.tensor_copy(GP[:, :, 1, 2, :], pl[:, 8:14].rearrange("p (k c) -> p k c", k=2)))
            for q in range(2):
                ins = v.tensor_copy(GP[:, :, :, 3 + q, :],
                                    pl[:, 16 + 12 * q:28 + 12 * q].rearrange("p (k e c) -> p k e c", k=2, e=2))
            ins.then_inc(S["placed"], 1)
            for e in range(2):
                v.tensor_copy(WE[:, e:2 * CH:2, HID], pl[:, 48 + e:49 + e].to_broadcast([128, CH]))
            v.memset(WE[0:HALF, 2 * CH:NCHUNK, HID:HID + 1], 1.0 / FEAT).then_inc(S["cnt_done"], 1)

            for k in range(2, NCHUNK):
                features_out(k)

            dve.wait_ge(S["placed"], 1)
            order = [((0, 0), (0, 1)), ((1, 1), (1, 0)), ((2, 1), (2, 0)), ((3, 0), (3, 1)), ((4, 0), (4, 1))]
            arrive = [16, 48, 48, 16, 16]
            for q, pair in enumerate(order):
                if q == 0:
                    continue
                dve.wait_ge(S[f"w{q}_in"], arrive[q])
                for e2, (s, e) in enumerate(pair):
                    for c in range(CH):
                        dst = WE[:, 2 * c + e2, 0:HID]
                        gcol = GP[:, 0, e, s, c:c + 1]
                        n = CH * e2 + c + 1
                        if q == 1:
                            dve.wait_ge(S["weff_a"], n)
                        else:
                            dve.wait_ge(S["weff"], 6 * (q - 2) + n)
                        v.scalar_tensor_tensor(out=dst, in0=WP[:, s, e, c, :], scalar=gcol, in1=dst,
                                               op0=ALU.mult, op1=ALU.add).then_inc(S["weff"], 1)
            dve.wait_ge(S["wh_in"], 16 * 4)
            dve.wait_ge(S["gh_in"], 16 * 8)
            for k in range(2):
                v.tensor_scalar(WE[0:HALF, 2 * CH + k, 0:HID], WH[:, k, :], GH[:, k, 0:1], None, ALU.mult)\
                 .then_inc(S["weff"], 1)

            dve.wait_ge(S["sums_mm"], 1)
            v.tensor_copy(R[0:2, :], bank[5][0:2, 0:HID]).then_inc(S["sums_sb"], 1)
            dve.wait_ge(S["xs_sum"], 5)
            dve.wait_ge(S["xs_a"], NCHUNK)
            dve.wait_ge(S["cnt_done"], 1)
            link(v.tensor_scalar(XS[:, 0, :], XS[:, 0, :], WE[:, 0, HID:HID + 1], None, ALU.mult))
            link(v.scalar_tensor_tensor(out=XS[:, 0, :], in0=XS[:, 1, :], scalar=WE[:, 1, HID:HID + 1], in1=XS[:, 0, :],
                                        op0=ALU.mult, op1=ALU.add))
            v.scalar_tensor_tensor(out=XS[0:HALF, 0, :], in0=XS[0:HALF, 6, :], scalar=1.0 / FEAT, in1=XS[0:HALF, 0, :],
                                   op0=ALU.mult, op1=ALU.add).then_inc(S["sq_sum"], 1)

            for i in range(NT + 2):
                if i >= 2:
                    k = i - 2
                    n = TILES[k][1]
                    dve.wait_ge(S["std1_ready"], k + 1)
                    link(v.reciprocal(rstd1[0:n, k:k + 1], std1[0:n, k:k + 1]))
                    v.tensor_scalar(hn[0:n, k], h1[0:n, k], mv[0:n, k, 0:1], rstd1[0:n, k:k + 1],
                                    ALU.subtract, ALU.mult).then_inc(S["hn_ready"], 1)
                if 1 <= i <= NT:
                    k = i - 1
                    n = TILES[k][1]
                    if k == 0:
                        dve.wait_ge(S["g1_sb"], 1)
                        dve.wait_ge(S["base_sb"], 3)
                    link(v.scalar_tensor_tensor(out=u[0:n, k % 2], in0=g1n[0:n, :], scalar=st[0:n, k, 0:1],
                                                in1=bank[k][0:n, 0:HID], op0=ALU.mult, op1=ALU.add))
                    dve.wait_ge(S["std_ready"], k + 1)
                    link(v.reciprocal(rstd[0:n, k:k + 1], std[0:n, k:k + 1]))
                    v.scalar_tensor_tensor(out=h1[0:n, k], in0=u[0:n, k % 2], scalar=rstd[0:n, k:k + 1],
                                           in1=BASE[0:n, k], op0=ALU.mult, op1=ALU.add).then_inc(S["h1_ready"], 1)
                    dve.wait_ge(S["h1_ready"], k + 1)
                    link(v.bn_stats(bn[0:n, k], h1[0:n, k]))
                    v.bn_aggr(mv[0:n, k], bn[0:n, k]).then_inc(S["mv_ready"], 1)
                if i < NT:
                    n = TILES[i][1]
                    dve.wait_ge(S["sq_mm"], NT)
                    if i >= 2:
                        dve.wait_ge(S["emb_mm"], i - 1)
                    link(v.tensor_copy(st[0:n, i, :], bank[i][0:n, HID:HID + 2]))
                    link(v.scalar_tensor_tensor(out=nvar[0:n, i:i + 1], in0=st[0:n, i, 0:1], scalar=st[0:n, i, 0:1],
                                                in1=st[0:n, i, 1:2], op0=ALU.mult, op1=ALU.subtract))
                    v.tensor_scalar(nvar[0:n, i:i + 1], nvar[0:n, i:i + 1], 0.0, None, ALU.min)\
                     .then_inc(S["nvar_ready"], 1)

            def mask_rows(buf, half, hd, images, done):
                v.tensor_scalar(head_rows(half, hd, *images), tokens(buf, half, *images), mask6[:, hd:hd + 1], None, ALU.mult)\
                 .then_inc(done, 1)

            for th in range(2):
                for half in range(2):
                    dve.wait_ge(S["k_mm"], 2 * th + half + 1)
                    v.tensor_copy(kT[:, half, TH * th:TH * (th + 1)], bank[(7, 2, 6, 7)[2 * th + half]][0:HALF, 0:TH])\
                     .then_inc(S["k_sb"], 1)
                if th == 0:
                    dve.wait_ge(S["masks_ready"], 3)
                    dve.wait_ge(S["k_sb"], 2)
                    for half, hd in MASKED[:8]:
                        mask_rows(kT, half, hd, (0, NIMG // 2), S["k6_v"])
                    dve.wait_ge(S["v2_ones"], 1)
                    for p in range(EARLY):
                        dve.wait_ge(S["v2_mm"], p - p % 2 + 2)
                        v.tensor_copy(v2_rows(p), pair_values(bank[3 + p // 2], HID * (p % 2))).then_inc(S["v2_sb"], 1)
            def normalise(parts, p, done):
                for b, p0, p1 in parts:
                    ins = v.reciprocal(ro[p0:p1, p % 2], bank[b][p0:p1, 0:NH * VW].rearrange("p (h d) -> p h d", d=VW)[:, :, D])
                link(ins)
                for b, p0, p1 in parts:
                    o = bank[b][p0:p1, 0:NH * VW].rearrange("p (h d) -> p h d", d=VW)
                    ins = v.tensor_tensor(On[p0:p1, p % 2].rearrange("p (h d) -> p h d", d=D), o[:, :, 0:D],
                                          ro[p0:p1, p % 2].unsqueeze(2).to_broadcast([p1 - p0, NH, D]), ALU.mult)
                ins.then_inc(done, 1)

            def mask_group(g):
                b0, b1, tiles = GROUPS[g]
                dve.wait_ge(S["yt_sb"], tiles)
                dve.wait_ge(S["s_mm"], b1 // 2)
                for half, hd in MASKED[:8]:
                    mask_rows(YT, half, hd, (b0, b1), S["t6_v"])

            def drop(p):
                dve.wait_ge(S["e1_ready"], p + 1)
                if p >= 3:
                    dve.wait_ge(S["pv2_mm"], p - 2)
                v.scalar_tensor_tensor(out=E2[:, p % 3], in0=bank[p % 2][0:PP, 0:NH * N], scalar=0.0,
                                       in1=E1[:, p % 2], op0=ALU.is_ge, op1=ALU.mult).then_inc(S["e2_ready"], 1)

            for i in range(STEPS):
                if i < NPAIR:
                    dve.wait_ge(S["s_mm"], i + 1)
                    s3 = bank[i % 2][0:PP, 0:NH * N].rearrange("p (h m) -> p h m", m=N)
                    link(v.tensor_reduce(mx[:, i % 2], s3, AX.X, ALU.max))
                    if i >= 2:
                        dve.wait_ge(S["pt_mm"], i - 1)
                    v.tensor_tensor(Pr[:, i % 2], s3, mx[:, i % 2].unsqueeze(2).to_broadcast([PP, NH, N]),
                                    ALU.subtract).then_inc(S["p_sub"], 1)
                if i < EARLY:
                    dve.wait_ge(S["k_sb"], 4)
                    for half, hd in MASKED[2 * i:2 * i + 2]:
                        mask_rows(kT, half, hd, (NIMG // 2, NIMG), S["k6_v"])
                if 2 <= i < NPAIR + 2:
                    p = i - 2
                    dve.wait_ge(S["pv_mm"], p + 1)
                    if p >= 2:
                        dve.wait_ge(S["ot_mm"], p - 1)
                    normalise([(3, 0, PP)], p, S["on_ready"])
                for k, (t0, n) in enumerate(TILES):
                    if i == T_STEP[k]:
                        dve.wait_ge(S["nrm_ready"], k + 1)
                        link(v.tensor_scalar(nrm[0:n, k], nrm[0:n, k], NORM_EPS, None, ALU.max))
                        link(v.reciprocal(rn[0:n, k], nrm[0:n, k]))
                        dve.wait_ge(S["ysb_ready"], k + 1)
                        v.tensor_tensor(Y[0:n, k].rearrange("p (h d) -> p h d", d=D),
                                        Y[0:n, k].rearrange("p (h d) -> p h d", d=D),
                                        rn[0:n, k].unsqueeze(2).to_broadcast([n, NH, D]), ALU.mult)\
                         .then_inc(S["y_ready"], 1)
                for k, (t0, n) in enumerate(TILES):
                    if i == Y_STEP[k]:
                        dve.wait_ge(S["ysq_ready"], k + 1)
                        v.tensor_reduce(ss[0:n, k], ysq[0:n, k % 2].rearrange("p (h d) -> p h d", d=D), AX.X, ALU.add)\
                         .then_inc(S["ss_ready"], 1)
                if i == T_STEP[1]:
                    mask_group(0)
            mask_group(1)
            for p in range(AHEAD):
                drop(p)

            for i in range(AHEAD, STEPS):
                if i == AHEAD:
                    mask_group(2)
                if i < NPAIR:
                    drop(i)
                if 2 <= i < NPAIR + 2:
                    p = i - 2
                    dve.wait_ge(S["pv2_mm"], p + 1)
                    if p >= 2:
                        dve.wait_ge(S["ot2_mm"], p - 1)
                    normalise([(OUT_BANKS[p][0], 0, N), (OUT_BANKS[p][1], 64, PP)], p, S["on2_ready"])
                for k, (t0, n) in enumerate(TILES):
                    if i == (T_STEP[k] - 1 if k < 2 else T_STEP[k]):
                        dve.wait_ge(S["std2_ready"], k + 1)
                        link(v.reciprocal(rstd2[0:n, k:k + 1], std2[0:n, k:k + 1]))
                        v.tensor_scalar(hn2[0:n, k], h2[0:n, k], mv2[0:n, k, 0:1], rstd2[0:n, k:k + 1],
                                        ALU.subtract, ALU.mult).then_inc(S["hn2_ready"], 1)
                for k, (t0, n) in enumerate(TILES):
                    if i == Y_STEP[k]:
                        dve.wait_ge(S["y2_mm"], k + 1)
                        link(v.tensor_tensor(h2[0:n, k], bank[6 + k % 2][0:n, 0:HID], h1[0:n, k], ALU.add))
                        link(v.bn_stats(bn2[0:n, k], h2[0:n, k]))
                        v.bn_aggr(mv2[0:n, k], bn2[0:n, k]).then_inc(S["h2_mv"], 1)
            for i, (t0, n) in enumerate(TILES):
                dve.wait_ge(S["down_mm"], i + 1)
                v.tensor_tensor(res[0:n, i], bank[DOWN_BANKS[i]][0:n, 0:HID], h2[0:n, i], ALU.add).then_inc(S["res_ready"], 1)

        @block.tensor
        def _(pe):
            t = nc.tensor
            pe.wait_ge(S["gb_in"], 32)
            pe.wait_ge(S["consts_ready"], 7)
            pl = bank[4]
            t.matmul(pl[:, 0:6], sh[0][:, :], GN[:, :, 0, 1, :], start=True, stop=True)
            t.matmul(pl[:, 8:14], sh[1][:, :], GN[:, :, 1, 2, :], start=True, stop=True)
            for q in range(2):
                ins = t.matmul(pl[:, 16 + 12 * q:28 + 12 * q], sh[2 + q][:, :], GN[:, :, :, 3 + q, :], start=True, stop=True)
            ins.then_inc(S["placed_mm"], 1)
            t.matmul(pl[:, 48:50], ident[:, :], inv_n[:, 2:4], start=True, stop=False)
            for q in range(2):
                t.matmul(pl[:, 48:50], sh[2 + q][:, :], inv_n[:, 0:2], start=False, stop=False)
            t.matmul(pl[:, 48:49], sh[1][:, :], inv_n[:, 0:1], start=False, stop=False)
            t.matmul(pl[:, 49:50], sh[0][:, :], inv_n[:, 0:1], start=False, stop=True).then_inc(S["placed_mm"], 1)

            for k in range(NCHUNK):
                if k < 2 * CH:
                    pe.wait_ge(S["xr_a" if k % 2 else "xr_v"], k // 2 + 1)
                elif k == 2 * CH:
                    pe.wait_ge(S["xlr_ready"], 4 * CH)
                else:
                    pe.wait_ge(S["xtb_ready"], 1)
                if k >= 2:
                    pe.wait_ge(S["xt_evac_v"], k - 1)
                    pe.wait_ge(S["xt_evac_a"], k - 1)
                for wx in range(GR):
                    if k < 2 * CH:
                        src = XR[:, k, wx]
                    elif k == 2 * CH:
                        src = XLR[:, wx].rearrange("p s c r -> p (s c r)")
                    else:
                        src = XTBR[:, wx].rearrange("p s q -> p (s q)")
                    dst = bank[2 * (k % 2) + wx // 3][0:KCH[k], ROWS * (wx % 3):ROWS * (wx % 3 + 1)]
                    ins = t.transpose(dst, src, ident[0:ROWS, 0:ROWS])
                    if wx % 3 == 2:
                        ins.then_inc(S["xt_mm"], 1)

            pe.wait_ge(S["placed"], 1)
            arrive = [16, 48, 48, 16, 16]
            for s in range(NSH):
                pe.wait_ge(S[f"w{s}_in"], arrive[s])
                for e in range(2):
                    for c in range(CH):
                        t.matmul(bank[5][0:2, 0:HID], GP[:, :, e, s, c], WP[:, s, e, c, :],
                                 start=(s, e, c) == (0, 0, 0), stop=False)
            pe.wait_ge(S["wh_in"], 16 * 4)
            pe.wait_ge(S["gh_in"], 16 * 8)
            for k in range(2):
                ins = t.matmul(bank[5][0:2, 0:HID], GH[:, k, :], WH[:, k, :], start=False, stop=k == 1)
            ins.then_inc(S["sums_mm"], 1)

            def emb(i, ks):
                t0, n = TILES[i]
                for k in ks:
                    ins = t.matmul(bank[i][0:n, 0:HID + 1], XT[0:KCH[k], k, t0:t0 + n], WE[0:KCH[k], k, :],
                                   start=k == 0, stop=k == NCHUNK - 1)
                return ins

            for n, k in enumerate((0, 2, 4, 1, 3, 5)):
                pe.wait_ge(S["weff"], 6 * (NSH - 2) + n + 1)
                for i in range(2):
                    emb(i, [k])
            pe.wait_ge(S["weff"], 6 * (NSH - 1) + 2)
            for i in range(2):
                emb(i, (6, 7))
            pe.wait_ge(S["sums_sb"], 1)
            pe.wait_ge(S["rows_in"], 32)
            pe.wait_ge(S["masks_ready"], 2)
            t.matmul(bank[7][:, 0:HID], neg0[:, :], R[:, :], start=True, stop=True)

            def base(i, dst, c0):
                t0, n = TILES[i]
                return t.matmul(dst[0:n, c0:c0 + HID], IND[:, :, :].rearrange("p b n -> p (b n)")[:, t0:t0 + n], R[:, :],
                                start=True, stop=True)

            base(NT - 1, bank[7], HID).then_inc(S["base_mm"], 1)
            for q in range(2):
                for i in range(2):
                    ins = base(2 * q + i, bank[6 - q], HID * i)
                ins.then_inc(S["base_mm"], 1)
            pe.wait_ge(S["sq_sum"], 1)
            pe.wait_ge(S["one_ready"], 1)
            for i, (t0, n) in enumerate(TILES):
                t.matmul(bank[i][0:n, HID + 1:HID + 2], XS[:, 0, t0:t0 + n], one[:, :], start=True, stop=True)\
                    .then_inc(S["sq_mm"], 1)

            for i in range(2, NT):
                if i == NT - 1:
                    pe.wait_ge(S["qkv_in"], 16)
                    pe.wait_ge(S["base_sb"], 3)
                    for kh in range(2):
                        for o in range(4):
                            ins = t.transpose(bank[6 + kh][0:HALF, HALF * o:HALF * (o + 1)],
                                              qkvw[:, o, HALF * kh:HALF * (kh + 1)], ident[0:HALF, 0:HALF])
                    ins.then_inc(S["wt_mm"], 1)
                    for kh in range(2):
                        for o in range(2):
                            ins = t.transpose(bank[5][0:HALF, HID * kh + HALF * o:HID * kh + HALF * (o + 1)],
                                              qkvw[:, 4 + o, HALF * kh:HALF * (kh + 1)], ident[0:HALF, 0:HALF])
                    ins.then_inc(S["wt_mm"], 1)
                emb(i, (0, 2, 4, 1, 3, 5, 6, 7)).then_inc(S["emb_mm"], 1)

            def to_features(src, i, dst):
                n = TILES[i][1]
                for kh in range(2):
                    ins = t.transpose(dst[0:HALF, 128 * kh:128 * kh + n], src[0:n, i, HALF * kh:HALF * (kh + 1)],
                                      ident[0:n, 0:n])
                return ins

            def queries_keys(th):
                for qk, done in ((1, S["k_mm"]), (0, S["q_mm"])):
                    if th == 1 and qk == 0:
                        pe.wait_ge(S["v2_sb"], EARLY)
                    for half in range(2):
                        dst = bank[((5, 6, 3, 4), (7, 2, 6, 7))[qk][2 * th + half]][0:HALF, 0:TH]
                        for kh in range(2):
                            K = HALF + kh
                            ins = t.matmul(dst, WQ[0:K, kh, qk, HALF * half:HALF * (half + 1)],
                                           hnT[0:K, kh, TH * th:TH * (th + 1)], start=kh == 0, stop=kh == 1)
                        ins.then_inc(done, 1)

            def to_feature_rows(i):
                pe.wait_ge(S["hn_ready"], i + 1)
                if i >= 2:
                    pe.wait_ge(S["hnt_sb"], i - 1)
                to_features(hn, i, bank[i % 2]).then_inc(S["hnt_mm"], 1)

            def rows_of(bb):
                return 64 if bb == 0 else N

            def pair_v(p, dst, c0):
                for kh in range(2):
                    for bb in range(2):
                        K, M, t0 = HALF + kh, rows_of(bb), N * (2 * p + bb)
                        ins = t.matmul(dst[64 * bb:64 * bb + M, c0:c0 + HID], hnT[0:K, kh, t0:t0 + M], WQ[0:K, kh, 2, :],
                                       start=kh == 0, stop=kh == 1)
                return ins

            for i in range(2):
                to_feature_rows(i)
            pe.wait_ge(S["ffnw_in"], 32)
            pe.wait_ge(S["wt_a"], 6)
            for q in range(2 * NF):
                kh, f = divmod(q, NF)
                ins = t.transpose(bank[7 - q // 4][0:HALF, 128 * (q % 4):128 * (q % 4 + 1)],
                                  inw[:, f, HALF * kh:HALF * (kh + 1)], ident[:, :])
                if q % 4 == 3:
                    ins.then_inc(S["wi_mm"], 1)
            to_feature_rows(2)
            pe.wait_ge(S["ones_rows"], 2)
            pe.wait_ge(S["bias_in"], 16 * 7)
            pe.wait_ge(S["wt_a"], 6)
            pe.wait_ge(S["hnt_sb"], 3)
            pe.wait_ge(S["wi_sb"], 3)
            queries_keys(0)
            pe.wait_ge(S["hn_ready"], NT)
            for i in range(3, NT):
                to_feature_rows(i)
            for p in range(EARLY):
                pair_v(p, bank[3 + p // 2], HID * (p % 2)).then_inc(S["v2_mm"], 1)
            pe.wait_ge(S["hnt_sb"], NT)
            pe.wait_ge(S["k_sb"], 1)
            pe.wait_ge(S["q_sb"], 2)
            queries_keys(1)

            def scores(p):
                for bb in range(2):
                    b, M = 2 * p + bb, rows_of(bb)
                    for half in range(2):
                        ins = t.matmul(bank[p % 2][64 * bb:64 * bb + M, 6 * N * half:6 * N * (half + 1)],
                                       qT[:, half, N * b:N * b + M],
                                       K6[:, half, :, b].rearrange("p q j n -> p q (j n)"),
                                       start=True, stop=True)
                return ins

            def values(p):
                for bb in range(2):
                    for g in range(4):
                        o = bank[3][64 * bb:64 * bb + rows_of(bb), 0:NH * VW].rearrange(
                            "p (h j q d) -> p h q j d", h=2, j=3, q=2)[:, g // 2, g % 2]
                        ins = t.matmul(o, PT[:, p % 2, g, 64 * bb:64 * bb + rows_of(bb)],
                                       VB[:, 2 * p + bb, :, VW * g:VW * (g + 1)], start=True, stop=True)
                return ins

            def similarities(p):
                for bb in range(2):
                    b, M = 2 * p + bb, rows_of(bb)
                    for half in range(2):
                        ins = t.matmul(bank[p % 2][64 * bb:64 * bb + M, 6 * N * half:6 * N * (half + 1)],
                                       YT[:, half, N * b:N * b + M],
                                       K6[:, half, :, b].rearrange("p q j n -> p q (j n)"), start=True, stop=True)
                return ins

            def values2(p):
                for k in range(NH):
                    g, j = divmod(k, 3)
                    c0 = VW * (6 * (g // 2) + 2 * j + g % 2)
                    for bb in range(2):
                        a0, a1 = 64 * bb, 64 * bb + N
                        ins = t.matmul(bank[OUT_BANKS[p][bb]][a0:a1, c0:c0 + VW], E2[a0:a1, p % 3, N * k:N * (k + 1)],
                                       V2[a0:a1, p, 4 * j + g, :], start=True, stop=True)
                return ins

            def up(q):
                th, f = divmod(q, NF)
                pe.wait_ge(S["hn2t_sb"], 3 if th == 0 else NT)
                if q >= len(UP_BANKS):
                    pe.wait_ge(S["gelu_done"], q - len(UP_BANKS) + 1)
                for kh in range(2):
                    ins = t.matmul(bank[UP_BANKS[q % 3]][:, 0:TH], WI[:, kh, 128 * f:128 * (f + 1)],
                                   hn2T[:, kh, TH * th:TH * (th + 1)], start=kh == 0, stop=kh == 1)
                ins.then_inc(S["up_mm"], 1)

            def out_features(p, dst):
                for kh in range(2):
                    ins = t.transpose(dst[0:HALF, 128 * kh:128 * kh + PP], On[:, p % 2, HALF * kh:HALF * (kh + 1)],
                                      ident[0:PP, 0:PP])
                return ins

            def project(i):
                t0, n = TILES[i]
                for kh in range(2):
                    K = HALF + kh
                    ins = t.matmul(bank[6 + i % 2][0:n, 0:HID], OT[0:K, kh, t0:t0 + n], WO[0:K, kh, :],
                                   start=kh == 0, stop=kh == 1)
                return ins

            def transpose_hn2(k):
                pe.wait_ge(S["hn2_ready"], k + 1)
                if k >= 3:
                    pe.wait_ge(S["hn2t_sb"], k - 2)
                to_features(hn2, k, bank[HN2T_BANKS[k]]).then_inc(S["hn2t_mm"], 1)

            pe.wait_ge(S["k6_v"], 8)
            pe.wait_ge(S["k6_a"], 4)
            for i in range(STEPS):
                if i < NPAIR:
                    if i >= 2:
                        pe.wait_ge(S["p_sub"], i - 1)
                    if i == EARLY:
                        pe.wait_ge(S["k6_v"], 16)
                        pe.wait_ge(S["k6_a"], 8)
                    scores(i).then_inc(S["s_mm"], 1)
                    if i < EARLY:
                        if i:
                            pe.wait_ge(S["v2_sb"], EARLY + i)
                        pair_v(EARLY + i, bank[5], 0).then_inc(S["v2_mm"], 1)
                if i == 3:
                    pe.wait_ge(S["proj_in"], 16)
                    pe.wait_ge(S["k_sb"], 4)
                    for kh in range(2):
                        for o in range(2):
                            src = projw[:, o, HALF * kh:HALF * (kh + 1)]
                            t.transpose(bank[7][0:HALF, HID * kh + HALF * o:HID * kh + HALF * (o + 1)], src,
                                        ident[0:HALF, 0:HALF])
                    t.transpose(bank[7][:, 2 * HID:2 * HID + NF], inbr[:, :], ident[0:NF, 0:NF])\
                        .then_inc(S["wt_mm"], 1)
                if 1 <= i <= NPAIR:
                    p = i - 1
                    pe.wait_ge(S["p_exp"], p + 1)
                    if p >= 1:
                        pe.wait_ge(S["pt_sb"], p)
                    else:
                        pe.wait_ge(S["k_sb"], 2)
                    for g in range(4):
                        ins = t.transpose(bank[2][0:G3, PP * g:PP * (g + 1)],
                                          Pr[:, p % 2, 3 * g:3 * g + 3, :].rearrange("p h m -> p (h m)"),
                                          ident[0:PP, 0:PP])
                    ins.then_inc(S["pt_mm"], 1)
                if 2 <= i <= NPAIR + 1:
                    p = i - 2
                    pe.wait_ge(S["pt_sb"], p + 1)
                    pe.wait_ge(S[f"vb{p // EARLY}_in"], 16 * 6)
                    if p == 0:
                        pe.wait_ge(S["q_sb"], 4)
                    if p >= 1:
                        pe.wait_ge(S["on_ready"], p)
                    values(p).then_inc(S["pv_mm"], 1)
                if 3 <= i < NPAIR + 3:
                    p = i - 3
                    pe.wait_ge(S["on_ready"], p + 1)
                    if p >= 1:
                        pe.wait_ge(S["ot_sb"], p)
                    out_features(p, bank[4]).then_inc(S["ot_mm"], 1)
                for k in range(NT):
                    if i == Y_STEP[k]:
                        pe.wait_ge(S["wo_sb"], 2)
                        pe.wait_ge(S["ot_sb"], LAST_PAIR[k] + 1)
                        if k >= 2:
                            pe.wait_ge(S["ysq_ready"], k - 1)
                        project(k).then_inc(S["y_mm"], 1)
                if i == STEPS - 1:
                    pe.wait_ge(S["t6_v"], 8)
                    pe.wait_ge(S["t6_a"], 4)
                    for p in range(AHEAD):
                        similarities(p).then_inc(S["s2_mm"], 1)
                for k in range(NT):
                    if i == T_STEP[k]:
                        pe.wait_ge(S["y_ready"], k + 1)
                        if k >= 2:
                            pe.wait_ge(S["yt_sb"], k - 1)
                        else:
                            pe.wait_ge(S["v2_sb"], NPAIR)
                            pe.wait_ge(S["pt_sb"], NPAIR)
                        to_features(Y, k, bank[(5, 2)[k % 2]]).then_inc(S["yt_mm"], 1)

            for i in range(AHEAD, STEPS):
                if i < NPAIR:
                    pe.wait_ge(S["e2_ready"], i - 1)
                    groups = sum(b0 < 2 * i + 2 for b0, _, _ in GROUPS)
                    pe.wait_ge(S["t6_v"], 8 * groups)
                    pe.wait_ge(S["t6_a"], 4 * groups)
                    similarities(i).then_inc(S["s2_mm"], 1)
                if 2 <= i <= NPAIR + 1:
                    p = i - 2
                    pe.wait_ge(S["e2_ready"], p + 1)
                    if 1 <= p < NPAIR - 1:
                        pe.wait_ge(S["on2_ready"], p)
                    else:
                        pe.wait_ge(S["yt_sb"], NT)
                    values2(p).then_inc(S["pv2_mm"], 1)
                if 3 <= i < NPAIR + 3:
                    p = i - 3
                    pe.wait_ge(S["on2_ready"], p + 1)
                    pe.wait_ge(*((S["ot2_sb"], p) if p else (S["ot_sb"], NPAIR)))
                    out_features(p, bank[4]).then_inc(S["ot2_mm"], 1)
                for k in range(2):
                    if i == T_STEP[k]:
                        transpose_hn2(k)
                for k in range(NT):
                    if i == Y_STEP[k]:
                        if k == NT - 1:
                            transpose_hn2(2)
                        pe.wait_ge(S["ot2_sb"], LAST_PAIR[k] + 1)
                        if k >= 2:
                            pe.wait_ge(S["h2_mv"], k - 1)
                        else:
                            pe.wait_ge(S["ysq_ready"], NT)
                        project(k).then_inc(S["y2_mm"], 1)
                if i == STEPS - 1:
                    for q in range(UP_FIRST):
                        up(q)
                for k in range(NT):
                    if k >= 3 and i == T_STEP[k]:
                        transpose_hn2(k)

            for q in range(UP_FIRST, 2 * NF):
                up(q)
            for i, (t0, n) in enumerate(TILES):
                pe.wait_ge(S["gelu_done"], NF if t0 + n <= TH else 2 * NF)
                for f in range(NF):
                    ins = t.matmul(bank[DOWN_BANKS[i]][0:n, 0:HID], hT[:, f, t0:t0 + n], w2[:, f, :],
                                   start=f == 0, stop=f == NF - 1)
                ins.then_inc(S["down_mm"], 1)


_INS = ["x", "cls_tok", "L0_tok_ln_gamma", "L0_tok_ln_beta", "L0_tok_W", "L0_tok_b", "L0_attn_qkv_w",
        "L0_attn_qkv_b", "L0_attn_proj_w", "L0_attn_proj_b", "L0_ffn_in_weight", "L0_ffn_in_bias",
        "L0_ffn_out_weight"]


def kernel(**inputs):
    import numpy as _np
    import concourse.bacc as _bacc
    from concourse import mybir as _mybir
    from concourse.bass_utils import run_bass_kernel_spmd as _run

    nc = _bacc.Bacc("TRN2", target_bir_lowering=False, num_devices=1)
    arrays, args = {}, []
    for name in _INS:
        a = _np.ascontiguousarray(inputs[name])
        arrays[f"in_{name}"] = a
        args.append(nc.dram_tensor(f"in_{name}", a.shape, _mybir.dt.from_np(a.dtype), kind="ExternalInput").ap())
    args.append(nc.dram_tensor("out_0", (NIMG, N, HID), F32, kind="ExternalOutput").ap())
    vit(nc, *args)
    r = _run(nc, [arrays], core_ids=[0])
    return r.results[0]["out_0"]
```
